# Optimizing a Trainium2 kernel written in Bass

```python
import numpy as np
import jax
import jax.numpy as jnp

def _softmax(x, axis=-1):
    return jax.nn.softmax(x, axis=axis)

def _gelu(x):
    return jax.nn.gelu(x, approximate=True)

def _silu(x):
    return jax.nn.silu(x)

def _sigmoid(x):
    return jax.nn.sigmoid(x)

def _layernorm(x, axis=-1, eps=1e-05):
    m = jnp.mean(x, axis=axis, keepdims=True)
    v = jnp.var(x, axis=axis, keepdims=True)
    return (x - m) / jnp.sqrt(v + eps)

def _scatter_add(tgt, idx, src, axis=0):
    return tgt.at[idx].add(src)

def _segment_sum(src, seg, n):
    return jax.ops.segment_sum(src, seg, n)
kernel_name = 'mk_vit_tower_d2_tok_img256_r4_65f983'

def setup_inputs(seed: int=0):
    np.random.seed(seed)
    _w = jnp.asarray

    def _rec_inputs():
        import jax
        import jax.numpy as jnp
        _rk = jax.random.key(seed)
        x = -4.65018e-05 + 0.999886 * jax.random.normal(jax.random.fold_in(_rk, 1), (8, 3, 128, 128), jnp.float32)
        return x
    x = _rec_inputs()

    def _L0_tok_setup():
        import jax, jax.numpy as jnp
        import numpy as np
        B, C, H, P, D = (64, 3, 128, 16, 64)
        NP = H // P
        key = jax.random.key(seed)
        ks = jax.random.split(key, 7)
        s = lambda fan_in: 1.0 / np.sqrt(fan_in)
        return {'x': jax.random.normal(ks[0], (B, C, H, H), dtype=jnp.float32), 'Wp': jax.random.normal(ks[1], (P * P * C, D), dtype=jnp.float32) * s(P * P * C), 'bp': jax.random.normal(ks[2], (D,), dtype=jnp.float32) * 0.01, 'W1': jax.random.normal(ks[3], (2, D), dtype=jnp.float32) * s(2), 'b1': jax.random.normal(ks[4], (D,), dtype=jnp.float32) * 0.01, 'W2': jax.random.normal(ks[5], (D, D), dtype=jnp.float32) * s(D), 'b2': jax.random.normal(ks[6], (D,), dtype=jnp.float32) * 0.01}
    _L0_tok_all = _L0_tok_setup()
    _L0_tok_in = {k: v for k, v in _L0_tok_all.items() if k in ('Wp', 'bp', 'W1', 'b1', 'W2', 'b2')}
    del _L0_tok_all

    def _L0_attn_setup():
        import jax, jax.numpy as jnp
        import numpy as np
        N_HEADS, EMB, KQ = (8, 64, 64)
        BATCH, SEQ = (4, 512)
        key = jax.random.key(seed)
        ks = jax.random.split(key, 5)
        x = jax.random.normal(ks[0], (BATCH, SEQ, EMB), dtype=jnp.float32)
        key_matrices = 0.1 * jax.random.normal(ks[1], (N_HEADS, EMB, KQ), dtype=jnp.float32)
        query_matrices = 0.1 * jax.random.normal(ks[2], (N_HEADS, EMB, KQ), dtype=jnp.float32)
        value_in_matrices = 0.1 * jax.random.normal(ks[3], (N_HEADS, EMB, KQ), dtype=jnp.float32)
        value_out_matrices = 0.1 * jax.random.normal(ks[4], (N_HEADS, KQ, EMB), dtype=jnp.float32)
        return {'x': x, 'key_matrices': key_matrices, 'query_matrices': query_matrices, 'value_in_matrices': value_in_matrices, 'value_out_matrices': value_out_matrices}
    _L0_attn_all = _L0_attn_setup()
    _L0_attn_in = {k: v for k, v in _L0_attn_all.items() if k in ('key_matrices', 'query_matrices', 'value_in_matrices', 'value_out_matrices')}
    del _L0_attn_all

    def _L0_ffn_setup():
        import math
        import jax, jax.numpy as jnp
        import numpy as np
        CAPACITY_FACTOR = 1.25
        key = jax.random.key(seed)
        ks = jax.random.split(key, 5)
        B, L, D, F, E = (8, 2048, 64, 256, 8)
        h = jax.random.normal(ks[0], (B, L, D), dtype=jnp.float32)
        gate_w = jax.random.normal(ks[1], (D, E), dtype=jnp.float32) * 0.02
        gate_b = jnp.zeros((E,), dtype=jnp.float32)
        w1 = jax.random.normal(ks[2], (E, D, F), dtype=jnp.float32) * (1.0 / math.sqrt(D))
        b1 = jnp.zeros((E, F), dtype=jnp.float32)
        w2 = jax.random.normal(ks[3], (E, F, D), dtype=jnp.float32) * (1.0 / math.sqrt(F))
        b2 = jnp.zeros((E, D), dtype=jnp.float32)
        return {'h': h, 'gate_w': gate_w, 'gate_b': gate_b, 'w1': w1, 'b1': b1, 'w2': w2, 'b2': b2}
    _L0_ffn_all = _L0_ffn_setup()
    _L0_ffn_in = {k: v for k, v in _L0_ffn_all.items() if k in ('gate_w', 'gate_b', 'w1', 'b1', 'w2', 'b2')}
    del _L0_ffn_all

    def _L1_attn_setup():
        import jax, jax.numpy as jnp
        import numpy as np
        A, Bc, Cc = (0.5, 1.0, 1.0)
        H = 8
        EPS = 1e-12

        def _normalize(t):
            n = jnp.linalg.norm(t, axis=-1, keepdims=True)
            return t / jnp.maximum(n, EPS)
        key = jax.random.key(seed)
        ks = jax.random.split(key, 5)
        B, N, C = (8, 512, 64)
        D = C // H
        x = jax.random.normal(ks[0], (B, N, C), dtype=jnp.float32)
        Wqkv = jax.random.normal(ks[1], (3 * H * D, C), dtype=jnp.float32) * 0.02
        bqkv = jnp.zeros((3 * H * D,), dtype=jnp.float32)
        Wproj = jax.random.normal(ks[2], (C, H * D), dtype=jnp.float32) * 0.02
        bproj = jnp.zeros((C,), dtype=jnp.float32)
        temperature = jnp.ones((1, H, 1, 1), dtype=jnp.float32)
        return {'x': x, 'Wqkv': Wqkv, 'bqkv': bqkv, 'Wproj': Wproj, 'bproj': bproj, 'temperature': temperature}
    _L1_attn_all = _L1_attn_setup()
    _L1_attn_in = {k: v for k, v in _L1_attn_all.items() if k in ('Wqkv', 'bqkv', 'Wproj', 'bproj', 'temperature')}
    del _L1_attn_all

    def _L1_ffn_setup():
        import jax, jax.numpy as jnp
        import numpy as np
        B, T, C = (64, 96, 64)
        NH, NKV = (4, 2)
        HD = C // NH
        NREP = NH // NKV
        NE, TOPK = (8, 2)
        HID = int(8 / 3 * C)
        EPS_RMS = 1e-06

        def _rope_tables(t_len):
            inv_freq = 1.0 / 10000.0 ** (np.arange(0, HD, 2, dtype=np.float32) / HD)
            t = np.arange(t_len, dtype=np.float32)
            freqs = np.outer(t, inv_freq)
            emb = np.concatenate([freqs, freqs], axis=-1)
            return (jnp.asarray(np.cos(emb)), jnp.asarray(np.sin(emb)))

        def _rotate_half(x):
            h = x.shape[-1] // 2
            return jnp.concatenate([-x[..., h:], x[..., :h]], axis=-1)

        def _rmsnorm(v, w):
            return v * jax.lax.rsqrt(jnp.mean(v * v, axis=-1, keepdims=True) + EPS_RMS) * w
        key = jax.random.key(seed)
        ks = jax.random.split(key, 10)
        s = lambda k, shape: jax.random.normal(k, shape, jnp.float32) * 0.02
        return {'x': jax.random.normal(ks[0], (B, T, C), jnp.float32), 'ln1_w': jnp.ones((C,), jnp.float32), 'ln2_w': jnp.ones((C,), jnp.float32), 'wq': s(ks[1], (NH * HD, C)), 'wk': s(ks[2], (NKV * HD, C)), 'wv': s(ks[3], (NKV * HD, C)), 'wo': s(ks[4], (C, C)), 'router_w': s(ks[5], (NE, C)), 'w1': s(ks[6], (NE, HID, C)), 'w2': s(ks[7], (NE, C, HID)), 'w3': s(ks[8], (NE, HID, C))}
    _L1_ffn_all = _L1_ffn_setup()
    _L1_ffn_in = {k: v for k, v in _L1_ffn_all.items() if k in ('ln1_w', 'ln2_w', 'wq', 'wk', 'wv', 'wo', 'router_w', 'w1', 'w2', 'w3')}
    del _L1_ffn_all
    return {'x': x, 'L0_tok_Wp': _L0_tok_in['Wp'], 'L0_tok_bp': _L0_tok_in['bp'], 'L0_tok_W1': _L0_tok_in['W1'], 'L0_tok_b1': _L0_tok_in['b1'], 'L0_tok_W2': _L0_tok_in['W2'], 'L0_tok_b2': _L0_tok_in['b2'], 'L0_attn_key_matrices': _L0_attn_in['key_matrices'], 'L0_attn_query_matrices': _L0_attn_in['query_matrices'], 'L0_attn_value_in_matrices': _L0_attn_in['value_in_matrices'], 'L0_attn_value_out_matrices': _L0_attn_in['value_out_matrices'], 'L0_ffn_gate_w': _L0_ffn_in['gate_w'], 'L0_ffn_gate_b': _L0_ffn_in['gate_b'], 'L0_ffn_w1': _L0_ffn_in['w1'], 'L0_ffn_b1': _L0_ffn_in['b1'], 'L0_ffn_w2': _L0_ffn_in['w2'], 'L0_ffn_b2': _L0_ffn_in['b2'], 'L1_attn_Wqkv': _L1_attn_in['Wqkv'], 'L1_attn_bqkv': _L1_attn_in['bqkv'], 'L1_attn_Wproj': _L1_attn_in['Wproj'], 'L1_attn_bproj': _L1_attn_in['bproj'], 'L1_attn_temperature': _L1_attn_in['temperature'], 'L1_ffn_ln1_w': _L1_ffn_in['ln1_w'], 'L1_ffn_ln2_w': _L1_ffn_in['ln2_w'], 'L1_ffn_wq': _L1_ffn_in['wq'], 'L1_ffn_wk': _L1_ffn_in['wk'], 'L1_ffn_wv': _L1_ffn_in['wv'], 'L1_ffn_wo': _L1_ffn_in['wo'], 'L1_ffn_router_w': _L1_ffn_in['router_w'], 'L1_ffn_w1': _L1_ffn_in['w1'], 'L1_ffn_w2': _L1_ffn_in['w2'], 'L1_ffn_w3': _L1_ffn_in['w3']}

def reference(x, L0_tok_Wp, L0_tok_bp, L0_tok_W1, L0_tok_b1, L0_tok_W2, L0_tok_b2, L0_attn_key_matrices, L0_attn_query_matrices, L0_attn_value_in_matrices, L0_attn_value_out_matrices, L0_ffn_gate_w, L0_ffn_gate_b, L0_ffn_w1, L0_ffn_b1, L0_ffn_w2, L0_ffn_b2, L1_attn_Wqkv, L1_attn_bqkv, L1_attn_Wproj, L1_attn_bproj, L1_attn_temperature, L1_ffn_ln1_w, L1_ffn_ln2_w, L1_ffn_wq, L1_ffn_wk, L1_ffn_wv, L1_ffn_wo, L1_ffn_router_w, L1_ffn_w1, L1_ffn_w2, L1_ffn_w3):
    import jax
    import jax.numpy as jnp

    def _L0_tok_ref(x, Wp, bp, W1, b1, W2, b2):
        import jax, jax.numpy as jnp
        import numpy as np
        B, C, H, P, D = (64, 3, 128, 16, 64)
        NP = H // P
        b = x.shape[0]
        patches = x.reshape(b, C, NP, P, NP, P)
        patches = patches.transpose(0, 2, 4, 1, 3, 5).reshape(b, NP * NP, C * P * P)
        embedded = jnp.einsum('bnk,kd->bnd', patches, Wp) + bp
        gx, gy = jnp.meshgrid(jnp.arange(NP, dtype=jnp.float32), jnp.arange(NP, dtype=jnp.float32), indexing='ij')
        xy = jnp.stack([gx, gy], axis=-1).reshape(1, -1, 2) / (NP - 1)
        pos = jax.nn.relu(xy @ W1 + b1) @ W2 + b2
        return embedded + pos

    def _L0_attn_ref(x, key_matrices, query_matrices, value_in_matrices, value_out_matrices):
        import jax, jax.numpy as jnp
        import numpy as np
        N_HEADS, EMB, KQ = (8, 64, 64)
        BATCH, SEQ = (4, 512)
        seq_len = x.shape[1]
        queries = jnp.einsum('ned,bse->nbsd', query_matrices, x)
        keys = jnp.einsum('ned,bse->nbsd', key_matrices, x)
        kq = jnp.einsum('nbjd,nbkd->nbjk', keys, queries)
        mask = jnp.triu(jnp.ones((seq_len, seq_len), dtype=bool), k=1)
        kq = jnp.where(mask, -jnp.inf, kq)
        attention_pattern = jax.nn.softmax(kq, axis=3)
        v = jnp.einsum('bjp,npd->nbjd', x, value_in_matrices)
        ctx = jnp.einsum('nbsj,nbjd->nbsd', attention_pattern, v)
        return jnp.einsum('nbsd,nde->bse', ctx, value_out_matrices)

    def _L0_ffn_ref(h, gate_w, gate_b, w1, b1, w2, b2):
        import math
        import jax, jax.numpy as jnp
        import numpy as np
        CAPACITY_FACTOR = 1.25
        B, L, D = h.shape
        E = gate_w.shape[1]
        T = B * L
        C = max(1, math.ceil(CAPACITY_FACTOR * T / E))
        x = h.reshape(T, D)
        logits = x @ gate_w + gate_b
        probs = jax.nn.softmax(logits, axis=-1)
        idx = jnp.argmax(probs, axis=-1)
        prb = jnp.take_along_axis(probs, idx[:, None], axis=1)[:, 0]
        one_hot = jax.nn.one_hot(idx, E, dtype=jnp.float32)
        pos = (jnp.cumsum(one_hot, axis=0) * one_hot).sum(-1).astype(jnp.int32) - 1
        kept = pos < C
        pos_safe = jnp.where(kept, pos, C)
        buf = jnp.zeros((E, C, D), dtype=h.dtype).at[idx, pos_safe].set(x, mode='drop')
        hmid = jax.nn.relu(jnp.einsum('ecd,edf->ecf', buf, w1) + b1[:, None, :])
        ybuf = jnp.einsum('ecf,efd->ecd', hmid, w2) + b2[:, None, :]
        pos_g = jnp.minimum(pos, C - 1)
        y_tok = ybuf[idx, pos_g] * (prb * kept)[:, None]
        y = y_tok.reshape(B, L, D)
        y = jnp.nan_to_num(y, nan=0.0, posinf=10000.0, neginf=-10000.0)
        return y

    def _L1_attn_ref(x, Wqkv, bqkv, Wproj, bproj, temperature):
        import jax, jax.numpy as jnp
        import numpy as np
        A, Bc, Cc = (0.5, 1.0, 1.0)
        H = 8
        EPS = 1e-12

        def _normalize(t):
            n = jnp.linalg.norm(t, axis=-1, keepdims=True)
            return t / jnp.maximum(n, EPS)
        B, N, C = x.shape
        D = C // H
        scale = float(D) ** 0.25
        qkv = (x @ Wqkv.T + bqkv).reshape(B, N, 3, H, D)
        qkv = jnp.transpose(qkv, (2, 0, 3, 1, 4))
        q, k, v = (qkv[0], qkv[1], qkv[2])
        q = q * scale
        v1 = jnp.concatenate([jnp.ones((B, H, N, 1), dtype=v.dtype), v], axis=-1)
        qn = _normalize(q) * (scale * temperature)
        kn = _normalize(k) * scale
        vN = v1 / N
        kv_mod = jnp.einsum('bhni,bhnj,bhne->bhije', kn, kn, vN)
        kv = jnp.einsum('bhnd,bhne->bhde', kn, vN)
        vsum = jnp.sum(vN, axis=-2)[:, :, None, :]
        y = A * jnp.einsum('bhni,bhnj,bhije->bhne', qn, qn, kv_mod) + scale ** 2 * Bc * jnp.einsum('bhnd,bhde->bhne', qn, kv) + scale ** 4 * Cc * vsum
        y_norm, y = (y[..., :1], y[..., 1:])
        y = y / y_norm
        out = jnp.transpose(y, (0, 2, 1, 3)).reshape(B, N, H * D)
        return out @ Wproj.T + bproj

    def _L1_ffn_ref(x, ln1_w, ln2_w, wq, wk, wv, wo, router_w, w1, w2, w3):
        import jax, jax.numpy as jnp
        import numpy as np
        B, T, C = (64, 96, 64)
        NH, NKV = (4, 2)
        HD = C // NH
        NREP = NH // NKV
        NE, TOPK = (8, 2)
        HID = int(8 / 3 * C)
        EPS_RMS = 1e-06

        def _rope_tables(t_len):
            inv_freq = 1.0 / 10000.0 ** (np.arange(0, HD, 2, dtype=np.float32) / HD)
            t = np.arange(t_len, dtype=np.float32)
            freqs = np.outer(t, inv_freq)
            emb = np.concatenate([freqs, freqs], axis=-1)
            return (jnp.asarray(np.cos(emb)), jnp.asarray(np.sin(emb)))

        def _rotate_half(x):
            h = x.shape[-1] // 2
            return jnp.concatenate([-x[..., h:], x[..., :h]], axis=-1)

        def _rmsnorm(v, w):
            return v * jax.lax.rsqrt(jnp.mean(v * v, axis=-1, keepdims=True) + EPS_RMS) * w
        Bx, Tx, Cx = x.shape
        h = _rmsnorm(x, ln1_w)
        q = (h @ wq.T).reshape(Bx, Tx, NH, HD).transpose(0, 2, 1, 3)
        k = (h @ wk.T).reshape(Bx, Tx, NKV, HD).transpose(0, 2, 1, 3)
        v = (h @ wv.T).reshape(Bx, Tx, NKV, HD).transpose(0, 2, 1, 3)
        cos, sin = _rope_tables(Tx)
        cos, sin = (cos[None, None], sin[None, None])
        q = q * cos + _rotate_half(q) * sin
        k = k * cos + _rotate_half(k) * sin
        k = jnp.repeat(k, NREP, axis=1)
        v = jnp.repeat(v, NREP, axis=1)
        scores = jnp.einsum('bhtd,bhsd->bhts', q, k) / jnp.sqrt(jnp.float32(HD))
        causal = jnp.tril(jnp.ones((Tx, Tx), dtype=bool))
        scores = jnp.where(causal[None, None], scores, jnp.float32(-1e+30))
        att = jax.nn.softmax(scores, axis=-1)
        y = jnp.einsum('bhts,bhsd->bhtd', att, v).transpose(0, 2, 1, 3).reshape(Bx, Tx, Cx)
        x = x + y @ wo.T
        flat = _rmsnorm(x, ln2_w).reshape(-1, Cx)
        probs = jax.nn.softmax(flat @ router_w.T, axis=-1)
        tp, ti = jax.lax.top_k(probs, TOPK)
        tp = tp / (jnp.sum(tp, axis=-1, keepdims=True) + 1e-09)
        weights = jnp.sum(tp[..., None] * jax.nn.one_hot(ti, NE, dtype=flat.dtype), axis=1)
        out = jnp.zeros_like(flat)
        for e in range(NE):
            hh = jax.nn.silu(flat @ w1[e].T) * (flat @ w3[e].T)
            out = out + weights[:, e:e + 1] * (hh @ w2[e].T)
        return x + out.reshape(Bx, Tx, Cx)
    h = _L0_tok_ref(x, L0_tok_Wp, L0_tok_bp, L0_tok_W1, L0_tok_b1, L0_tok_W2, L0_tok_b2)
    h = h + _L0_attn_ref(_layernorm(h, axis=-1), L0_attn_key_matrices, L0_attn_query_matrices, L0_attn_value_in_matrices, L0_attn_value_out_matrices)
    h = h + _L0_ffn_ref(_layernorm(h, axis=-1), L0_ffn_gate_w, L0_ffn_gate_b, L0_ffn_w1, L0_ffn_b1, L0_ffn_w2, L0_ffn_b2)
    h = h + _L1_attn_ref(_layernorm(h, axis=-1), L1_attn_Wqkv, L1_attn_bqkv, L1_attn_Wproj, L1_attn_bproj, L1_attn_temperature)
    h = h + _L1_ffn_ref(_layernorm(h, axis=-1), L1_ffn_ln1_w, L1_ffn_ln2_w, L1_ffn_wq, L1_ffn_wk, L1_ffn_wv, L1_ffn_wo, L1_ffn_router_w, L1_ffn_w1, L1_ffn_w2, L1_ffn_w3)
    return h

_drawn_inputs = setup_inputs


def setup_inputs(seed=0):
    import zlib

    import numpy as np

    out = dict(_drawn_inputs(seed))
    spreads = {'L0_ffn_gate_b': (0.0, 0.1),
     'L0_ffn_b1': (0.0, 0.8),
     'L0_ffn_b2': (0.0, 0.8),
     'L1_attn_bqkv': (0.0, 0.8),
     'L1_attn_bproj': (0.0, 0.1),
     'L1_attn_temperature': (1.0, 0.6),
     'L1_ffn_ln1_w': (1.0, 0.6),
     'L1_ffn_ln2_w': (1.0, 0.6)}
    factors = {'L0_tok_bp': 3.204,
     'L0_tok_b1': 3.765,
     'L0_tok_b2': 2.685,
     'L1_attn_Wqkv': 8.0,
     'L1_attn_Wproj': 5.683,
     'L1_ffn_wq': 8.0,
     'L1_ffn_wk': 8.0,
     'L1_ffn_wv': 8.0,
     'L1_ffn_wo': 8.0,
     'L1_ffn_router_w': 8.0,
     'L1_ffn_w1': 8.0,
     'L1_ffn_w2': 8.0,
     'L1_ffn_w3': 8.0}
    for name, (base, spread) in spreads.items():
        noise = np.random.default_rng([zlib.crc32(name.encode()), seed]).standard_normal(out[name].shape)
        drawn = base * np.exp(spread * noise) if base else spread * noise
        out[name] = jnp.asarray(drawn.astype(out[name].dtype))
    for name, factor in factors.items():
        out[name] = (out[name] * factor).astype(out[name].dtype)
    return out
```

```python
from contextlib import ExitStack

import numpy as np

import concourse.bass as bass
from concourse import mybir

F32 = mybir.dt.float32
BF16 = mybir.dt.bfloat16
U32 = mybir.dt.uint32
ALU = mybir.AluOpType
ACT = mybir.ActivationFunctionType
AX_X = mybir.AxisListType.X

P = 128
D = 64
IMG = 8
SEQ = 64
TOK = IMG * SEQ
NT = TOK // P
PATCH = 16
KC = 3 * PATCH * PATCH // P
H0 = 8
PAIRS0 = H0 // 2
E = 8
F0 = 256
CAP = -(-5 * TOK // (4 * E))
CH0 = E * F0 // P
H1, HD1 = 8, 8
H2, KV2, HD2 = 4, 2, 16
HID1 = 170
CH1 = -(-E * HID1 // P)
LN_EPS, RMS_EPS = 1e-5, 1e-6
NORM_EPS = 1e-12
F32_MAX = float(np.finfo(np.float32).max)
NEG = -1e30


def chunk_rows(c):
    return min(P, E * HID1 - c * P)


def chunk_experts(c):
    first = c * P // HID1
    return first, (c * P + chunk_rows(c) - 1) // HID1 - first + 1


DOWN_AT = [sum(chunk_experts(b)[1] for b in range(c)) for c in range(CH1 + 1)]


def build(nc, patches, consts, consts_bf, w_embed, w_pos, w_attn0, w_up0, w_down0, w_small0, w_b2,
          w_attn1, w_temp, w_ffn1, w_up1, w_down1, out):
    with ExitStack() as ctx:
        sems = {}

        def S(name):
            if name not in sems:
                sems[name] = ctx.enter_context(nc.semaphore(name))
            return sems[name]

        def sb(name, shape, dt=F32):
            return ctx.enter_context(nc.sbuf_tensor(name, shape, dt))

        def wide(ap, axis, n):
            ap = ap.unsqueeze(axis)
            shape = list(ap.shape)
            shape[axis] = n
            return ap.broadcast_to(shape)

        ps = ctx.enter_context(nc.psum_tensor("ps", [P, 8, 512], F32))

        pat = sb("pat", [P, NT, KC, P])
        con = sb("con", list(consts.shape))
        cbf32 = sb("cbf32", list(consts_bf.shape))
        cbf = sb("cbf", list(consts_bf.shape), BF16)
        wem = sb("wem", list(w_embed.shape))
        wpo = sb("wpo", list(w_pos.shape))
        wa0 = sb("wa0", list(w_attn0.shape))
        wu0 = sb("wu0", [P, E, P])
        wd0 = sb("wd0", [P, CH0, D])
        ws0 = sb("ws0", list(w_small0.shape))
        wb2 = sb("wb2", list(w_b2.shape))
        wa1 = sb("wa1", list(w_attn1.shape))
        wte = sb("wte", list(w_temp.shape))
        wf1 = sb("wf1", list(w_ffn1.shape))
        wu1 = sb("wu1", list(w_up1.shape))
        wd1 = sb("wd1", list(w_down1.shape))

        ident = con[:, 0:128]
        rope = con[:, 128:384]
        headmask1 = con[0:D, 384:388]
        headmask2 = con[0:D, 388:390]
        rank = con[:, 390:398]
        grid1 = con[0:3, 398:526]
        ident_b = cbf[:, 0:128]
        causal_b = cbf[:, 128:384]
        upto_b = cbf[:, 384:512]
        ones_b = cbf[:, 512:640]
        pos_w2 = wpo[0:66, 0:64]
        pos_w1 = wpo[0:3, 64:130]
        kT, qT0 = wa0[:, 0:512], wa0[:, 512:1024]
        vinT, vout = wa0[:, 1024:1536], wa0[:, 1536:2048]
        moe0_b1 = ws0[:, 0:16]
        gate_w = ws0[0:D, 16:24]
        gate_b = ws0[:, 24:32]
        qkv_w1 = wa1[0:65, 0:192]
        proj_w1 = wa1[0:65, 192:256]
        qk_w2 = wf1[0:D, 0:256]
        wv2 = wf1[0:HD2, 256:384]
        wo2 = wf1[0:HD2, 384:640]
        ln1_w, ln2_w = wf1[0:D, 640:641], wf1[:, 641:642]
        router_w = wf1[0:D, 642:650]

        ones = sb("ones", [P, P])
        half = sb("half", [P, 16])
        big = sb("big", [P, 2, NT * D])
        zero = sb("zero", [P, NT * D])
        kq0 = sb("kq0", [D, 512])
        vo0 = sb("vo0", [D, 512])
        vo2 = sb("vo2", [D, 256])
        poshid = sb("poshid", [66, P])

        h = sb("h", [P, NT, D])
        x = sb("x", [P, NT, D])
        stats = sb("stats", [P, NT, 6])
        meanvar = sb("meanvar", [P, NT, 2])
        vareps = sb("vareps", [P, NT, 2])
        rstd = sb("rstd", [P, NT, 2])
        xn = sb("xn", [P, NT, 2, D])
        xT = sb("xT", [P, NT, P])
        zs = sb("zs", [P, NT, PAIRS0, P])
        vs = sb("vs", [P, NT, 2, PAIRS0 * D])
        prob = sb("prob", [P, NT, 512])
        mx = sb("mx", [P, NT, 8])
        den = sb("den", [P, NT, 8])
        rden = sb("rden", [P, NT, 8])
        probT = sb("probT", [P, NT, 4, P])
        lg = sb("lg", [P, NT, E])
        lgm = sb("lgm", [P, NT])
        ex = sb("ex", [P, NT, E])
        exs = sb("exs", [P, NT])
        prb = sb("prb", [P, NT])
        tie = sb("tie", [P, NT, E])
        top = sb("top", [P, NT])
        tiem = sb("tiem", [P, NT])
        hot = sb("hot", [P, NT, E])
        hot2 = sb("hot2", [P, NT, E])
        rest = sb("rest", [P, NT, E])
        both = sb("both", [P, NT, E])
        hot_b = sb("hot_b", [P, NT, E], BF16)
        gate = sb("gate", [P, NT, E])
        hid = sb("hid", [P, CH0, TOK])
        yg = sb("yg", [P, NT, E, D])
        ysum = sb("ysum", [P, NT, D])
        bad = sb("bad", [P, 3, NT * D], U32)
        xT1 = sb("xT1", [65, NT, P])
        qk = sb("qk", [P, NT, P])
        qksq = sb("qksq", [P, NT, P])
        qkss = sb("qkss", [P, NT, 16])
        qkr = sb("qkr", [P, NT, 16])
        v1 = sb("v1", [P, NT, 2, H1, HD1 + 1])
        kTs = sb("kTs", [D, NT, P])
        qm = sb("qm", [D, NT, 4, P])
        rnorm = sb("rnorm", [D, NT, 16])
        ya = sb("ya", [D, NT, 2, D])
        yaT = sb("yaT", [65, NT, P])
        rot = sb("rot", [P, NT, 2, P])
        up = sb("up", [P, 4, TOK])

        block = ctx.enter_context(nc.Block())

        @block.sync
        def _(sp):
            sp.dma_start(wem[:], w_embed).then_inc(S("wem_in"), 16)
            for t in range(NT):
                sp.dma_start(pat[:, t], patches[:, t]).then_inc(S(f"pat{t}_in"), 16)
            sp.dma_start(wu0[:], w_up0.rearrange("p (e f) -> p e f", f=P)).then_inc(S("wu0_in"), 16)
            sp.dma_start(wd0[:], w_down0.rearrange("p (c d) -> p c d", d=D)).then_inc(S("wd0_in"), 16)
            sp.dma_start(wa1[:], w_attn1).then_inc(S("wa1_in"), 16)
            sp.dma_start(wu1[:], w_up1).then_inc(S("wu1_in"), 16)
            sp.dma_start(wd1[:], w_down1).then_inc(S("wd1_in"), 16)
            for t in range(NT):
                sp.wait_ge(S("h5"), t + 1)
                sp.dma_start(out[t * P:(t + 1) * P, :], h[:, t]).then_inc(S("stored"), 16)
            sp.wait_ge(S("stored"), 16 * NT)

        @block.gpsimd
        def _(pool):
            nc.gpsimd.memset(half[:], -0.5).then_inc(S("half_set"), 1)
            nc.gpsimd.memset(ones[:], 1.0).then_inc(S("ones_set"), 1)
            nc.gpsimd.memset(big[:, 0], 1e4).then_inc(S("big_set"), 1)
            nc.gpsimd.memset(big[:, 1], -1e4).then_inc(S("big_set"), 1)
            nc.gpsimd.memset(zero[:], 0.0).then_inc(S("big_set"), 1)
            pool.wait_ge(S("half_set"), 1)

            def inverse_roots(n, var, eps):
                for t in range(NT):
                    pool.wait_ge(S("var"), NT * n + t + 1)
                    nc.gpsimd.tensor_scalar(vareps[:, t, 0:1], var[:, t], eps, None,
                                            ALU.add).then_inc(S("vareps"), 1)
                    pool.wait_ge(S("vareps"), NT * min(n, 3) + t + 1)
                    nc.gpsimd.tensor_tensor(rstd[:, t, 0:1], vareps[:, t, 0:1], half[:, 0:1],
                                            ALU.pow).then_inc(S("rstd"), 1)

            def normalise(n, width):
                for t in range(NT):
                    pool.wait_ge(S("rden"), NT * n + t + 1)
                    nc.gpsimd.tensor_tensor(prob[:, t, 0:width].rearrange("p (g k) -> p g k", k=SEQ),
                                            prob[:, t, 0:width].rearrange("p (g k) -> p g k", k=SEQ),
                                            wide(rden[:, t, 0:width // SEQ], 2, SEQ),
                                            ALU.mult).then_inc(S("prob"), 1)

            inverse_roots(0, meanvar[:, :, 1:2], LN_EPS)
            normalise(0, 512)
            inverse_roots(1, meanvar[:, :, 1:2], LN_EPS)
            inverse_roots(2, meanvar[:, :, 1:2], LN_EPS)
            for t in range(NT):
                pool.wait_ge(S("qkss"), t + 1)
                nc.gpsimd.tensor_tensor(qkr[:, t], qkss[:, t], half[:], ALU.pow).then_inc(S("qkr"), 1)
            for t in range(NT):
                pool.wait_ge(S("var"), NT * 3 + t + 1)
                nc.gpsimd.tensor_scalar(vareps[:, t, 0:1], meanvar[:, t, 1:2], LN_EPS, None,
                                        ALU.add).then_inc(S("vareps2"), 1)
                nc.gpsimd.tensor_scalar(vareps[:, t, 1:2], meanvar[:, t, 1:2], 1.0 + RMS_EPS,
                                        LN_EPS * RMS_EPS, ALU.mult, ALU.add).then_inc(S("vareps2"), 1)
                pool.wait_ge(S("vareps2"), 2 * (t + 1))
                nc.gpsimd.tensor_tensor(rstd[:, t], vareps[:, t], half[:, 0:2],
                                        ALU.pow).then_inc(S("rstd"), 1)
            normalise(1, 256)
            inverse_roots(4, meanvar[:, :, 1:2], RMS_EPS)
            for t in range(NT):
                nc.gpsimd.tensor_tensor(h[:, t], h[:, t], x[:, t], ALU.add).then_inc(S("h4"), 1)

        @block.scalar
        def _(act):
            act.dma_start(con[:], consts).then_inc(S("con_in"), 16)
            act.dma_start(wpo[:], w_pos).then_inc(S("wpo_in"), 16)
            act.dma_start(wa0[:], w_attn0).then_inc(S("wa0_in"), 16)
            act.dma_start(cbf32[:], consts_bf).then_inc(S("cbf_in"), 16)
            act.dma_start(wf1[:], w_ffn1).then_inc(S("wf1_in"), 16)
            act.dma_start(ws0[:], w_small0).then_inc(S("ws0_in"), 16)
            act.dma_start(wb2[:], w_b2).then_inc(S("wb2_in"), 16)
            act.dma_start(wte[:], w_temp).then_inc(S("wte_in"), 16)

            act.wait_ge(S("poshid_ps"), 1)
            nc.scalar.activation(poshid[:], ps[0:66, 7, 0:P], ACT.Relu).then_inc(S("poshid"), 1)
            act.wait_ge(S("kq0_ps"), 1)
            nc.scalar.copy(kq0[:], ps[0:D, 1, :]).then_inc(S("kq0"), 1)
            act.wait_ge(S("vo0_ps"), 1)
            nc.scalar.copy(vo0[:], ps[0:D, 3, :]).then_inc(S("vo0"), 1)
            act.wait_ge(S("vo2_ps"), 1)
            nc.scalar.copy(vo2[:], ps[0:D, 5, 0:256]).then_inc(S("vo2"), 1)

            for t in range(NT):
                act.wait_ge(S("embed_ps"), t + 1)
                nc.scalar.copy(h[:, t], ps[:, 2 * t, 0:D]).then_inc(S("h0"), 1)

            for t in range(NT):
                act.wait_ge(S("xT_ps"), t + 1)
                nc.scalar.copy(xT[:, t], ps[:, 2 * t + 1, 0:P]).then_inc(S("xT"), 1)
            for t in range(NT):
                act.wait_ge(S("z_ps"), t + 1)
                nc.scalar.copy(zs[:, t].rearrange("p a b -> p (a b)"), ps[:, 2 * t, :]).then_inc(S("z"), 1)
            for t in range(NT):
                act.wait_ge(S("shifted"), t + 1)
                nc.scalar.activation(prob[:, t], prob[:, t], ACT.Exp).then_inc(S("exp"), 1)
            for t in range(NT):
                act.wait_ge(S("probT_ps"), t + 1)
                nc.scalar.copy(probT[:, t].rearrange("p a b -> p (a b)"), ps[:, 2 * t, :]).then_inc(S("probT"), 1)

            for t in range(NT):
                act.wait_ge(S("xT_ps"), NT + t + 1)
                nc.scalar.copy(xT[:, t], ps[:, 2 * t, 0:P]).then_inc(S("xT"), 1)
            act.wait_ge(S("ws0_in"), 16)
            for c in range(0, CH0, 2):
                act.wait_ge(S("hid_ps"), c + 1)
                nc.scalar.activation(hid[:, c], ps[:, HID_BANKS[c % 6], :], ACT.Relu,
                                     bias=moe0_b1[:, c:c + 1]).then_inc(S("hid_even"), 1)
                if c == 4:
                    act.wait_ge(S("lg"), 1)
                    nc.scalar.activation(ex[:].rearrange("p t e -> p (t e)"), lg[:].rearrange("p t e -> p (t e)"),
                                         ACT.Exp).then_inc(S("ex"), 1)

            act.wait_ge(S("ones_rows"), 2)
            for t in range(NT):
                act.wait_ge(S("xT_ps"), 2 * NT + t + 1)
                nc.scalar.copy(xT1[0:D, t], ps[0:D, 2 * t + 1, 0:P]).then_inc(S("xT"), 1)
            act.wait_ge(S("v1_ones"), 2)
            for t in range(NT):
                act.wait_ge(S("qkv_ps"), t + 1)
                for i in range(2):
                    rows = slice(i * D, (i + 1) * D)
                    nc.scalar.copy(v1[rows, t, i, :, 1:],
                                   ps[rows, 2 * t, 128:192].rearrange("p (h d) -> p h d", d=HD1)
                                   ).then_inc(S("v1"), 1)
                nc.scalar.activation(qksq[:, t], ps[:, 2 * t, 0:P], ACT.Square).then_inc(S("qksq"), 1)
            for t in range(NT):
                act.wait_ge(S("taylor_ps"), t + 1)
                nc.scalar.activation(prob[:, t].rearrange("p (g k) -> p g k", g=2),
                                     ps[:, 2 * t:2 * t + 2, 0:256], ACT.Square,
                                     bias=ones[:, 0:1]).then_inc(S("taylor"), 1)
            for t in range(NT):
                act.wait_ge(S("yaT_ps"), t + 1)
                nc.scalar.copy(yaT[0:D, t], ps[0:D, 2 * t + 1, 0:P]).then_inc(S("yaT"), 1)

            act.wait_ge(S("wf1_in"), 16)
            for t in range(NT):
                act.wait_ge(S("xT_ps"), 3 * NT + t + 1)
                nc.scalar.mul(xT[0:D, t], ps[0:D, 2 * t + 1, 0:P], ln1_w).then_inc(S("xT"), 1)
            for t in range(NT):
                act.wait_ge(S("v2_ps"), t + 1)
                nc.scalar.copy(vs[:, t, :, 0:P], ps[:, 2 * t + 1, 0:256].rearrange("p (i n) -> p i n", i=2)
                               ).then_inc(S("v2"), 1)
            for t in range(NT):
                act.wait_ge(S("shifted"), NT + t + 1)
                nc.scalar.activation(prob[:, t, 0:256], prob[:, t, 0:256], ACT.Exp,
                                     scale=HD2 ** -0.5).then_inc(S("exp"), 1)
            for t in range(NT):
                act.wait_ge(S("probT_ps"), NT + t + 1)
                nc.scalar.copy(probT[:, t, 0:2].rearrange("p a b -> p (a b)"), ps[:, 2 * t, 0:256]
                               ).then_inc(S("probT"), 1)

            for t in range(NT):
                act.wait_ge(S("xT_ps"), 4 * NT + t + 1)
                nc.scalar.mul(xT[:, t], ps[:, 2 * t, 0:P], ln2_w).then_inc(S("xT"), 1)
            act.wait_ge(S("lg"), 2)
            nc.scalar.activation(ex[:].rearrange("p t e -> p (t e)"), lg[:].rearrange("p t e -> p (t e)"),
                                 ACT.Exp).then_inc(S("ex"), 1)
            for c in range(CH1):
                n = chunk_rows(c)
                act.wait_ge(S("up_ps"), c + 1)
                if c >= 4:
                    act.wait_ge(S("hid1"), c - 3)
                nc.scalar.activation(up[0:n, c % 4], ps[0:n, UP_BANKS[c % 3], :], ACT.Silu).then_inc(S("silu"), 1)

        @block.vector
        def _(dve):
            def layer_norm(n):
                for t in range(NT):
                    dve.wait_ge(S(f"h{n}"), t + 1)
                    nc.vector.bn_stats(stats[:, t], h[:, t]).then_inc(S("stats"), 1)
                for t in range(NT):
                    dve.wait_ge(S("stats"), NT * n + t + 1)
                    nc.vector.bn_aggr(meanvar[:, t], stats[:, t]).then_inc(S("var"), 1)
                k = 1 if n == 3 else 0
                for t in range(NT):
                    dve.wait_ge(S("rstd"), NT * n + t + 1)
                    nc.vector.tensor_scalar(xn[:, t], wide(h[:, t], 1, 2), meanvar[:, t, 0:1], rstd[:, t, k:k + 1],
                                            ALU.subtract, ALU.mult).then_inc(S("xn"), 1)

            def rms_norm(n):
                for t in range(NT):
                    dve.wait_ge(S("x1"), t + 1)
                    nc.vector.tensor_tensor_reduce(xn[:, t, 0], x[:, t], x[:, t], 1.0 / D, 0.0, ALU.mult,
                                                   ALU.add, meanvar[:, t, 1:2]).then_inc(S("var"), 1)
                for t in range(NT):
                    dve.wait_ge(S("rstd"), NT * n + t + 1)
                    nc.vector.tensor_scalar(xn[:, t], wide(x[:, t], 1, 2), rstd[:, t, 0:1], None,
                                            ALU.mult).then_inc(S("xn"), 1)

            def softmax_front(n, heads):
                for t in range(NT):
                    scores = ps[:, 2 * t:2 * t + 2, 0:heads * SEQ // 2].rearrange("p g (h k) -> p g h k", k=SEQ)
                    m = mx[:, t, 0:heads].rearrange("p (g h) -> p g h", g=2)
                    if n == 0:
                        shifted = prob[:, t, 0:heads * SEQ].rearrange("p (h g k) -> p g h k", g=2, k=SEQ)
                    else:
                        shifted = prob[:, t, 0:heads * SEQ].rearrange("p (g h k) -> p g h k", g=2, k=SEQ)
                    dve.wait_ge(S("scores_ps"), NT * n + t + 1)
                    nc.vector.tensor_reduce(m, scores, AX_X, ALU.max).then_inc(S("mx"), 1)
                    dve.wait_ge(S("mx"), NT * n + t + 1)
                    nc.vector.tensor_tensor(shifted, scores, wide(m, 3, SEQ), ALU.subtract).then_inc(S("shifted"), 1)

            def softmax_sums(n, heads):
                for t in range(NT):
                    dve.wait_ge(S("exp"), NT * n + t + 1)
                    nc.vector.tensor_reduce(den[:, t, 0:heads],
                                            prob[:, t, 0:heads * SEQ].rearrange("p (g k) -> p g k", k=SEQ),
                                            AX_X, ALU.add).then_inc(S("den"), 1)
                    dve.wait_ge(S("den"), NT * n + t + 1)
                    nc.vector.reciprocal(rden[:, t, 0:heads], den[:, t, 0:heads]).then_inc(S("rden"), 1)

            def add_to(stream, source, bank, name):
                for t in range(NT):
                    dve.wait_ge(S(source[0]), source[1] + t + 1)
                    nc.vector.tensor_tensor(stream[:, t], stream[:, t], ps[:, 2 * t + bank, 0:D],
                                            ALU.add).then_inc(S(name), 1)

            step = [0]

            def link(ins):
                step[0] += 1
                ins.then_inc(S("gating_step"), 1)
                dve.wait_ge(S("gating_step"), step[0])

            def first_best(values, best, onehot):
                link(nc.vector.tensor_reduce(best[:], values[:], AX_X, ALU.max))
                link(nc.vector.tensor_tensor(tie[:], values[:], wide(best[:], 2, E), ALU.is_equal))
                link(nc.vector.tensor_tensor(tie[:], tie[:], wide(rank, 1, NT), ALU.mult))
                link(nc.vector.tensor_reduce(tiem[:], tie[:], AX_X, ALU.max))
                link(nc.vector.tensor_tensor(onehot[:], tie[:], wide(tiem[:], 2, E), ALU.is_equal))

            def gated_sum(n, name):
                for t in range(NT):
                    dve.wait_ge(S("moe_ps"), NT * n + t + 1)
                    nc.vector.tensor_tensor(yg[:, t], ps[:, 2 * t, :].rearrange("p (e d) -> p e d", d=D),
                                            wide(gate[:, t], 2, D), ALU.mult).then_inc(S("yg"), 1)
                    dve.wait_ge(S("yg"), NT * n + t + 1)
                    nc.vector.tensor_reduce(ysum[:, t], yg[:, t].rearrange("p e d -> p d e"), AX_X,
                                            ALU.add).then_inc(S(name), 1)

            nc.vector.memset(v1[:], 0.0).then_inc(S("v1_zero"), 1)
            dve.wait_ge(S("v1_zero"), 1)
            for i in range(2):
                nc.vector.memset(v1[i * D:(i + 1) * D, :, i, :, 0:1], 1.0).then_inc(S("v1_ones"), 1)
            nc.vector.memset(xT1[64:65], 1.0).then_inc(S("ones_rows"), 1)
            nc.vector.memset(yaT[64:65], 1.0).then_inc(S("ones_rows"), 1)
            dve.wait_ge(S("cbf_in"), 16)
            nc.vector.tensor_copy(cbf[:], cbf32[:]).then_inc(S("cbf"), 1)

            layer_norm(0)
            for t in range(NT):
                dve.wait_ge(S("v_ps"), t + 1)
                nc.vector.tensor_copy(vs[:, t].rearrange("p i n -> p (i n)"), ps[:, 2 * t + 1, :]).then_inc(S("v"), 1)
            softmax_front(0, H0)
            softmax_sums(0, H0)
            add_to(h, ("attn_ps", 0), 1, "h1")

            layer_norm(1)
            dve.wait_ge(S("ws0_in"), 16)
            dve.wait_ge(S("con_in"), 16)
            dve.wait_ge(S("logits_ps"), 1)
            link(nc.vector.tensor_tensor(lg[:], ps[:, 1, 0:NT * E].rearrange("p (t e) -> p t e", e=E),
                                         wide(gate_b, 1, NT), ALU.add))
            link(nc.vector.tensor_reduce(lgm[:], lg[:], AX_X, ALU.max))
            nc.vector.tensor_tensor(lg[:], lg[:], wide(lgm[:], 2, E), ALU.subtract).then_inc(S("lg"), 1)

            def relu_chunk(c):
                dve.wait_ge(S("hid_ps"), c + 1)
                nc.vector.tensor_scalar(hid[:, c], ps[:, HID_BANKS[c % 6], :], moe0_b1[:, c:c + 1], 0.0,
                                        ALU.add, ALU.max).then_inc(S("hid_odd"), 1)

            relu_chunk(1)
            relu_chunk(3)
            relu_chunk(5)
            dve.wait_ge(S("ex"), 1)
            first_best(ex, top, hot)
            nc.vector.tensor_copy(hot_b[:], hot[:]).then_inc(S("hot_b"), 1)
            link(nc.vector.tensor_reduce(exs[:], ex[:], AX_X, ALU.add))
            link(nc.vector.reciprocal(prb[:], exs[:]))
            relu_chunk(7)
            relu_chunk(9)
            dve.wait_ge(S("counts_ps"), 1)
            link(nc.vector.scalar_tensor_tensor(gate[:].rearrange("p t e -> p (t e)"), ps[:, 7, 0:NT * E],
                                                float(CAP), hot[:].rearrange("p t e -> p (t e)"),
                                                ALU.is_le, ALU.mult))
            link(nc.vector.tensor_tensor(gate[:], gate[:], wide(prb[:], 2, E), ALU.mult))
            for c in range(11, CH0, 2):
                relu_chunk(c)
            gated_sum(0, "ysum")
            dve.wait_ge(S("ysum"), NT)
            dve.wait_ge(S("big_set"), 3)
            y = ysum[:].rearrange("p t d -> p (t d)")
            nc.vector.tensor_scalar(bad[:, 0], y, F32_MAX, None, ALU.is_gt).then_inc(S("bad"), 1)
            nc.vector.tensor_scalar(bad[:, 1], y, -F32_MAX, None, ALU.is_lt).then_inc(S("bad"), 1)
            nc.vector.tensor_tensor(bad[:, 2], y, y, ALU.not_equal).then_inc(S("bad"), 1)
            dve.wait_ge(S("bad"), 3)
            link(nc.vector.copy_predicated(y, bad[:, 0], big[:, 0]))
            link(nc.vector.copy_predicated(y, bad[:, 1], big[:, 1]))
            link(nc.vector.copy_predicated(y, bad[:, 2], zero[:]))
            for t in range(NT):
                nc.vector.tensor_tensor(h[:, t], h[:, t], ysum[:, t], ALU.add).then_inc(S("h2"), 1)

            layer_norm(2)
            for t in range(NT):
                dve.wait_ge(S("qksq"), t + 1)
                link(nc.vector.tensor_reduce(qkss[:, t], qksq[:, t].rearrange("p (g d) -> p g d", d=HD1),
                                             AX_X, ALU.add))
                nc.vector.tensor_scalar(qkss[:, t], qkss[:, t], NORM_EPS ** 2 / HD1 ** 0.5, None,
                                        ALU.max).then_inc(S("qkss"), 1)
            dve.wait_ge(S("wte_in"), 16)
            for t in range(NT):
                dve.wait_ge(S("qkr"), t + 1)
                link(nc.vector.tensor_tensor(qkr[:, t], qkr[:, t], wte[:], ALU.mult))
                nc.vector.tensor_tensor(qk[:, t].rearrange("p (g d) -> p g d", d=HD1),
                                        ps[:, 2 * t, 0:P].rearrange("p (g d) -> p g d", d=HD1),
                                        wide(qkr[:, t], 2, HD1), ALU.mult).then_inc(S("qk"), 1)
            for t in range(NT):
                dve.wait_ge(S("qkT_ps"), t + 1)
                nc.vector.tensor_copy(kTs[:, t], ps[0:D, 2 * t + 1, P:2 * P]).then_inc(S("qkT"), 1)
                nc.vector.tensor_tensor(qm[:, t], wide(ps[0:D, 2 * t + 1, 0:P], 1, 4), wide(headmask1, 2, P),
                                        ALU.mult).then_inc(S("qkT"), 1)
            for t in range(NT):
                dve.wait_ge(S("ynum_ps"), t + 1)
                num = ps[0:D, 2 * t, 0:144].rearrange("p (g d) -> p g d", d=HD1 + 1)
                link(nc.vector.reciprocal(rnorm[:, t].unsqueeze(2), num[:, :, 0:1]))
                nc.vector.tensor_tensor(ya[:, t].rearrange("p i (h d) -> p (i h) d", d=HD1), num[:, :, 1:],
                                        wide(rnorm[:, t], 2, HD1), ALU.mult).then_inc(S("ya"), 1)
            add_to(h, ("proj_ps", 0), 0, "h3")

            layer_norm(3)
            for t in range(NT):
                nc.vector.tensor_scalar(x[:, t], h[:, t], meanvar[:, t, 0:1], rstd[:, t, 0:1],
                                        ALU.subtract, ALU.mult).then_inc(S("x0"), 1)
            for t in range(NT):
                dve.wait_ge(S("qk2_ps"), t + 1)
                nc.vector.tensor_tensor(rot[:, t].rearrange("p a b -> p (a b)"), ps[:, 2 * t, 0:256], rope,
                                        ALU.mult).then_inc(S("rot"), 1)
                dve.wait_ge(S("rot"), t + 1)
                nc.vector.tensor_tensor(qk[:, t], rot[:, t, 0], rot[:, t, 1], ALU.add).then_inc(S("qk"), 1)
            for t in range(NT):
                dve.wait_ge(S("qkT_ps"), NT + t + 1)
                nc.vector.tensor_copy(kTs[:, t], ps[0:D, 2 * t, 0:P]).then_inc(S("qkT"), 1)
                nc.vector.tensor_tensor(qm[:, t, 0:2], wide(ps[0:D, 2 * t, P:2 * P], 1, 2),
                                        wide(headmask2, 2, P), ALU.mult).then_inc(S("qkT"), 1)
            softmax_front(1, H2)
            softmax_sums(1, H2)
            dve.wait_ge(S("x0"), NT)
            add_to(x, ("attn_ps", NT), 1, "x1")

            rms_norm(4)
            dve.wait_ge(S("logits_ps"), 2)
            link(nc.vector.tensor_copy(lg[:], ps[:, 7, 0:NT * E].rearrange("p (t e) -> p t e", e=E)))
            link(nc.vector.tensor_reduce(lgm[:], lg[:], AX_X, ALU.max))
            nc.vector.tensor_tensor(lg[:], lg[:], wide(lgm[:], 2, E), ALU.subtract).then_inc(S("lg"), 1)
            dve.wait_ge(S("ex"), 2)
            first_best(ex, top, hot)
            link(nc.vector.scalar_tensor_tensor(rest[:].rearrange("p t e -> p (t e)"),
                                                hot[:].rearrange("p t e -> p (t e)"), -2.0,
                                                ex[:].rearrange("p t e -> p (t e)"), ALU.mult, ALU.add))
            first_best(rest, top, hot2)
            link(nc.vector.tensor_tensor(both[:], hot[:], hot2[:], ALU.add))
            link(nc.vector.tensor_tensor(both[:], both[:], ex[:], ALU.mult))
            link(nc.vector.tensor_reduce(prb[:], both[:], AX_X, ALU.add))
            link(nc.vector.tensor_reduce(exs[:], ex[:], AX_X, ALU.add))
            link(nc.vector.scalar_tensor_tensor(prb[:], exs[:], 1e-9, prb[:], ALU.mult, ALU.add))
            link(nc.vector.reciprocal(prb[:], prb[:]))
            link(nc.vector.tensor_tensor(gate[:], both[:], wide(prb[:], 2, E), ALU.mult))
            for c in range(CH1):
                n = chunk_rows(c)
                dve.wait_ge(S("silu"), c + 1)
                nc.vector.tensor_tensor(hid[0:n, c], up[0:n, c % 4], ps[0:n, UP_BANKS[c % 3] + 1, :],
                                        ALU.mult).then_inc(S("hid1"), 1)
            gated_sum(1, "ysum")
            for t in range(NT):
                dve.wait_ge(S("ysum"), NT + t + 1)
                if t == 0:
                    dve.wait_ge(S("h4"), NT)
                nc.vector.tensor_tensor(h[:, t], h[:, t], ysum[:, t], ALU.add).then_inc(S("h5"), 1)

        @block.tensor
        def _(pe):
            def transpose_xn(n, bank):
                for t in range(NT):
                    pe.wait_ge(S("xn"), NT * n + t + 1)
                    nc.tensor.transpose(ps[:, 2 * t + bank, 0:P], xn[:, t].rearrange("p a b -> p (a b)"),
                                        ident).then_inc(S("xT_ps"), 1)

            def attend(n, pairs):
                for t in range(NT):
                    pe.wait_ge(S("prob"), NT * n + t + 1)
                    for c in range(pairs):
                        mm = nc.tensor.transpose(ps[:, 2 * t, c * P:(c + 1) * P], prob[:, t, c * P:(c + 1) * P], ident)
                    mm.then_inc(S("probT_ps"), 1)
                for t in range(NT):
                    pe.wait_ge(S("probT"), NT * n + t + 1)
                    for i in range(2):
                        for c in range(pairs):
                            mm = nc.tensor.matmul(ps[i * D:(i + 1) * D, 2 * t + 1, 0:D],
                                                  probT[:, t, c, i * D:(i + 1) * D],
                                                  vs[:, t, i, c * D:(c + 1) * D],
                                                  start=(c == 0), stop=(c == pairs - 1))
                    mm.then_inc(S("attn_ps"), 1)

            pe.wait_ge(S("wpo_in"), 16)
            pe.wait_ge(S("con_in"), 16)
            nc.tensor.matmul(ps[0:66, 7, 0:P], pos_w1, grid1, start=True, stop=True).then_inc(S("poshid_ps"), 1)
            pe.wait_ge(S("wa0_in"), 16)
            for n in range(H0):
                cols = slice(n * D, (n + 1) * D)
                mm = nc.tensor.matmul(ps[0:D, 1, cols], qT0[:, cols], kT[:, cols], start=True, stop=True)
            mm.then_inc(S("kq0_ps"), 1)
            for n in range(H0):
                cols = slice(n * D, (n + 1) * D)
                mm = nc.tensor.matmul(ps[0:D, 3, cols], vinT[:, cols], vout[:, cols], start=True, stop=True)
            mm.then_inc(S("vo0_ps"), 1)
            pe.wait_ge(S("wf1_in"), 16)
            for n in range(H2):
                kv = n // (H2 // KV2)
                mm = nc.tensor.matmul(ps[0:D, 5, n * D:(n + 1) * D], wv2[:, kv * D:(kv + 1) * D],
                                      wo2[:, n * D:(n + 1) * D], start=True, stop=True)
            mm.then_inc(S("vo2_ps"), 1)

            pe.wait_ge(S("wem_in"), 16)
            for t in range(NT):
                pe.wait_ge(S(f"pat{t}_in"), 16)
                for c in range(KC):
                    nc.tensor.matmul(ps[:, 2 * t, 0:D], pat[:, t, c], wem[:, c * D:(c + 1) * D],
                                     start=(c == 0), stop=False)
                if t == 0:
                    pe.wait_ge(S("poshid"), 1)
                nc.tensor.matmul(ps[:, 2 * t, 0:D], poshid[:], pos_w2, start=False,
                                 stop=True).then_inc(S("embed_ps"), 1)

            pe.wait_ge(S("vo2"), 1)
            transpose_xn(0, 1)
            pe.wait_ge(S("kq0"), 1)
            for t in range(NT):
                pe.wait_ge(S("xT"), t + 1)
                for c in range(PAIRS0):
                    mm = nc.tensor.matmul(ps[:, 2 * t, c * P:(c + 1) * P], kq0[:, c * P:(c + 1) * P],
                                          xT[0:D, t], start=True, stop=True)
                mm.then_inc(S("z_ps"), 1)
            pe.wait_ge(S("vo0"), 1)
            vo0_heads = vo0[:].rearrange("p (c g e) -> p g c e", g=2, e=D)
            for t in range(NT):
                for i in range(2):
                    for g in range(2):
                        mm = nc.tensor.matmul(ps[g * D:(g + 1) * D, 2 * t + 1, i * 256:(i + 1) * 256],
                                              xT[0:D, t, i * D:(i + 1) * D], vo0_heads[:, g],
                                              start=True, stop=True)
                mm.then_inc(S("v_ps"), 1)
            pe.wait_ge(S("cbf"), 1)
            for t in range(NT):
                pe.wait_ge(S("z"), t + 1)
                pe.wait_ge(S("v"), t + 1)
                for g in range(2):
                    nc.tensor.matmul(ps[:, 2 * t + g, 0:256], ident_b, causal_b, start=True, stop=False,
                                     skip_group_check=True)
                for g in range(2):
                    for i in range(2):
                        mm = nc.tensor.matmul(ps[i * D:(i + 1) * D, 2 * t + g, 0:256],
                                              xT[g * D:(g + 1) * D, t, i * D:(i + 1) * D],
                                              zs[g * D:(g + 1) * D, t, :, i * D:(i + 1) * D],
                                              start=False, stop=True, skip_group_check=True)
                mm.then_inc(S("scores_ps"), 1)
            attend(0, PAIRS0)

            transpose_xn(1, 0)
            pe.wait_ge(S("ws0_in"), 16)
            pe.wait_ge(S("h1"), NT)
            for t in range(NT):
                pe.wait_ge(S("xT"), NT + t + 1)
                mm = nc.tensor.matmul(ps[:, 1, t * E:(t + 1) * E], xT[0:D, t], gate_w, start=True, stop=True)
            mm.then_inc(S("logits_ps"), 1)
            pe.wait_ge(S("wu0_in"), 16)
            xT_all = xT[:].rearrange("p t n -> p (t n)")
            for c in range(CH0):
                e, g = c // 2, c % 2
                if c >= 6:
                    pe.wait_ge(S("hid_odd" if g else "hid_even"), (c - 6) // 2 + 1)
                nc.tensor.matmul(ps[:, HID_BANKS[c % 6], :], wu0[g * D:(g + 1) * D, e],
                                 xT_all[g * D:(g + 1) * D], start=True, stop=True).then_inc(S("hid_ps"), 1)
                if c == 11:
                    pe.wait_ge(S("hot_b"), 1)
                    hots = hot_b[:].rearrange("p t e -> p (t e)")
                    nc.tensor.matmul(ps[:, 7, 0:NT * E], upto_b, hots, start=True, stop=True,
                                     skip_group_check=True)
                    for d in range(1, NT):
                        mm = nc.tensor.matmul(ps[:, 7, d * E:NT * E], ones_b, hots[:, 0:(NT - d) * E],
                                              start=False, stop=True, skip_group_check=True)
                    mm.then_inc(S("counts_ps"), 1)
            pe.wait_ge(S("wd0_in"), 16)
            pe.wait_ge(S("wb2_in"), 16)
            pe.wait_ge(S("ones_set"), 1)
            pe.wait_ge(S("hid_even"), CH0 // 2)
            pe.wait_ge(S("hid_odd"), CH0 // 2)
            for t in range(NT):
                nc.tensor.matmul(ps[:, 2 * t, :], ones[0:1, :], wb2[:], start=True, stop=False,
                                 skip_group_check=True)
                for c in range(CH0):
                    e = c // 2
                    mm = nc.tensor.matmul(ps[:, 2 * t, e * D:(e + 1) * D], hid[:, c, t * P:(t + 1) * P],
                                          wd0[:, c], start=False, stop=(c % 2 == 1), skip_group_check=True)
                mm.then_inc(S("moe_ps"), 1)

            transpose_xn(2, 1)
            pe.wait_ge(S("wa1_in"), 16)
            for t in range(NT):
                pe.wait_ge(S("xT"), 2 * NT + t + 1)
                nc.tensor.matmul(ps[:, 2 * t, 0:192], xT1[:, t], qkv_w1, start=True,
                                 stop=True).then_inc(S("qkv_ps"), 1)
            for t in range(NT):
                pe.wait_ge(S("qk"), t + 1)
                for s in range(2):
                    mm = nc.tensor.transpose(ps[0:D, 2 * t + 1, s * P:(s + 1) * P],
                                             qk[:, t, s * D:(s + 1) * D], ident)
                mm.then_inc(S("qkT_ps"), 1)
            for t in range(NT):
                pe.wait_ge(S("qkT"), 2 * (t + 1))
                for g in range(2):
                    rows = slice(g * 32, (g + 1) * 32)
                    for i in range(2):
                        mm = nc.tensor.matmul(ps[i * D:(i + 1) * D, 2 * t + g, 0:256],
                                              kTs[rows, t, i * D:(i + 1) * D],
                                              qm[rows, t, :, i * D:(i + 1) * D],
                                              start=True, stop=True)
                mm.then_inc(S("taylor_ps"), 1)
            pe.wait_ge(S("v1"), 2 * NT)
            for t in range(NT):
                pe.wait_ge(S("taylor"), t + 1)
                nc.tensor.matmul(ps[0:D, 2 * t, 0:144], ones[:, 0:D],
                                 v1[:, t].rearrange("p i h d -> p (i h d)"), start=True, stop=False,
                                 skip_group_check=True)
                num = ps[0:D, 2 * t, 0:144].rearrange("p (i h d) -> p i h d", i=2, h=H1)
                for n in range(H1):
                    mm = nc.tensor.matmul(num[:, :, n], prob[:, t, n * SEQ:(n + 1) * SEQ], v1[:, t, :, n],
                                          start=False, stop=True, skip_group_check=True)
                mm.then_inc(S("ynum_ps"), 1)
            for t in range(NT):
                pe.wait_ge(S("ya"), t + 1)
                for i in range(2):
                    mm = nc.tensor.transpose(ps[0:D, 2 * t + 1, i * D:(i + 1) * D], ya[:, t, i],
                                             ident[0:D, 0:D])
                mm.then_inc(S("yaT_ps"), 1)
            for t in range(NT):
                pe.wait_ge(S("yaT"), t + 1)
                nc.tensor.matmul(ps[:, 2 * t, 0:D], yaT[:, t], proj_w1, start=True,
                                 stop=True).then_inc(S("proj_ps"), 1)

            transpose_xn(3, 1)
            for t in range(NT):
                pe.wait_ge(S("xT"), 3 * NT + t + 1)
                nc.tensor.matmul(ps[:, 2 * t, 0:256], xT[0:D, t], qk_w2, start=True,
                                 stop=True).then_inc(S("qk2_ps"), 1)
                for i in range(2):
                    for g in range(2):
                        mm = nc.tensor.matmul(ps[g * D:(g + 1) * D, 2 * t + 1, i * P:(i + 1) * P],
                                              xT[0:D, t, i * D:(i + 1) * D],
                                              vo2[:].rearrange("p (c g e) -> p g c e", g=2, e=D)[:, g],
                                              start=True, stop=True)
                mm.then_inc(S("v2_ps"), 1)
            for t in range(NT):
                pe.wait_ge(S("qk"), NT + t + 1)
                for s in range(2):
                    mm = nc.tensor.transpose(ps[0:D, 2 * t, s * P:(s + 1) * P], qk[:, t, s * D:(s + 1) * D], ident)
                mm.then_inc(S("qkT_ps"), 1)
            for t in range(NT):
                pe.wait_ge(S("qkT"), 2 * (NT + t + 1))
                pe.wait_ge(S("v2"), t + 1)
                for g in range(2):
                    nc.tensor.matmul(ps[:, 2 * t + g, 0:P], ident_b, causal_b[:, 0:P], start=True, stop=False,
                                     skip_group_check=True)
                for g in range(2):
                    rows = slice(g * 32, (g + 1) * 32)
                    for i in range(2):
                        mm = nc.tensor.matmul(ps[i * D:(i + 1) * D, 2 * t + g, 0:P],
                                              kTs[rows, t, i * D:(i + 1) * D],
                                              qm[rows, t, 0:2, i * D:(i + 1) * D],
                                              start=False, stop=True, skip_group_check=True)
                mm.then_inc(S("scores_ps"), 1)
            attend(1, 2)

            transpose_xn(4, 0)
            pe.wait_ge(S("x1"), NT)
            for t in range(NT):
                pe.wait_ge(S("xT"), 4 * NT + t + 1)
                mm = nc.tensor.matmul(ps[:, 7, t * E:(t + 1) * E], xT[0:D, t], router_w, start=True, stop=True)
            mm.then_inc(S("logits_ps"), 1)
            pe.wait_ge(S("wu1_in"), 16)
            for c in range(CH1):
                n = chunk_rows(c)
                if c >= 3:
                    pe.wait_ge(S("hid1"), c - 2)
                for g in range(2):
                    mm = nc.tensor.matmul(ps[0:n, UP_BANKS[c % 3] + g, :], wu1[g * D:(g + 1) * D, c * P:c * P + n],
                                          xT_all[g * D:(g + 1) * D], start=True, stop=True)
                mm.then_inc(S("up_ps"), 1)
            pe.wait_ge(S("wd1_in"), 16)
            for t in range(NT):
                for c in range(CH1):
                    n = chunk_rows(c)
                    e, ne = chunk_experts(c)
                    if t == 0:
                        pe.wait_ge(S("hid1"), c + 1)
                        if c == 0:
                            pe.wait_ge(S("hid1"), CH1)
                    mm = nc.tensor.matmul(ps[:, 2 * t, e * D:(e + ne) * D], hid[0:n, c, t * P:(t + 1) * P],
                                          wd1[0:n, DOWN_AT[c] * D:DOWN_AT[c + 1] * D],
                                          start=(c == 0), stop=True, skip_group_check=True)
                mm.then_inc(S("moe_ps"), 1)


HID_BANKS = [0, 2, 3, 4, 5, 6]
UP_BANKS = [0, 2, 4]


def shape_constants():
    con = np.zeros((P, 526), np.float32)
    con[:, 0:128] = np.eye(P)
    inv_freq = 1.0 / 10000.0 ** (np.arange(0, HD2, 2, dtype=np.float32) / HD2)
    freqs = np.outer(np.arange(SEQ, dtype=np.float32), inv_freq)
    emb = np.concatenate([freqs, freqs], axis=-1)
    sign = np.where(np.arange(HD2) < HD2 // 2, -1.0, 1.0).astype(np.float32)
    con[:, 128:256] = np.tile(np.cos(emb), (2, 8))
    con[:, 256:384] = np.tile(np.sin(emb) * sign, (2, 8))
    row = np.arange(D)
    con[0:D, 384:388] = (row[:, None] % 32 // HD1) == np.arange(4)
    con[0:D, 388:390] = (row[:, None] % 32 // HD2) == np.arange(2)
    con[:, 390:398] = np.arange(E, 0, -1)
    side = 128 // PATCH
    token = np.arange(P) % SEQ
    con[0, 398:526] = (token // side).astype(np.float32) / np.float32(side - 1)
    con[1, 398:526] = (token % side).astype(np.float32) / np.float32(side - 1)
    con[2, 398:526] = 1.0
    bf = np.zeros((P, 640), np.float32)
    bf[:, 0:128] = np.eye(P)
    pos = np.arange(P) % SEQ
    bf[:, 128:384] = np.where(np.tile(np.arange(SEQ), 4)[None, :] > pos[:, None], NEG, 0.0)
    bf[:, 384:512] = np.triu(np.ones((P, P)))
    bf[:, 512:640] = 1.0
    return con, bf


def lay_out(a):
    f = np.float32
    con, bf = shape_constants()
    side = 128 // PATCH
    x = a["x"].reshape(IMG, 3, side, PATCH, side, PATCH).transpose(0, 2, 4, 1, 3, 5).reshape(NT, P, KC, P)
    m = {"patches": x.transpose(3, 0, 2, 1), "consts": con, "consts_bf": bf}
    m["w_embed"] = a["L0_tok_Wp"].reshape(KC, P, D).transpose(1, 0, 2).reshape(P, KC * D)
    w = np.zeros((66, 130), f)
    w[0:64, 0:64], w[64, 0:64], w[65, 0:64] = a["L0_tok_W2"], a["L0_tok_b2"], a["L0_tok_bp"]
    w[0:2, 64:128], w[2, 64:128], w[2, 128:130] = a["L0_tok_W1"], a["L0_tok_b1"], 1.0
    m["w_pos"] = w
    m["w_attn0"] = np.concatenate([
        a["L0_attn_key_matrices"].transpose(2, 0, 1).reshape(D, 512),
        a["L0_attn_query_matrices"].transpose(2, 0, 1).reshape(D, 512),
        a["L0_attn_value_in_matrices"].transpose(2, 0, 1).reshape(D, 512),
        a["L0_attn_value_out_matrices"].transpose(1, 0, 2).reshape(D, 512)], axis=1)
    m["w_up0"] = a["L0_ffn_w1"].reshape(E, D, 2, P).transpose(2, 1, 0, 3).reshape(P, E * P)
    m["w_down0"] = a["L0_ffn_w2"].reshape(CH0, P, D).transpose(1, 0, 2).reshape(P, CH0 * D)
    w = np.zeros((P, 32), f)
    w[:, 0:16] = a["L0_ffn_b1"].reshape(CH0, P).T
    w[0:D, 16:24] = a["L0_ffn_gate_w"]
    w[:, 24:32] = a["L0_ffn_gate_b"][None, :]
    m["w_small0"] = w
    m["w_b2"] = a["L0_ffn_b2"].reshape(1, E * D)
    w = np.zeros((65, 256), f)
    w[0:64, 0:192], w[64, 0:192] = a["L1_attn_Wqkv"].T, a["L1_attn_bqkv"]
    w[0:64, 192:256], w[64, 192:256] = a["L1_attn_Wproj"].T, a["L1_attn_bproj"]
    m["w_attn1"] = w
    w = np.ones((P, 16), f)
    w[:, 0:8] = a["L1_attn_temperature"].reshape(1, H1)
    m["w_temp"] = w
    w = np.zeros((P, 650), f)
    half = np.arange(HD2)
    swapped = (half + HD2 // 2) % HD2
    wq = a["L1_ffn_wq"].reshape(H2, HD2, D)
    wk = np.repeat(a["L1_ffn_wk"].reshape(KV2, HD2, D), H2 // KV2, axis=0)
    w[0:D, 0:64] = wq.reshape(64, D).T
    w[0:D, 64:128] = wk.reshape(64, D).T
    w[0:D, 128:192] = wq[:, swapped].reshape(64, D).T
    w[0:D, 192:256] = wk[:, swapped].reshape(64, D).T
    w[0:HD2, 256:384] = a["L1_ffn_wv"].reshape(KV2, HD2, D).transpose(1, 0, 2).reshape(HD2, 128)
    w[0:HD2, 384:640] = a["L1_ffn_wo"].reshape(D, H2, HD2).transpose(2, 1, 0).reshape(HD2, 256)
    w[0:D, 640] = a["L1_ffn_ln1_w"]
    w[:, 641] = np.concatenate([a["L1_ffn_ln2_w"]] * 2)
    w[0:D, 642:650] = a["L1_ffn_router_w"].T
    m["w_ffn1"] = w
    m["w_up1"] = np.concatenate([a["L1_ffn_w1"].reshape(E * HID1, D).T, a["L1_ffn_w3"].reshape(E * HID1, D).T])
    w2 = a["L1_ffn_w2"].transpose(0, 2, 1).reshape(E * HID1, D)
    w = np.zeros((P, DOWN_AT[-1] * D), f)
    for c in range(CH1):
        first, count = chunk_experts(c)
        for k in range(count):
            lo = max(c * P, (first + k) * HID1)
            hi = min(c * P + chunk_rows(c), (first + k + 1) * HID1)
            at = (DOWN_AT[c] + k) * D
            w[lo - c * P:hi - c * P, at:at + D] = w2[lo:hi]
    m["w_down1"] = w
    return {k: np.ascontiguousarray(v) for k, v in m.items()}


def kernel(**inputs):
    import concourse.bacc as bacc
    from concourse.bass_utils import run_bass_kernel_spmd

    arrays = lay_out({k: np.asarray(v) for k, v in inputs.items()})
    nc = bacc.Bacc("TRN2", target_bir_lowering=False, num_devices=1)
    args = {k: nc.dram_tensor(k, v.shape, mybir.dt.from_np(v.dtype), kind="ExternalInput").ap()
            for k, v in arrays.items()}
    out = nc.dram_tensor("out", (TOK, D), F32, kind="ExternalOutput").ap()
    build(nc, **args, out=out)
    result = run_bass_kernel_spmd(nc, [arrays], core_ids=[0])
    return result.results[0]["out"].reshape(IMG, SEQ, D)
```

```python
from contextlib import ExitStack

import numpy as np

import concourse.bass as bass
from concourse import mybir

F32 = mybir.dt.float32
BF16 = mybir.dt.bfloat16
F32R = mybir.dt.float32r
U32 = mybir.dt.uint32
ALU = mybir.AluOpType
ACT = mybir.ActivationFunctionType
AX_X = mybir.AxisListType.X

P = 128
D = 64
IMG = 8
SEQ = 64
TOK = IMG * SEQ
NT = TOK // P
PATCH = 16
KC = 3 * PATCH * PATCH // P
H0 = 8
PAIRS0 = H0 // 2
E = 8
F0 = 256
CAP = -(-5 * TOK // (4 * E))
CH0 = E * F0 // P
SLOTS = E * CAP
SC = SLOTS // P
H1, HD1 = 8, 8
H2, KV2, HD2 = 4, 2, 16
HID1 = 170
CH1 = -(-E * HID1 // P)
LN_EPS, RMS_EPS = 1e-5, 1e-6
NORM_EPS = 1e-12
F32_MAX = float(np.finfo(np.float32).max)
NEG = -1e30


def chunk_rows(c):
    return min(P, E * HID1 - c * P)


def chunk_experts(c):
    first = c * P // HID1
    return first, (c * P + chunk_rows(c) - 1) // HID1 - first + 1


DOWN_AT = [sum(chunk_experts(b)[1] for b in range(c)) for c in range(CH1 + 1)]


def build(nc, patches, consts, slot_row, consts_bf, w_embed, w_pos, w_attn0, w_up0, w_down0, w_small0,
          w_attn1, w_temp, w_ffn1, w_up1, w_down1, out):
    with ExitStack() as ctx:
        sems = {}

        def S(name):
            if name not in sems:
                sems[name] = ctx.enter_context(nc.semaphore(name))
            return sems[name]

        def sb(name, shape, dt=F32):
            return ctx.enter_context(nc.sbuf_tensor(name, shape, dt))

        def wide(ap, axis, n):
            ap = ap.unsqueeze(axis)
            shape = list(ap.shape)
            shape[axis] = n
            return ap.broadcast_to(shape)

        ps = ctx.enter_context(nc.psum_tensor("ps", [P, 8, 512], F32))

        pat = sb("pat", [P, NT, KC, P])
        con = sb("con", list(consts.shape))
        cbf32 = sb("cbf32", list(consts_bf.shape))
        cbf = sb("cbf", list(consts_bf.shape), BF16)
        wem = sb("wem", list(w_embed.shape))
        wpo = sb("wpo", list(w_pos.shape))
        hid_more = sb("hid_more", [P, CH1 - KC, TOK])
        wa0 = hid_more[0:D].rearrange("p c n -> p (c n)")[:, 0:2048]
        wu0 = sb("wu0", [P, E * F0])
        wu0_hi = sb("wu0_hi", [P, E * F0], F32R)
        wu0_lo = sb("wu0_lo", [P, E * F0], F32R)
        wd0 = sb("wd0", [P, CH0, D])
        ws0 = sb("ws0", list(w_small0.shape))
        wa1 = sb("wa1", list(w_attn1.shape))
        wte = sb("wte", list(w_temp.shape))
        wf1 = sb("wf1", list(w_ffn1.shape))
        wu1 = sb("wu1", [P, 2 * E * HID1])
        wu1_hi = sb("wu1_hi", [P, 2 * E * HID1], F32R)
        wu1_lo = sb("wu1_lo", [P, 2 * E * HID1], F32R)
        wd1 = sb("wd1", list(w_down1.shape))

        ident = con[:, 0:128]
        rope = con[:, 128:384]
        headmask1 = con[0:D, 384:388]
        headmask2 = con[0:D, 388:390]
        rank = con[:, 390:398]
        slot_base = con[:, 526:534]
        slot_id = con[:, 534:534 + SC]
        grid1 = con[0:3, 398:526]
        ident_b = cbf[:, 0:128]
        causal_b = cbf[:, 128:384]
        upto_b = cbf[:, 384:512]
        ones_b = cbf[:, 512:640]
        pos_w2 = wpo[0:66, 0:64]
        pos_w1 = wpo[0:3, 64:130]
        kT, qT0 = wa0[:, 0:512], wa0[:, 512:1024]
        vinT, vout = wa0[:, 1024:1536], wa0[:, 1536:2048]
        moe0_b1 = ws0[:, 0:16]
        gate_w = ws0[0:D, 16:24]
        gate_b = ws0[:, 24:32]
        moe0_b2 = ws0[0:D, 32:40]
        qkv_w1 = wa1[0:65, 0:192]
        proj_w1 = wa1[0:65, 192:256]
        qk_w2 = wf1[0:D, 0:256]
        wv2 = wf1[0:HD2, 256:384]
        wo2 = wf1[0:HD2, 384:640]
        ln1_w, ln2_w = wf1[0:D, 640:641], wf1[:, 641:642]
        router_w = wf1[:, 642:650]

        ones = sb("ones", [P, P])
        half = sb("half", [P, 16])
        slots = sb("slots", [P, SLOTS])
        kq0 = sb("kq0", [D, 512])
        vo0 = sb("vo0", [D, 512])
        vo2 = sb("vo2", [D, 256])
        poshid = sb("poshid", [66, P])

        h = sb("h", [P, NT, D])
        x = sb("x", [P, NT, D])
        stats = sb("stats", [P, NT, 6])
        meanvar = sb("meanvar", [P, NT, 2])
        vareps = sb("vareps", [P, NT, 2])
        rstd = sb("rstd", [P, NT, 2])
        xn = sb("xn", [P, NT, 2, D])
        xT = sb("xT", [P, NT, P])
        zs = sb("zs", [P, NT, PAIRS0, P])
        vs = sb("vs", [P, NT, 2, PAIRS0 * D])
        prob = sb("prob", [P, NT, 512])
        mx = sb("mx", [P, NT, 8])
        den = sb("den", [P, NT, 8])
        rden = sb("rden", [P, NT, 8])
        probT = sb("probT", [P, NT, 4, P])
        lg = sb("lg", [P, NT, E])
        lgm = sb("lgm", [P, NT])
        ex = sb("ex", [P, NT, E])
        exs = sb("exs", [P, NT])
        prb = sb("prb", [P, NT])
        tie = sb("tie", [P, NT, E])
        top = sb("top", [P, NT])
        tiem = sb("tiem", [P, NT])
        hot = sb("hot", [P, NT, E])
        hot2 = sb("hot2", [P, NT, E])
        rest = sb("rest", [P, NT, E])
        both = sb("both", [P, NT, E])
        hot_b = sb("hot_b", [P, NT, E], BF16)
        gate = sb("gate", [P, NT, E])
        xs = sb("xs", [P, NT, 2, D], F32R)
        over = sb("over", [P, NT, E])
        place = sb("place", [P, NT, E])
        slot = sb("slot", [P, NT])
        slot_all = sb("slot_all", [P, TOK])
        take = sb("take", [P, NT, SLOTS], F32R)
        put = sb("put", [P, SC, TOK], F32R)
        xg = sb("xg", [P, SLOTS], F32R)
        hid0 = sb("hid0", [P, CH0, CAP])
        yT = sb("yT", [D, SLOTS])
        yslot = sb("yslot", [P, SC, 2, D], F32R)
        y = sb("y", [P, NT, D])
        yinf = sb("yinf", [P, NT, 3, D])
        finite = sb("finite", [P, NT, D], U32)
        xsT = sb("xsT", [P, NT, P], F32R)
        pat_flat = pat[:].rearrange("p t c n -> p (t c n)")
        def hid(c):
            return pat_flat[:, c * TOK:(c + 1) * TOK] if c < KC else hid_more[:, c - KC]

        yg = probT[:].rearrange("p t a (b d) -> p t (a b) d", d=D)
        ysum = sb("ysum", [P, NT, D])
        xT1 = sb("xT1", [65, NT, P])
        qk = sb("qk", [P, NT, P])
        qksq = sb("qksq", [P, NT, P])
        qkss = sb("qkss", [P, NT, 16])
        qkr = sb("qkr", [P, NT, 16])
        v1 = sb("v1", [P, NT, 2, H1, HD1 + 1])
        kTs = sb("kTs", [D, NT, P])
        qm = wu0[0:D].rearrange("p (t h n) -> p t h n", t=NT, h=4)
        rnorm = sb("rnorm", [D, NT, 16])
        ya = sb("ya", [D, NT, 2, D])
        yaT = sb("yaT", [65, NT, P])
        rot = wu1[:, 0:NT * 2 * P].rearrange("p (t a n) -> p t a n", t=NT, a=2)
        up = zs[:].rearrange("p a b n -> p a (b n)")

        block = ctx.enter_context(nc.Block())

        @block.sync
        def _(sp):
            sp.dma_start(wem[:], w_embed).then_inc(S("wem_in"), 16)
            for t in range(NT):
                sp.dma_start(pat[:, t], patches[:, t]).then_inc(S(f"pat{t}_in"), 16)
            for g in range(2):
                sp.dma_start(wu0[g * D:(g + 1) * D], w_up0).then_inc(S("wu0_in"), 16)
            sp.dma_start(wd0[:], w_down0.rearrange("p (c d) -> p c d", d=D)).then_inc(S("wd0_in"), 16)
            sp.dma_start(wa1[:], w_attn1).then_inc(S("wa1_in"), 16)
            for g in range(2):
                sp.dma_start(wu1[g * D:(g + 1) * D], w_up1).then_inc(S("wu1_in"), 16)
            sp.dma_start(wd1[:], w_down1).then_inc(S("wd1_in"), 16)
            for t in range(NT):
                sp.wait_ge(S("h5"), t + 1)
                sp.dma_start(out[t * P:(t + 1) * P, :], h[:, t]).then_inc(S("stored"), 16)
            sp.wait_ge(S("stored"), 16 * NT)

        @block.gpsimd
        def _(pool):
            nc.gpsimd.memset(half[:], -0.5).then_inc(S("half_set"), 1)
            nc.gpsimd.memset(ones[:], 1.0).then_inc(S("ones_set"), 1)
            pool.wait_ge(S("half_set"), 1)

            def inverse_roots(n, var, eps):
                for t in range(NT):
                    pool.wait_ge(S("var"), NT * n + t + 1)
                    nc.gpsimd.tensor_scalar(vareps[:, t, 0:1], var[:, t], eps, None,
                                            ALU.add).then_inc(S("vareps"), 1)
                    pool.wait_ge(S("vareps"), NT * min(n, 3) + t + 1)
                    nc.gpsimd.tensor_tensor(rstd[:, t, 0:1], vareps[:, t, 0:1], half[:, 0:1],
                                            ALU.pow).then_inc(S("rstd"), 1)

            def normalise(n, width):
                for t in range(NT):
                    pool.wait_ge(S("rden"), NT * n + t + 1)
                    nc.gpsimd.tensor_tensor(prob[:, t, 0:width].rearrange("p (g k) -> p g k", k=SEQ),
                                            prob[:, t, 0:width].rearrange("p (g k) -> p g k", k=SEQ),
                                            wide(rden[:, t, 0:width // SEQ], 2, SEQ),
                                            ALU.mult).then_inc(S("prob"), 1)

            def split(whole, hi, lo, loaded, name):
                pool.wait_ge(S(loaded), 32)
                nc.gpsimd.tensor_copy(hi[:], whole[:]).then_inc(S(name), 1)
                pool.wait_ge(S(name), 1)
                nc.gpsimd.tensor_tensor(lo[:], whole[:], hi[:].bitcast(F32), ALU.subtract).then_inc(S(name), 1)

            inverse_roots(0, meanvar[:, :, 1:2], LN_EPS)
            split(wu0, wu0_hi, wu0_lo, "wu0_in", "wu0_split")
            normalise(0, 512)
            inverse_roots(1, meanvar[:, :, 1:2], LN_EPS)
            split(wu1, wu1_hi, wu1_lo, "wu1_in", "wu1_split")
            for t in range(NT):
                pool.wait_ge(S("y"), t + 1)
                nc.gpsimd.tensor_scalar(yinf[:, t, 0], y[:, t], F32_MAX, 1e4, ALU.is_gt,
                                        ALU.mult).then_inc(S("yinf_sides"), 1)
                nc.gpsimd.tensor_scalar(yinf[:, t, 1], y[:, t], -F32_MAX, 1e4, ALU.is_lt,
                                        ALU.mult).then_inc(S("yinf_sides"), 1)
                pool.wait_ge(S("yinf_sides"), 2 * (t + 1))
                nc.gpsimd.tensor_tensor(yinf[:, t, 2], yinf[:, t, 0], yinf[:, t, 1],
                                        ALU.subtract).then_inc(S("yinf"), 1)
            inverse_roots(2, meanvar[:, :, 1:2], LN_EPS)
            for t in range(NT):
                pool.wait_ge(S("qkss"), t + 1)
                nc.gpsimd.tensor_tensor(qkr[:, t], qkss[:, t], half[:], ALU.pow).then_inc(S("qkr"), 1)
            for t in range(NT):
                pool.wait_ge(S("var"), NT * 3 + t + 1)
                nc.gpsimd.tensor_scalar(vareps[:, t, 0:1], meanvar[:, t, 1:2], LN_EPS, None,
                                        ALU.add).then_inc(S("vareps2"), 1)
                nc.gpsimd.tensor_scalar(vareps[:, t, 1:2], meanvar[:, t, 1:2], 1.0 + RMS_EPS,
                                        LN_EPS * RMS_EPS, ALU.mult, ALU.add).then_inc(S("vareps2"), 1)
                pool.wait_ge(S("vareps2"), 2 * (t + 1))
                nc.gpsimd.tensor_tensor(rstd[:, t], vareps[:, t], half[:, 0:2],
                                        ALU.pow).then_inc(S("rstd"), 1)
            normalise(1, 256)
            inverse_roots(4, meanvar[:, :, 1:2], RMS_EPS)
            for t in range(NT):
                nc.gpsimd.tensor_tensor(h[:, t], h[:, t], x[:, t], ALU.add).then_inc(S("h4"), 1)

        @block.scalar
        def _(act):
            act.dma_start(con[:], consts).then_inc(S("con_in"), 16)
            act.dma_start(wpo[:], w_pos).then_inc(S("wpo_in"), 16)
            act.dma_start(wa0, w_attn0).then_inc(S("wa0_in"), 16)
            act.dma_start(cbf32[:], consts_bf).then_inc(S("cbf_in"), 16)
            act.dma_start(wf1[:], w_ffn1).then_inc(S("wf1_in"), 16)
            act.dma_start(ws0[:], w_small0).then_inc(S("ws0_in"), 16)
            act.dma_start(slots[:], slot_row.partition_broadcast(P)).then_inc(S("slots_in"), 16)
            act.dma_start(wte[:], w_temp).then_inc(S("wte_in"), 16)

            act.wait_ge(S("poshid_ps"), 1)
            nc.scalar.activation(poshid[:], ps[0:66, 7, 0:P], ACT.Relu).then_inc(S("poshid"), 1)
            act.wait_ge(S("kq0_ps"), 1)
            nc.scalar.copy(kq0[:], ps[0:D, 1, :]).then_inc(S("kq0"), 1)
            act.wait_ge(S("vo0_ps"), 1)
            nc.scalar.copy(vo0[:], ps[0:D, 3, :]).then_inc(S("vo0"), 1)
            act.wait_ge(S("vo2_ps"), 1)
            nc.scalar.copy(vo2[:], ps[0:D, 5, 0:256]).then_inc(S("vo2"), 1)

            for t in range(NT):
                act.wait_ge(S("embed_ps"), t + 1)
                nc.scalar.copy(h[:, t], ps[:, 2 * t, 0:D]).then_inc(S("h0"), 1)

            for t in range(NT):
                act.wait_ge(S("xT_ps"), t + 1)
                nc.scalar.copy(xT[:, t], ps[:, 2 * t + 1, 0:P]).then_inc(S("xT"), 1)
            for t in range(NT):
                act.wait_ge(S("z_ps"), t + 1)
                nc.scalar.copy(zs[:, t].rearrange("p a b -> p (a b)"), ps[:, 2 * t, :]).then_inc(S("z"), 1)
            for t in range(NT):
                act.wait_ge(S("shifted"), t + 1)
                nc.scalar.activation(prob[:, t], prob[:, t], ACT.Exp).then_inc(S("exp"), 1)
            for t in range(NT):
                act.wait_ge(S("probT_ps"), t + 1)
                nc.scalar.copy(probT[:, t].rearrange("p a b -> p (a b)"), ps[:, 2 * t, :]).then_inc(S("probT"), 1)

            for t in range(NT):
                act.wait_ge(S("xT_ps"), NT + t + 1)
                nc.scalar.copy(xT[:, t], ps[:, 2 * t, 0:P]).then_inc(S("xT"), 1)
            act.wait_ge(S("lg"), 1)
            nc.scalar.activation(ex[:].rearrange("p t e -> p (t e)"), lg[:].rearrange("p t e -> p (t e)"),
                                 ACT.Exp).then_inc(S("ex"), 1)
            act.wait_ge(S("slot_ps"), 1)
            nc.scalar.copy(slot_all[:], ps[:, 3, :]).then_inc(S("slot_all"), 1)
            act.wait_ge(S("xg_ps"), 1)
            nc.scalar.copy(xg[:, 0:SLOTS // 2], ps[:, 0, 0:SLOTS // 2]).then_inc(S("xg0"), 1)
            act.wait_ge(S("ws0_in"), 16)
            for b, (bank, chunks) in enumerate(HID0_BANKS):
                if b % 2 == 0:
                    act.wait_ge(S("hid0_ps"), b + 1)
                    for k, c in enumerate(chunks):
                        nc.scalar.activation(hid0[:, c], ps[:, bank, k * CAP:(k + 1) * CAP], ACT.Relu,
                                             bias=moe0_b1[:, c:c + 1]).then_inc(S("hid0_even"), 1)
            act.wait_ge(S("yslot_ps"), 1)
            nc.scalar.copy(yslot[:, :, 0], ps[:, 4, 0:SC * D].rearrange("p (c d) -> p c d", d=D)
                           ).then_inc(S("yslot_hi"), 1)

            act.wait_ge(S("ones_rows"), 2)
            for t in range(NT):
                act.wait_ge(S("xT_ps"), 2 * NT + t + 1)
                nc.scalar.copy(xT1[0:D, t], ps[0:D, 2 * t + 1, 0:P]).then_inc(S("xT"), 1)
            act.wait_ge(S("v1_ones"), 2)
            for t in range(NT):
                act.wait_ge(S("qkv_ps"), t + 1)
                for i in range(2):
                    rows = slice(i * D, (i + 1) * D)
                    nc.scalar.copy(v1[rows, t, i, :, 1:],
                                   ps[rows, 2 * t, 128:192].rearrange("p (h d) -> p h d", d=HD1)
                                   ).then_inc(S("v1"), 1)
                nc.scalar.activation(qksq[:, t], ps[:, 2 * t, 0:P], ACT.Square).then_inc(S("qksq"), 1)
            for t in range(NT):
                act.wait_ge(S("taylor_ps"), t + 1)
                nc.scalar.activation(prob[:, t].rearrange("p (g k) -> p g k", g=2),
                                     ps[:, 2 * t:2 * t + 2, 0:256], ACT.Square,
                                     bias=ones[:, 0:1]).then_inc(S("taylor"), 1)
            for t in range(NT):
                act.wait_ge(S("yaT_ps"), t + 1)
                nc.scalar.copy(yaT[0:D, t], ps[0:D, 2 * t + 1, 0:P]).then_inc(S("yaT"), 1)

            act.wait_ge(S("wf1_in"), 16)
            for t in range(NT):
                act.wait_ge(S("xT_ps"), 3 * NT + t + 1)
                nc.scalar.mul(xT[0:D, t], ps[0:D, 2 * t + 1, 0:P], ln1_w).then_inc(S("xT"), 1)
            for t in range(NT):
                act.wait_ge(S("v2_ps"), t + 1)
                nc.scalar.copy(vs[:, t, :, 0:P], ps[:, 2 * t + 1, 0:256].rearrange("p (i n) -> p i n", i=2)
                               ).then_inc(S("v2"), 1)
            for t in range(NT):
                act.wait_ge(S("shifted"), NT + t + 1)
                nc.scalar.activation(prob[:, t, 0:256], prob[:, t, 0:256], ACT.Exp,
                                     scale=HD2 ** -0.5).then_inc(S("exp"), 1)
            for t in range(NT):
                act.wait_ge(S("probT_ps"), NT + t + 1)
                nc.scalar.copy(probT[:, t, 0:2].rearrange("p a b -> p (a b)"), ps[:, 2 * t, 0:256]
                               ).then_inc(S("probT"), 1)

            for t in range(NT):
                act.wait_ge(S("xT_ps"), 4 * NT + t + 1)
                nc.scalar.mul(xsT[:, t], ps[:, 2 * t, 0:P], ln2_w).then_inc(S("xT"), 1)
            act.wait_ge(S("lg"), 2)
            nc.scalar.activation(ex[:].rearrange("p t e -> p (t e)"), lg[:].rearrange("p t e -> p (t e)"),
                                 ACT.Exp).then_inc(S("ex"), 1)
            for c in range(CH1):
                n = chunk_rows(c)
                act.wait_ge(S("up_ps"), c + 1)
                if c >= 4:
                    act.wait_ge(S("hid1"), c - 3)
                nc.scalar.activation(up[0:n, c % 4], ps[0:n, UP_BANKS[c % 3], :], ACT.Silu).then_inc(S("silu"), 1)

        @block.vector
        def _(dve):
            def layer_norm(n):
                for t in range(NT):
                    dve.wait_ge(S(f"h{n}"), t + 1)
                    nc.vector.bn_stats(stats[:, t], h[:, t]).then_inc(S("stats"), 1)
                for t in range(NT):
                    dve.wait_ge(S("stats"), NT * n + t + 1)
                    nc.vector.bn_aggr(meanvar[:, t], stats[:, t]).then_inc(S("var"), 1)
                k = 1 if n == 3 else 0
                for t in range(NT):
                    dve.wait_ge(S("rstd"), NT * n + t + 1)
                    nc.vector.tensor_scalar(xn[:, t], wide(h[:, t], 1, 2), meanvar[:, t, 0:1], rstd[:, t, k:k + 1],
                                            ALU.subtract, ALU.mult).then_inc(S("xn"), 1)

            def rms_norm(n):
                for t in range(NT):
                    dve.wait_ge(S("x1"), t + 1)
                    nc.vector.tensor_tensor_reduce(xn[:, t, 0], x[:, t], x[:, t], 1.0 / D, 0.0, ALU.mult,
                                                   ALU.add, meanvar[:, t, 1:2]).then_inc(S("var"), 1)
                for t in range(NT):
                    dve.wait_ge(S("rstd"), NT * n + t + 1)
                    nc.vector.tensor_scalar(xn[:, t], wide(x[:, t], 1, 2), rstd[:, t, 0:1], None,
                                            ALU.mult).then_inc(S("xn"), 1)

            def softmax_front(n, heads):
                for t in range(NT):
                    scores = ps[:, 2 * t:2 * t + 2, 0:heads * SEQ // 2].rearrange("p g (h k) -> p g h k", k=SEQ)
                    m = mx[:, t, 0:heads].rearrange("p (g h) -> p g h", g=2)
                    if n == 0:
                        shifted = prob[:, t, 0:heads * SEQ].rearrange("p (h g k) -> p g h k", g=2, k=SEQ)
                    else:
                        shifted = prob[:, t, 0:heads * SEQ].rearrange("p (g h k) -> p g h k", g=2, k=SEQ)
                    dve.wait_ge(S("scores_ps"), NT * n + t + 1)
                    nc.vector.tensor_reduce(m, scores, AX_X, ALU.max).then_inc(S("mx"), 1)
                    dve.wait_ge(S("mx"), NT * n + t + 1)
                    nc.vector.tensor_tensor(shifted, scores, wide(m, 3, SEQ), ALU.subtract).then_inc(S("shifted"), 1)

            def softmax_sums(n, heads):
                for t in range(NT):
                    dve.wait_ge(S("exp"), NT * n + t + 1)
                    nc.vector.tensor_reduce(den[:, t, 0:heads],
                                            prob[:, t, 0:heads * SEQ].rearrange("p (g k) -> p g k", k=SEQ),
                                            AX_X, ALU.add).then_inc(S("den"), 1)
                    dve.wait_ge(S("den"), NT * n + t + 1)
                    nc.vector.reciprocal(rden[:, t, 0:heads], den[:, t, 0:heads]).then_inc(S("rden"), 1)

            def add_to(stream, source, bank, name):
                for t in range(NT):
                    dve.wait_ge(S(source[0]), source[1] + t + 1)
                    nc.vector.tensor_tensor(stream[:, t], stream[:, t], ps[:, 2 * t + bank, 0:D],
                                            ALU.add).then_inc(S(name), 1)

            step = [0]

            def link(ins):
                step[0] += 1
                ins.then_inc(S("gating_step"), 1)
                dve.wait_ge(S("gating_step"), step[0])

            def first_best(values, best, onehot):
                link(nc.vector.tensor_reduce(best[:], values[:], AX_X, ALU.max))
                link(nc.vector.tensor_tensor(tie[:], values[:], wide(best[:], 2, E), ALU.is_equal))
                link(nc.vector.tensor_tensor(tie[:], tie[:], wide(rank, 1, NT), ALU.mult))
                link(nc.vector.tensor_reduce(tiem[:], tie[:], AX_X, ALU.max))
                link(nc.vector.tensor_tensor(onehot[:], tie[:], wide(tiem[:], 2, E), ALU.is_equal))

            def gated_sum(name):
                for t in range(NT):
                    dve.wait_ge(S("moe1_ps"), t + 1)
                    nc.vector.tensor_tensor(yg[:, t], ps[:, 2 * t, :].rearrange("p (e d) -> p e d", d=D),
                                            wide(gate[:, t], 2, D), ALU.mult).then_inc(S("yg"), 1)
                    dve.wait_ge(S("yg"), t + 1)
                    nc.vector.tensor_reduce(ysum[:, t], yg[:, t].rearrange("p e d -> p d e"), AX_X,
                                            ALU.add).then_inc(S(name), 1)

            nc.vector.memset(v1[:], 0.0).then_inc(S("v1_zero"), 1)
            dve.wait_ge(S("v1_zero"), 1)
            for i in range(2):
                nc.vector.memset(v1[i * D:(i + 1) * D, :, i, :, 0:1], 1.0).then_inc(S("v1_ones"), 1)
            nc.vector.memset(xT1[64:65], 1.0).then_inc(S("ones_rows"), 1)
            nc.vector.memset(yaT[64:65], 1.0).then_inc(S("ones_rows"), 1)
            dve.wait_ge(S("cbf_in"), 16)
            nc.vector.tensor_copy(cbf[:], cbf32[:]).then_inc(S("cbf"), 1)

            layer_norm(0)
            for t in range(NT):
                dve.wait_ge(S("v_ps"), t + 1)
                nc.vector.tensor_copy(vs[:, t].rearrange("p i n -> p (i n)"), ps[:, 2 * t + 1, :]).then_inc(S("v"), 1)
            softmax_front(0, H0)
            softmax_sums(0, H0)
            add_to(h, ("attn_ps", 0), 1, "h1")

            layer_norm(1)
            dve.wait_ge(S("ws0_in"), 16)
            dve.wait_ge(S("con_in"), 16)
            dve.wait_ge(S("logits_ps"), 1)
            link(nc.vector.tensor_tensor(lg[:], ps[:, 1, 0:NT * E].rearrange("p (t e) -> p t e", e=E),
                                         wide(gate_b, 1, NT), ALU.add))
            link(nc.vector.tensor_reduce(lgm[:], lg[:], AX_X, ALU.max))
            nc.vector.tensor_tensor(lg[:], lg[:], wide(lgm[:], 2, E), ALU.subtract).then_inc(S("lg"), 1)

            for t in range(NT):
                nc.vector.tensor_copy(xs[:, t, 0], xn[:, t, 0]).then_inc(S("xs_hi"), 1)
            for t in range(NT):
                dve.wait_ge(S("xs_hi"), t + 1)
                nc.vector.tensor_tensor(xs[:, t, 1], xn[:, t, 0], xs[:, t, 0].bitcast(F32),
                                        ALU.subtract).then_inc(S("xs"), 1)
            dve.wait_ge(S("ex"), 1)
            first_best(ex, top, hot)
            nc.vector.tensor_copy(hot_b[:], hot[:]).then_inc(S("hot_b"), 1)
            link(nc.vector.tensor_reduce(exs[:], ex[:], AX_X, ALU.add))
            link(nc.vector.reciprocal(prb[:], exs[:]))
            dve.wait_ge(S("counts_ps"), 1)
            counts = ps[:, 7, 0:NT * E].rearrange("p (t e) -> p t e", e=E)
            link(nc.vector.tensor_scalar(over[:], counts, float(CAP), float(2 * SLOTS), ALU.is_gt, ALU.mult))
            link(nc.vector.tensor_tensor(place[:], counts, over[:], ALU.add))
            link(nc.vector.tensor_tensor(place[:], place[:], wide(slot_base, 1, NT), ALU.add))
            link(nc.vector.tensor_tensor(place[:], place[:], hot[:], ALU.mult))
            nc.vector.tensor_reduce(slot[:], place[:], AX_X, ALU.add).then_inc(S("slot"), 1)
            dve.wait_ge(S("slots_in"), 16)
            dve.wait_ge(S("slot"), 1)
            for t in range(NT):
                nc.vector.tensor_scalar(take[:, t], slots[:], slot[:, t:t + 1], None,
                                        ALU.is_equal).then_inc(S("take"), 1)
            dve.wait_ge(S("slot_all"), 1)
            for c in range(SC):
                nc.vector.tensor_scalar(put[:, c], slot_all[:], slot_id[:, c:c + 1], None,
                                        ALU.is_equal).then_inc(S("put"), 1)
            dve.wait_ge(S("xg_ps"), 2)
            nc.vector.tensor_copy(xg[:, SLOTS // 2:], ps[:, 2, 0:SLOTS // 2]).then_inc(S("xg1"), 1)
            for b, (bank, chunks) in enumerate(HID0_BANKS):
                if b % 2 == 1:
                    dve.wait_ge(S("hid0_ps"), b + 1)
                    for k, c in enumerate(chunks):
                        nc.vector.tensor_scalar(hid0[:, c], ps[:, bank, k * CAP:(k + 1) * CAP],
                                                moe0_b1[:, c:c + 1], 0.0, ALU.add,
                                                ALU.max).then_inc(S("hid0_odd"), 1)
            for g in range(2):
                dve.wait_ge(S("yT_ps"), g + 1)
                half_e = E // 2
                nc.vector.tensor_tensor(
                    yT[:, g * SLOTS // 2:(g + 1) * SLOTS // 2].rearrange("p (e s) -> p e s", s=CAP),
                    ps[0:D, 2 * g, 0:SLOTS // 2].rearrange("p (e s) -> p e s", s=CAP),
                    wide(moe0_b2[:, g * half_e:(g + 1) * half_e], 2, CAP), ALU.add).then_inc(S("yT"), 1)
            dve.wait_ge(S("yslot_hi"), 1)
            nc.vector.tensor_tensor(yslot[:, :, 1], ps[:, 4, 0:SC * D].rearrange("p (c d) -> p c d", d=D),
                                    yslot[:, :, 0].bitcast(F32), ALU.subtract).then_inc(S("yslot_lo"), 1)
            for t in range(NT):
                dve.wait_ge(S("moe0_ps"), t + 1)
                link(nc.vector.tensor_scalar(y[:, t], ps[:, 2 * t, 0:D], prb[:, t:t + 1], None, ALU.mult))
                nc.vector.scalar_tensor_tensor(y[:, t], ps[:, 2 * t, D:2 * D], prb[:, t:t + 1], y[:, t],
                                               ALU.mult, ALU.add).then_inc(S("y"), 1)
            for t in range(NT):
                dve.wait_ge(S("y"), t + 1)
                nc.vector.tensor_scalar(finite[:, t], y[:, t], 0.0, 0.0, ALU.mult,
                                        ALU.is_equal).then_inc(S("finite"), 1)
            for t in range(NT):
                dve.wait_ge(S("finite"), t + 1)
                dve.wait_ge(S("yinf"), t + 1)
                nc.vector.copy_predicated(yinf[:, t, 2], finite[:, t], y[:, t]).then_inc(S("y_clean"), 1)
            for t in range(NT):
                dve.wait_ge(S("y_clean"), t + 1)
                nc.vector.tensor_tensor(h[:, t], h[:, t], yinf[:, t, 2], ALU.add).then_inc(S("h2"), 1)

            layer_norm(2)
            for t in range(NT):
                dve.wait_ge(S("qksq"), t + 1)
                link(nc.vector.tensor_reduce(qkss[:, t], qksq[:, t].rearrange("p (g d) -> p g d", d=HD1),
                                             AX_X, ALU.add))
                nc.vector.tensor_scalar(qkss[:, t], qkss[:, t], NORM_EPS ** 2 / HD1 ** 0.5, None,
                                        ALU.max).then_inc(S("qkss"), 1)
            dve.wait_ge(S("wte_in"), 16)
            for t in range(NT):
                dve.wait_ge(S("qkr"), t + 1)
                link(nc.vector.tensor_tensor(qkr[:, t], qkr[:, t], wte[:], ALU.mult))
                nc.vector.tensor_tensor(qk[:, t].rearrange("p (g d) -> p g d", d=HD1),
                                        ps[:, 2 * t, 0:P].rearrange("p (g d) -> p g d", d=HD1),
                                        wide(qkr[:, t], 2, HD1), ALU.mult).then_inc(S("qk"), 1)
            dve.wait_ge(S("wu0_split"), 2)
            dve.wait_ge(S("wu1_split"), 2)
            for t in range(NT):
                dve.wait_ge(S("qkT_ps"), t + 1)
                nc.vector.tensor_copy(kTs[:, t], ps[0:D, 2 * t + 1, P:2 * P]).then_inc(S("qkT"), 1)
                nc.vector.tensor_tensor(qm[:, t], wide(ps[0:D, 2 * t + 1, 0:P], 1, 4), wide(headmask1, 2, P),
                                        ALU.mult).then_inc(S("qkT"), 1)
            for t in range(NT):
                dve.wait_ge(S("ynum_ps"), t + 1)
                num = ps[0:D, 2 * t, 0:144].rearrange("p (g d) -> p g d", d=HD1 + 1)
                link(nc.vector.reciprocal(rnorm[:, t].unsqueeze(2), num[:, :, 0:1]))
                nc.vector.tensor_tensor(ya[:, t].rearrange("p i (h d) -> p (i h) d", d=HD1), num[:, :, 1:],
                                        wide(rnorm[:, t], 2, HD1), ALU.mult).then_inc(S("ya"), 1)
            add_to(h, ("proj_ps", 0), 0, "h3")

            layer_norm(3)
            for t in range(NT):
                nc.vector.tensor_scalar(x[:, t], h[:, t], meanvar[:, t, 0:1], rstd[:, t, 0:1],
                                        ALU.subtract, ALU.mult).then_inc(S("x0"), 1)
            for t in range(NT):
                dve.wait_ge(S("qk2_ps"), t + 1)
                nc.vector.tensor_tensor(rot[:, t].rearrange("p a b -> p (a b)"), ps[:, 2 * t, 0:256], rope,
                                        ALU.mult).then_inc(S("rot"), 1)
                dve.wait_ge(S("rot"), t + 1)
                nc.vector.tensor_tensor(qk[:, t], rot[:, t, 0], rot[:, t, 1], ALU.add).then_inc(S("qk"), 1)
            for t in range(NT):
                dve.wait_ge(S("qkT_ps"), NT + t + 1)
                nc.vector.tensor_copy(kTs[:, t], ps[0:D, 2 * t, 0:P]).then_inc(S("qkT"), 1)
                nc.vector.tensor_tensor(qm[:, t, 0:2], wide(ps[0:D, 2 * t, P:2 * P], 1, 2),
                                        wide(headmask2, 2, P), ALU.mult).then_inc(S("qkT"), 1)
            softmax_front(1, H2)
            softmax_sums(1, H2)
            dve.wait_ge(S("x0"), NT)
            add_to(x, ("attn_ps", NT), 1, "x1")

            rms_norm(4)
            for t in range(NT):
                dve.wait_ge(S("xT"), 4 * NT + t + 1)
                nc.vector.scalar_tensor_tensor(xsT[D:P, t], ps[D:P, 2 * t, 0:P], ln2_w[D:P], xsT[D:P, t].bitcast(F32),
                                               ALU.mult, ALU.subtract).then_inc(S("xsT"), 1)
            dve.wait_ge(S("logits_ps"), 2)
            link(nc.vector.tensor_copy(lg[:], ps[:, 7, 0:NT * E].rearrange("p (t e) -> p t e", e=E)))
            link(nc.vector.tensor_reduce(lgm[:], lg[:], AX_X, ALU.max))
            nc.vector.tensor_tensor(lg[:], lg[:], wide(lgm[:], 2, E), ALU.subtract).then_inc(S("lg"), 1)
            dve.wait_ge(S("ex"), 2)
            first_best(ex, top, hot)
            link(nc.vector.scalar_tensor_tensor(rest[:].rearrange("p t e -> p (t e)"),
                                                hot[:].rearrange("p t e -> p (t e)"), -2.0,
                                                ex[:].rearrange("p t e -> p (t e)"), ALU.mult, ALU.add))
            first_best(rest, top, hot2)
            link(nc.vector.tensor_tensor(both[:], hot[:], hot2[:], ALU.add))
            link(nc.vector.tensor_tensor(both[:], both[:], ex[:], ALU.mult))
            link(nc.vector.tensor_reduce(prb[:], both[:], AX_X, ALU.add))
            link(nc.vector.tensor_reduce(exs[:], ex[:], AX_X, ALU.add))
            link(nc.vector.scalar_tensor_tensor(prb[:], exs[:], 1e-9, prb[:], ALU.mult, ALU.add))
            link(nc.vector.reciprocal(prb[:], prb[:]))
            link(nc.vector.tensor_tensor(gate[:], both[:], wide(prb[:], 2, E), ALU.mult))
            for c in range(CH1):
                n = chunk_rows(c)
                dve.wait_ge(S("silu"), c + 1)
                nc.vector.tensor_tensor(hid(c)[0:n], up[0:n, c % 4], ps[0:n, UP_BANKS[c % 3] + 1, :],
                                        ALU.mult).then_inc(S("hid1"), 1)
            gated_sum("ysum")
            for t in range(NT):
                dve.wait_ge(S("ysum"), t + 1)
                if t == 0:
                    dve.wait_ge(S("h4"), NT)
                nc.vector.tensor_tensor(h[:, t], h[:, t], ysum[:, t], ALU.add).then_inc(S("h5"), 1)

        @block.tensor
        def _(pe):
            def transpose_xn(n, bank):
                for t in range(NT):
                    pe.wait_ge(S("xn"), NT * n + t + 1)
                    nc.tensor.transpose(ps[:, 2 * t + bank, 0:P], xn[:, t].rearrange("p a b -> p (a b)"),
                                        ident).then_inc(S("xT_ps"), 1)

            def attend(n, pairs):
                for t in range(NT):
                    pe.wait_ge(S("prob"), NT * n + t + 1)
                    for c in range(pairs):
                        mm = nc.tensor.transpose(ps[:, 2 * t, c * P:(c + 1) * P], prob[:, t, c * P:(c + 1) * P], ident)
                    mm.then_inc(S("probT_ps"), 1)
                for t in range(NT):
                    pe.wait_ge(S("probT"), NT * n + t + 1)
                    for i in range(2):
                        for c in range(pairs):
                            mm = nc.tensor.matmul(ps[i * D:(i + 1) * D, 2 * t + 1, 0:D],
                                                  probT[:, t, c, i * D:(i + 1) * D],
                                                  vs[:, t, i, c * D:(c + 1) * D],
                                                  start=(c == 0), stop=(c == pairs - 1))
                    mm.then_inc(S("attn_ps"), 1)

            pe.wait_ge(S("wpo_in"), 16)
            pe.wait_ge(S("con_in"), 16)
            nc.tensor.matmul(ps[0:66, 7, 0:P], pos_w1, grid1, start=True, stop=True).then_inc(S("poshid_ps"), 1)
            pe.wait_ge(S("wa0_in"), 16)
            for n in range(H0):
                cols = slice(n * D, (n + 1) * D)
                mm = nc.tensor.matmul(ps[0:D, 1, cols], qT0[:, cols], kT[:, cols], start=True, stop=True)
            mm.then_inc(S("kq0_ps"), 1)
            for n in range(H0):
                cols = slice(n * D, (n + 1) * D)
                mm = nc.tensor.matmul(ps[0:D, 3, cols], vinT[:, cols], vout[:, cols], start=True, stop=True)
            mm.then_inc(S("vo0_ps"), 1)
            pe.wait_ge(S("wf1_in"), 16)
            for n in range(H2):
                kv = n // (H2 // KV2)
                mm = nc.tensor.matmul(ps[0:D, 5, n * D:(n + 1) * D], wv2[:, kv * D:(kv + 1) * D],
                                      wo2[:, n * D:(n + 1) * D], start=True, stop=True)
            mm.then_inc(S("vo2_ps"), 1)

            pe.wait_ge(S("wem_in"), 16)
            for t in range(NT):
                pe.wait_ge(S(f"pat{t}_in"), 16)
                for c in range(KC):
                    nc.tensor.matmul(ps[:, 2 * t, 0:D], pat[:, t, c], wem[:, c * D:(c + 1) * D],
                                     start=(c == 0), stop=False)
                if t == 0:
                    pe.wait_ge(S("poshid"), 1)
                nc.tensor.matmul(ps[:, 2 * t, 0:D], poshid[:], pos_w2, start=False,
                                 stop=True).then_inc(S("embed_ps"), 1)

            pe.wait_ge(S("vo2"), 1)
            transpose_xn(0, 1)
            pe.wait_ge(S("kq0"), 1)
            for t in range(NT):
                pe.wait_ge(S("xT"), t + 1)
                for c in range(PAIRS0):
                    mm = nc.tensor.matmul(ps[:, 2 * t, c * P:(c + 1) * P], kq0[:, c * P:(c + 1) * P],
                                          xT[0:D, t], start=True, stop=True)
                mm.then_inc(S("z_ps"), 1)
            pe.wait_ge(S("vo0"), 1)
            vo0_heads = vo0[:].rearrange("p (c g e) -> p g c e", g=2, e=D)
            for t in range(NT):
                for i in range(2):
                    for g in range(2):
                        mm = nc.tensor.matmul(ps[g * D:(g + 1) * D, 2 * t + 1, i * 256:(i + 1) * 256],
                                              xT[0:D, t, i * D:(i + 1) * D], vo0_heads[:, g],
                                              start=True, stop=True)
                mm.then_inc(S("v_ps"), 1)
            pe.wait_ge(S("cbf"), 1)
            for t in range(NT):
                pe.wait_ge(S("z"), t + 1)
                pe.wait_ge(S("v"), t + 1)
                for g in range(2):
                    nc.tensor.matmul(ps[:, 2 * t + g, 0:256], ident_b, causal_b, start=True, stop=False,
                                     skip_group_check=True)
                for g in range(2):
                    for i in range(2):
                        mm = nc.tensor.matmul(ps[i * D:(i + 1) * D, 2 * t + g, 0:256],
                                              xT[g * D:(g + 1) * D, t, i * D:(i + 1) * D],
                                              zs[g * D:(g + 1) * D, t, :, i * D:(i + 1) * D],
                                              start=False, stop=True, skip_group_check=True)
                mm.then_inc(S("scores_ps"), 1)
            attend(0, PAIRS0)

            transpose_xn(1, 0)
            pe.wait_ge(S("ws0_in"), 16)
            pe.wait_ge(S("h1"), NT)
            for t in range(NT):
                pe.wait_ge(S("xT"), NT + t + 1)
                mm = nc.tensor.matmul(ps[:, 1, t * E:(t + 1) * E], xT[0:D, t], gate_w, start=True, stop=True)
            mm.then_inc(S("logits_ps"), 1)
            pe.wait_ge(S("hot_b"), 1)
            hots = hot_b[:].rearrange("p t e -> p (t e)")
            nc.tensor.matmul(ps[:, 7, 0:NT * E], upto_b, hots, start=True, stop=True, skip_group_check=True)
            for d in range(1, NT):
                mm = nc.tensor.matmul(ps[:, 7, d * E:NT * E], ones_b, hots[:, 0:(NT - d) * E],
                                      start=False, stop=True, skip_group_check=True)
            mm.then_inc(S("counts_ps"), 1)
            pe.wait_ge(S("slot"), 1)
            for t in range(NT):
                mm = nc.tensor.matmul(ps[:, 3, t * P:(t + 1) * P], slot[:, t:t + 1].broadcast_to([P, P]), ident,
                                      start=True, stop=True)
            mm.then_inc(S("slot_ps"), 1)
            pe.wait_ge(S("xs"), NT)
            for g in range(2):
                for t in range(NT):
                    pe.wait_ge(S("take"), t + 1)
                    mm = nc.tensor.matmul(ps[:, 2 * g, 0:SLOTS // 2], xs[:, t].rearrange("p a b -> p (a b)"),
                                          take[:, t, g * SLOTS // 2:(g + 1) * SLOTS // 2],
                                          start=(t == 0), stop=(t == NT - 1))
                mm.then_inc(S("xg_ps"), 1)
            pe.wait_ge(S("wu0_split"), 2)
            pe.wait_ge(S("slot_all"), 1)
            pe.wait_ge(S("xg0"), 1)
            for b, (bank, chunks) in enumerate(HID0_BANKS):
                for k, c in enumerate(chunks):
                    e = c // 2
                    if e >= E // 2:
                        pe.wait_ge(S("xg1"), 1)
                    for part in (wu0_hi, wu0_lo):
                        mm = nc.tensor.matmul(ps[:, bank, k * CAP:(k + 1) * CAP], part[:, c * P:(c + 1) * P],
                                              xg[:, e * CAP:(e + 1) * CAP], start=(part is wu0_hi),
                                              stop=(part is wu0_lo))
                mm.then_inc(S("hid0_ps"), 1)
            pe.wait_ge(S("wd0_in"), 16)
            for e in range(E):
                for c in (2 * e, 2 * e + 1):
                    pe.wait_ge(S("hid0_even"), HID0_READ[c][0])
                    if HID0_READ[c][1]:
                        pe.wait_ge(S("hid0_odd"), HID0_READ[c][1])
                    mm = nc.tensor.matmul(ps[0:D, 2 * (e // 4), e % 4 * CAP:(e % 4 + 1) * CAP], wd0[:, c],
                                          hid0[:, c], start=(c % 2 == 0), stop=(c % 2 == 1))
                if e % 4 == 3:
                    mm.then_inc(S("yT_ps"), 1)
            pe.wait_ge(S("yT"), 2)
            for c in range(SC):
                mm = nc.tensor.transpose(ps[:, 4, c * D:(c + 1) * D], yT[:, c * P:(c + 1) * P], ident[0:D, 0:D])
            mm.then_inc(S("yslot_ps"), 1)
            pe.wait_ge(S("put"), SC)
            pe.wait_ge(S("yslot_lo"), 1)
            for t in range(NT):
                for c in range(SC):
                    mm = nc.tensor.matmul(ps[:, 2 * t, 0:P], put[:, c, t * P:(t + 1) * P],
                                          yslot[:, c].rearrange("p a b -> p (a b)"),
                                          start=(c == 0), stop=(c == SC - 1))
                mm.then_inc(S("moe0_ps"), 1)

            transpose_xn(2, 1)
            pe.wait_ge(S("wa1_in"), 16)
            for t in range(NT):
                pe.wait_ge(S("xT"), 2 * NT + t + 1)
                nc.tensor.matmul(ps[:, 2 * t, 0:192], xT1[:, t], qkv_w1, start=True,
                                 stop=True).then_inc(S("qkv_ps"), 1)
            for t in range(NT):
                pe.wait_ge(S("qk"), t + 1)
                for s in range(2):
                    mm = nc.tensor.transpose(ps[0:D, 2 * t + 1, s * P:(s + 1) * P],
                                             qk[:, t, s * D:(s + 1) * D], ident)
                mm.then_inc(S("qkT_ps"), 1)
            for t in range(NT):
                pe.wait_ge(S("qkT"), 2 * (t + 1))
                for g in range(2):
                    rows = slice(g * 32, (g + 1) * 32)
                    for i in range(2):
                        mm = nc.tensor.matmul(ps[i * D:(i + 1) * D, 2 * t + g, 0:256],
                                              kTs[rows, t, i * D:(i + 1) * D],
                                              qm[rows, t, :, i * D:(i + 1) * D],
                                              start=True, stop=True)
                mm.then_inc(S("taylor_ps"), 1)
            pe.wait_ge(S("v1"), 2 * NT)
            for t in range(NT):
                pe.wait_ge(S("taylor"), t + 1)
                nc.tensor.matmul(ps[0:D, 2 * t, 0:144], ones[:, 0:D],
                                 v1[:, t].rearrange("p i h d -> p (i h d)"), start=True, stop=False,
                                 skip_group_check=True)
                num = ps[0:D, 2 * t, 0:144].rearrange("p (i h d) -> p i h d", i=2, h=H1)
                for n in range(H1):
                    mm = nc.tensor.matmul(num[:, :, n], prob[:, t, n * SEQ:(n + 1) * SEQ], v1[:, t, :, n],
                                          start=False, stop=True, skip_group_check=True)
                mm.then_inc(S("ynum_ps"), 1)
            for t in range(NT):
                pe.wait_ge(S("ya"), t + 1)
                for i in range(2):
                    mm = nc.tensor.transpose(ps[0:D, 2 * t + 1, i * D:(i + 1) * D], ya[:, t, i],
                                             ident[0:D, 0:D])
                mm.then_inc(S("yaT_ps"), 1)
            for t in range(NT):
                pe.wait_ge(S("yaT"), t + 1)
                nc.tensor.matmul(ps[:, 2 * t, 0:D], yaT[:, t], proj_w1, start=True,
                                 stop=True).then_inc(S("proj_ps"), 1)

            transpose_xn(3, 1)
            for t in range(NT):
                pe.wait_ge(S("xT"), 3 * NT + t + 1)
                nc.tensor.matmul(ps[:, 2 * t, 0:256], xT[0:D, t], qk_w2, start=True,
                                 stop=True).then_inc(S("qk2_ps"), 1)
                for i in range(2):
                    for g in range(2):
                        mm = nc.tensor.matmul(ps[g * D:(g + 1) * D, 2 * t + 1, i * P:(i + 1) * P],
                                              xT[0:D, t, i * D:(i + 1) * D],
                                              vo2[:].rearrange("p (c g e) -> p g c e", g=2, e=D)[:, g],
                                              start=True, stop=True)
                mm.then_inc(S("v2_ps"), 1)
            for t in range(NT):
                pe.wait_ge(S("qk"), NT + t + 1)
                for s in range(2):
                    mm = nc.tensor.transpose(ps[0:D, 2 * t, s * P:(s + 1) * P], qk[:, t, s * D:(s + 1) * D], ident)
                mm.then_inc(S("qkT_ps"), 1)
            for t in range(NT):
                pe.wait_ge(S("qkT"), 2 * (NT + t + 1))
                pe.wait_ge(S("v2"), t + 1)
                for g in range(2):
                    nc.tensor.matmul(ps[:, 2 * t + g, 0:P], ident_b, causal_b[:, 0:P], start=True, stop=False,
                                     skip_group_check=True)
                for g in range(2):
                    rows = slice(g * 32, (g + 1) * 32)
                    for i in range(2):
                        mm = nc.tensor.matmul(ps[i * D:(i + 1) * D, 2 * t + g, 0:P],
                                              kTs[rows, t, i * D:(i + 1) * D],
                                              qm[rows, t, 0:2, i * D:(i + 1) * D],
                                              start=False, stop=True, skip_group_check=True)
                mm.then_inc(S("scores_ps"), 1)
            attend(1, 2)

            transpose_xn(4, 0)
            pe.wait_ge(S("x1"), NT)
            for t in range(NT):
                pe.wait_ge(S("xsT"), t + 1)
                mm = nc.tensor.matmul(ps[:, 7, t * E:(t + 1) * E], xsT[:, t].bitcast(F32), router_w,
                                      start=True, stop=True)
            mm.then_inc(S("logits_ps"), 1)
            pe.wait_ge(S("wu1_split"), 2)
            xsT_all = xsT[:].rearrange("p t n -> p (t n)")
            for c in range(CH1):
                n = chunk_rows(c)
                if c >= 3:
                    pe.wait_ge(S("hid1"), c - 2)
                for g in range(2):
                    at = g * E * HID1 + c * P
                    for part in (wu1_hi, wu1_lo):
                        mm = nc.tensor.matmul(ps[0:n, UP_BANKS[c % 3] + g, :], part[:, at:at + n], xsT_all,
                                              start=(part is wu1_hi), stop=(part is wu1_lo))
                mm.then_inc(S("up_ps"), 1)
            pe.wait_ge(S("wd1_in"), 16)
            for t in range(NT):
                for c in range(CH1):
                    n = chunk_rows(c)
                    e, ne = chunk_experts(c)
                    if t == 0:
                        pe.wait_ge(S("hid1"), c + 1)
                        if c == 0:
                            pe.wait_ge(S("hid1"), CH1)
                    mm = nc.tensor.matmul(ps[:, 2 * t, e * D:(e + ne) * D], hid(c)[0:n, t * P:(t + 1) * P],
                                          wd1[0:n, DOWN_AT[c] * D:DOWN_AT[c + 1] * D],
                                          start=(c == 0), stop=True, skip_group_check=True)
                mm.then_inc(S("moe1_ps"), 1)


HID0_BANKS = [(4, [0, 1, 2]), (5, [3, 4, 5]), (6, [6, 7, 8]), (7, [9, 10, 11]), (1, [12, 13]), (3, [14, 15])]
HID0_READ = {}
for _b, (_, _chunks) in enumerate(HID0_BANKS):
    for _k, _c in enumerate(_chunks):
        _done = [sum(len(x) for _, x in HID0_BANKS[_b % 2:_b:2]) + _k + 1]
        _other = [sum(len(x) for _, x in HID0_BANKS[1 - _b % 2:_b:2])]
        HID0_READ[_c] = tuple(_done + _other) if _b % 2 == 0 else tuple(_other + _done)
UP_BANKS = [0, 2, 4]


def shape_constants():
    con = np.zeros((P, 534 + SC), np.float32)
    con[:, 0:128] = np.eye(P)
    inv_freq = 1.0 / 10000.0 ** (np.arange(0, HD2, 2, dtype=np.float32) / HD2)
    freqs = np.outer(np.arange(SEQ, dtype=np.float32), inv_freq)
    emb = np.concatenate([freqs, freqs], axis=-1)
    sign = np.where(np.arange(HD2) < HD2 // 2, -1.0, 1.0).astype(np.float32)
    con[:, 128:256] = np.tile(np.cos(emb), (2, 8))
    con[:, 256:384] = np.tile(np.sin(emb) * sign, (2, 8))
    row = np.arange(D)
    con[0:D, 384:388] = (row[:, None] % 32 // HD1) == np.arange(4)
    con[0:D, 388:390] = (row[:, None] % 32 // HD2) == np.arange(2)
    con[:, 390:398] = np.arange(E, 0, -1)
    side = 128 // PATCH
    token = np.arange(P) % SEQ
    con[0, 398:526] = (token // side).astype(np.float32) / np.float32(side - 1)
    con[1, 398:526] = (token % side).astype(np.float32) / np.float32(side - 1)
    con[2, 398:526] = 1.0
    con[:, 526:534] = CAP * np.arange(E) - 1
    con[:, 534:] = P * np.arange(SC) + np.arange(P)[:, None]
    bf = np.zeros((P, 640), np.float32)
    bf[:, 0:128] = np.eye(P)
    pos = np.arange(P) % SEQ
    bf[:, 128:384] = np.where(np.tile(np.arange(SEQ), 4)[None, :] > pos[:, None], NEG, 0.0)
    bf[:, 384:512] = np.triu(np.ones((P, P)))
    bf[:, 512:640] = 1.0
    return con, bf


def lay_out(a):
    f = np.float32
    con, bf = shape_constants()
    side = 128 // PATCH
    x = a["x"].reshape(IMG, 3, side, PATCH, side, PATCH).transpose(0, 2, 4, 1, 3, 5).reshape(NT, P, KC, P)
    m = {"patches": x.transpose(3, 0, 2, 1), "consts": con, "consts_bf": bf,
         "slot_row": np.arange(SLOTS, dtype=f)}
    m["w_embed"] = a["L0_tok_Wp"].reshape(KC, P, D).transpose(1, 0, 2).reshape(P, KC * D)
    w = np.zeros((66, 130), f)
    w[0:64, 0:64], w[64, 0:64], w[65, 0:64] = a["L0_tok_W2"], a["L0_tok_b2"], a["L0_tok_bp"]
    w[0:2, 64:128], w[2, 64:128], w[2, 128:130] = a["L0_tok_W1"], a["L0_tok_b1"], 1.0
    m["w_pos"] = w
    m["w_attn0"] = np.concatenate([
        a["L0_attn_key_matrices"].transpose(2, 0, 1).reshape(D, 512),
        a["L0_attn_query_matrices"].transpose(2, 0, 1).reshape(D, 512),
        a["L0_attn_value_in_matrices"].transpose(2, 0, 1).reshape(D, 512),
        a["L0_attn_value_out_matrices"].transpose(1, 0, 2).reshape(D, 512)], axis=1)
    m["w_up0"] = a["L0_ffn_w1"].transpose(1, 0, 2).reshape(D, E * F0)
    m["w_down0"] = a["L0_ffn_w2"].reshape(CH0, P, D).transpose(1, 0, 2).reshape(P, CH0 * D)
    w = np.zeros((P, 40), f)
    w[:, 0:16] = a["L0_ffn_b1"].reshape(CH0, P).T
    w[0:D, 16:24] = a["L0_ffn_gate_w"]
    w[:, 24:32] = a["L0_ffn_gate_b"][None, :]
    w[0:D, 32:40] = a["L0_ffn_b2"].T
    m["w_small0"] = w
    w = np.zeros((65, 256), f)
    w[0:64, 0:192], w[64, 0:192] = a["L1_attn_Wqkv"].T, a["L1_attn_bqkv"]
    w[0:64, 192:256], w[64, 192:256] = a["L1_attn_Wproj"].T, a["L1_attn_bproj"]
    m["w_attn1"] = w
    w = np.ones((P, 16), f)
    w[:, 0:8] = a["L1_attn_temperature"].reshape(1, H1)
    m["w_temp"] = w
    w = np.zeros((P, 650), f)
    half = np.arange(HD2)
    swapped = (half + HD2 // 2) % HD2
    wq = a["L1_ffn_wq"].reshape(H2, HD2, D)
    wk = np.repeat(a["L1_ffn_wk"].reshape(KV2, HD2, D), H2 // KV2, axis=0)
    w[0:D, 0:64] = wq.reshape(64, D).T
    w[0:D, 64:128] = wk.reshape(64, D).T
    w[0:D, 128:192] = wq[:, swapped].reshape(64, D).T
    w[0:D, 192:256] = wk[:, swapped].reshape(64, D).T
    w[0:HD2, 256:384] = a["L1_ffn_wv"].reshape(KV2, HD2, D).transpose(1, 0, 2).reshape(HD2, 128)
    w[0:HD2, 384:640] = a["L1_ffn_wo"].reshape(D, H2, HD2).transpose(2, 1, 0).reshape(HD2, 256)
    w[0:D, 640] = a["L1_ffn_ln1_w"]
    w[:, 641] = np.concatenate([a["L1_ffn_ln2_w"]] * 2)
    w[:, 642:650] = np.concatenate([a["L1_ffn_router_w"].T] * 2)
    m["w_ffn1"] = w
    m["w_up1"] = np.concatenate([a["L1_ffn_w1"].reshape(E * HID1, D).T, a["L1_ffn_w3"].reshape(E * HID1, D).T],
                                axis=1)
    w2 = a["L1_ffn_w2"].transpose(0, 2, 1).reshape(E * HID1, D)
    w = np.zeros((P, DOWN_AT[-1] * D), f)
    for c in range(CH1):
        first, count = chunk_experts(c)
        for k in range(count):
            lo = max(c * P, (first + k) * HID1)
            hi = min(c * P + chunk_rows(c), (first + k + 1) * HID1)
            at = (DOWN_AT[c] + k) * D
            w[lo - c * P:hi - c * P, at:at + D] = w2[lo:hi]
    m["w_down1"] = w
    return {k: np.ascontiguousarray(v) for k, v in m.items()}


def kernel(**inputs):
    import concourse.bacc as bacc
    from concourse.bass_utils import run_bass_kernel_spmd

    arrays = lay_out({k: np.asarray(v) for k, v in inputs.items()})
    nc = bacc.Bacc("TRN2", target_bir_lowering=False, num_devices=1)
    args = {k: nc.dram_tensor(k, v.shape, mybir.dt.from_np(v.dtype), kind="ExternalInput").ap()
            for k, v in arrays.items()}
    out = nc.dram_tensor("out", (TOK, D), F32, kind="ExternalOutput").ap()
    build(nc, **args, out=out)
    result = run_bass_kernel_spmd(nc, [arrays], core_ids=[0])
    return result.results[0]["out"].reshape(IMG, SEQ, D)
```

```python
from contextlib import ExitStack

import numpy as np

import concourse.bass as bass
from concourse import mybir

F32 = mybir.dt.float32
BF16 = mybir.dt.bfloat16
F32R = mybir.dt.float32r
U32 = mybir.dt.uint32
I32 = mybir.dt.int32
ALU = mybir.AluOpType
ACT = mybir.ActivationFunctionType
AX_X = mybir.AxisListType.X

P = 128
D = 64
IMG = 8
SEQ = 64
TOK = IMG * SEQ
NT = TOK // P
PAIRS = NT // 2
PATCH = 16
KC = 3 * PATCH * PATCH // P
H0 = 8
PAIRS0 = H0 // 2
E = 8
F0 = 256
CAP = -(-5 * TOK // (4 * E))
NORM_STEPS = 13
NORM_LAG = 9
MASK_AT = [NORM_STEPS + 2, NORM_STEPS + 4]
CH0 = E * F0 // P
SLOTS = E * CAP
SC = SLOTS // P
H1, HD1 = 8, 8
H2, KV2, HD2 = 4, 2, 16
HID1 = 170
LN_EPS, RMS_EPS = 1e-5, 1e-6
NORM_EPS = 1e-12
F32_MAX = float(np.finfo(np.float32).max)
NEG = -1e30


CH1 = -(-E * HID1 // P)
CHUNKS1 = []
for _c in range(CH1):
    _rows = [(e, max(_c * P, e * HID1), min((_c + 1) * P, (e + 1) * HID1)) for e in range(E)]
    CHUNKS1.append([(e, lo - e * HID1, hi - lo) for e, lo, hi in _rows if hi > lo])


def chunk_rows(c):
    return sum(units for _, _, units in CHUNKS1[c])


DOWN_AT = [sum(len(b) for b in CHUNKS1[:c]) for c in range(CH1 + 1)]
SPLIT_CHUNK = [c for c in range(CH1) if CHUNKS1[c][0][0] < E // 2 <= CHUNKS1[c][-1][0]][0]


def build(nc, patches, consts, slot_row, consts_bf, w_embed, w_pos, w_attn0, w_up0, w_down0, w_small0,
          w_attn1, w_temp, w_ffn1, w_up1, w_down1, out):
    with ExitStack() as ctx:
        sems = {}

        def S(name):
            if name not in sems:
                sems[name] = ctx.enter_context(nc.semaphore(name))
            return sems[name]

        def sb(name, shape, dt=F32):
            return ctx.enter_context(nc.sbuf_tensor(name, shape, dt))

        def wide(ap, axis, n):
            ap = ap.unsqueeze(axis)
            shape = list(ap.shape)
            shape[axis] = n
            return ap.broadcast_to(shape)

        ps = ctx.enter_context(nc.psum_tensor("ps", [P, 8, 512], F32))

        pat = sb("pat", [P, KC, TOK])
        con = sb("con", list(consts.shape))
        cbf32 = sb("cbf32", list(consts_bf.shape))
        cbf = sb("cbf", list(consts_bf.shape), BF16)
        wem = sb("wem", list(w_embed.shape))
        wpo = sb("wpo", list(w_pos.shape))
        hid_more = sb("hid_more", [P, CH1 - KC, TOK])
        wa0 = hid_more[0:D].rearrange("p c n -> p (c n)")[:, 0:2048]
        wu0 = sb("wu0", [P, E * F0])
        wu0_hi = sb("wu0_hi", [P, E * F0], F32R)
        wu0_lo = sb("wu0_lo", [P, E * F0], F32R)
        wd0 = sb("wd0", [P, CH0, D])
        ws0 = sb("ws0", list(w_small0.shape))
        wa1 = sb("wa1", list(w_attn1.shape))
        wte = sb("wte", list(w_temp.shape))
        wf1 = sb("wf1", list(w_ffn1.shape))
        wu1 = sb("wu1", [P, 2 * E * HID1])
        wu1_hi = sb("wu1_hi", [P, 2 * E * HID1], F32R)
        wu1_lo = sb("wu1_lo", [P, 2 * E * HID1], F32R)
        wd1 = sb("wd1", list(w_down1.shape))

        ident = con[:, 0:128]
        rope = con[:, 128:384]
        headmask1 = con[0:D, 384:388]
        headmask2 = con[0:D, 388:390]
        rank = con[:, 390:398]
        slot_base = con[:, 526:534]
        slot_id = con[:, 534:534 + SC]
        grid1 = con[0:3, 398:526]
        ident_b = cbf[:, 0:128]
        causal_b = cbf[:, 128:384]
        upto_b = cbf[:, 384:512]
        ones_b = cbf[:, 512:640]
        pos_w2 = wpo[0:66, 0:64]
        pos_w1 = wpo[0:3, 64:130]
        kT, qT0 = wa0[:, 0:512], wa0[:, 512:1024]
        vinT, vout = wa0[:, 1024:1536], wa0[:, 1536:2048]
        moe0_b1 = ws0[:, 0:16]
        gate_w = ws0[0:D, 16:24]
        gate_b = ws0[:, 24:32]
        moe0_b2 = ws0[0:D, 32:40]
        qkv_w1 = wa1[0:65, 0:192]
        proj_w1 = wa1[0:65, 192:256]
        qk_w2 = wf1[:, 0:256]
        wv2 = wf1[0:HD2, 256:384]
        wo2 = wf1[0:HD2, 384:640]
        ln1_w, ln2_w = wf1[:, 640:641], wf1[:, 641:642]
        router_w = wf1[:, 642:650]

        zeros = sb("zeros", [P, 512], BF16)
        ones = sb("ones", [P, P])
        half = sb("half", [P, 2])
        slots = sb("slots", [P, SLOTS])
        vo0 = sb("vo0", [D, 512])
        vo2 = sb("vo2", [D, 256])
        poshid = sb("poshid", [66, P])

        h = sb("h", [P, NT, D])
        x = sb("x", [P, NT, D])
        stats = sb("stats", [P, NT, 6])
        meanvar = sb("meanvar", [P, NT, 2])
        vareps = sb("vareps", [P, NT, 2])
        rstd = sb("rstd", [P, NT, 2])
        xn = sb("xn", [P, NT, 2, D])
        xT = sb("xT", [P, NT, P])
        zs = sb("zs", [P, NT, PAIRS0, P])
        vs = sb("vs", [P, NT, 2, PAIRS0 * D])
        prob = sb("prob", [P, NT, 512])
        mx = sb("mx", [P, NT, 8])
        den = sb("den", [P, NT, 8])
        rden = sb("rden", [P, NT, 8])
        probT = sb("probT", [P, NT, 4, P])
        lg = sb("lg", [P, NT, E])
        lgm = sb("lgm", [P, NT])
        ex = sb("ex", [P, NT, E])
        exs = sb("exs", [P, NT])
        prb = sb("prb", [P, NT])
        tie = sb("tie", [P, NT, E])
        top = sb("top", [P, NT])
        tiem = sb("tiem", [P, NT])
        hot = sb("hot", [P, NT, E])
        hot2 = sb("hot2", [P, NT, E])
        rest = sb("rest", [P, NT, E])
        both = sb("both", [P, NT, E])
        hot_b = sb("hot_b", [P, NT, E], BF16)
        gate = sb("gate", [P, NT, E])
        xs = sb("xs", [P, NT, 2, D], F32R)
        over = sb("over", [P, NT, E])
        place = sb("place", [P, NT, E])
        slot = sb("slot", [P, NT])
        slot_all = sb("slot_all", [P, TOK])
        take = sb("take", [P, NT, SLOTS], F32R)
        put = sb("put", [P, SC, TOK], F32R)
        xg = sb("xg", [P, SLOTS], F32R)
        hid0 = sb("hid0", [P, CH0, CAP])
        yT = sb("yT", [D, SLOTS])
        yslot = sb("yslot", [P, SC, 2, D], F32R)
        y = sb("y", [P, NT, D])
        above = sb("above", [P, NT, D])
        side = sb("side", [P, NT, D])
        finite = sb("finite", [P, NT, D], U32)
        xsT = sb("xsT", [P, NT, P], F32R)
        def hid(c):
            return pat[:, c] if c < KC else hid_more[:, c - KC]

        kq0_hi, kq0_lo = take[:, 0, 0:512], take[:, 1, 0:512]
        qk_w2_hi, qk_w2_lo = take[:, 2, 0:256], take[:, 3, 0:256]

        yg = probT[:].rearrange("p t a (b d) -> p t (a b) d", d=D)
        ysum = sb("ysum", [P, NT, D])
        eT = yT[:, 0:TOK]
        pos = ysum[:, 0]
        xT1 = sb("xT1", [65, NT, P])
        qk = sb("qk", [P, NT, P])
        qksq = sb("qksq", [P, NT, P])
        qkss = sb("qkss", [P, NT, 16])
        qkr = sb("qkr", [P, NT, 16])
        qkc = sb("qkc", [P, NT, 16])
        v1 = sb("v1", [P, NT, 2, H1, HD1 + 1])
        kTs = sb("kTs", [D, NT, P])
        qm = wu0[0:D].rearrange("p (t h n) -> p t h n", t=NT, h=4)
        rnorm = sb("rnorm", [D, NT, 16])
        ya = sb("ya", [D, NT, 2, D])
        yaT = sb("yaT", [65, NT, P])
        rot = wu1[:, 0:NT * 2 * P].rearrange("p (t a n) -> p t a n", t=NT, a=2)
        up = zs[:].rearrange("p a b n -> p a (b n)")

        block = ctx.enter_context(nc.Block())

        @block.sync
        def _(sp):
            sp.dma_start(wem[:], w_embed).then_inc(S("wem_in"), 16)
            for c in range(KC):
                sp.dma_start(pat[:, c], patches[:, c]).then_inc(S(f"pat{c}_in"), 16)
            sp.dma_start(ws0[:], w_small0).then_inc(S("ws0_in"), 16)
            sp.dma_start(slots[:], slot_row.partition_broadcast(P)).then_inc(S("slots_in"), 16)
            for g in range(2):
                sp.dma_start(wu0[g * D:(g + 1) * D], w_up0).then_inc(S("wu0_in"), 16)
            sp.dma_start(wd0[:], w_down0.rearrange("p (c d) -> p c d", d=D)).then_inc(S("wd0_in"), 16)
            sp.dma_start(wf1[:], w_ffn1).then_inc(S("wf1_in"), 16)
            sp.dma_start(wa1[:], w_attn1).then_inc(S("wa1_in"), 16)
            sp.dma_start(wte[:], w_temp).then_inc(S("wte_in"), 16)
            for g in range(2):
                sp.dma_start(wu1[g * D:(g + 1) * D], w_up1).then_inc(S("wu1_in"), 16)
            sp.dma_start(wd1[:], w_down1).then_inc(S("wd1_in"), 16)
            for t in range(NT):
                sp.wait_ge(S("h5"), t + 1 if t < NT - 1 else NT + 1)
                sp.dma_start(out[t * P:(t + 1) * P, :], h[:, t]).then_inc(S("stored"), 16)
            sp.wait_ge(S("stored"), 16 * NT)

        @block.gpsimd
        def _(pool):
            nc.gpsimd.memset(zeros[:], 0.0).then_inc(S("zeros_set"), 1)
            nc.gpsimd.memset(half[:], -0.5).then_inc(S("half_set"), 1)
            nc.gpsimd.memset(ones[:], 1.0).then_inc(S("ones_set"), 1)
            pool.wait_ge(S("half_set"), 1)

            def inverse_roots(n, k=0, name="rstd"):
                for p in range(PAIRS):
                    two = slice(2 * p, 2 * p + 2)
                    if k == 0:
                        pool.wait_ge(S("vareps"), PAIRS * n + p + 1)
                    else:
                        pool.wait_ge(S("vareps2"), p + 1)
                    nc.gpsimd.tensor_tensor(rstd[:, two, k:k + 1], vareps[:, two, k:k + 1],
                                            half[:].rearrange("p (t k) -> p t k", k=1),
                                            ALU.pow).then_inc(S(name), 1)

            def normalise(n, width, tiles):
                for t in tiles:
                    pool.wait_ge(S("rden"), NT * n + t + 1)
                    nc.gpsimd.tensor_tensor(prob[:, t, 0:width].rearrange("p (g k) -> p g k", k=SEQ),
                                            prob[:, t, 0:width].rearrange("p (g k) -> p g k", k=SEQ),
                                            wide(rden[:, t, 0:width // SEQ], 2, SEQ),
                                            ALU.mult).then_inc(S("prob"), 1)

            def split(whole, hi, lo, loaded, name):
                pool.wait_ge(S(loaded), 32)
                nc.gpsimd.tensor_copy(hi[:], whole[:]).then_inc(S(name), 1)
                pool.wait_ge(S(name), 1)
                nc.gpsimd.tensor_tensor(lo[:], whole[:], hi[:].bitcast(F32), ALU.subtract).then_inc(S(name), 1)

            inverse_roots(0)
            split(wu0, wu0_hi, wu0_lo, "wu0_in", "wu0_split")
            normalise(0, 512, range(NT - 1))
            inverse_roots(1)
            split(wu1, wu1_hi, wu1_lo, "wu1_in", "wu1_split")
            pool.wait_ge(S("xg_ps"), 2)
            pool.wait_ge(S("wf1_in"), 16)
            nc.gpsimd.tensor_copy(qk_w2_hi, qk_w2).then_inc(S("qk_w2_split"), 1)
            pool.wait_ge(S("qk_w2_split"), 1)
            nc.gpsimd.tensor_tensor(qk_w2_lo, qk_w2, qk_w2_hi.bitcast(F32), ALU.subtract).then_inc(S("qk_w2_split"), 1)
            inverse_roots(2)
            inverse_roots(3, k=1)
            inverse_roots(3, k=0, name="rstd_x")
            normalise(1, 256, range(NT))
            inverse_roots(4)
            for t in range(NT):
                nc.gpsimd.tensor_tensor(h[:, t], h[:, t], x[:, t], ALU.add).then_inc(S("h4"), 1)

        @block.scalar
        def _(act):
            act.dma_start(con[:], consts).then_inc(S("con_in"), 16)
            act.dma_start(wpo[:], w_pos).then_inc(S("wpo_in"), 16)
            act.dma_start(wa0, w_attn0).then_inc(S("wa0_in"), 16)
            act.dma_start(cbf32[:], consts_bf).then_inc(S("cbf_in"), 16)

            act.wait_ge(S("poshid_ps"), 1)
            nc.scalar.activation(poshid[:], ps[0:66, 5, 0:P], ACT.Relu).then_inc(S("poshid"), 1)
            act.wait_ge(S("pos_ps"), 1)
            nc.scalar.copy(pos, ps[:, 6, 0:D]).then_inc(S("pos"), 1)
            act.wait_ge(S("kq0_ps"), 1)
            nc.scalar.copy(kq0_hi, ps[:, 1, :]).then_inc(S("kq0_hi"), 1)

            act.wait_ge(S("embed_ps"), 1)
            for t in range(NT):
                nc.scalar.copy(eT[:, t * P:(t + 1) * P], ps[0:D, 7, t * P:(t + 1) * P]).then_inc(S("eT"), 1)
            act.wait_ge(S("vo0_ps"), 1)
            nc.scalar.copy(vo0[:], ps[0:D, 5, :]).then_inc(S("vo0"), 1)

            for t in range(NT):
                act.wait_ge(S("xT_ps"), t + 1)
                nc.scalar.copy(xsT[:, t], ps[:, XT_BANKS0[t], 0:P]).then_inc(S("high_part"), 1)
            for t in range(NT):
                act.wait_ge(S("two_parts"), t + 1)
                nc.scalar.copy(xT[:, t], ps[:, XT_BANKS0[t], 0:P]).then_inc(S("xT"), 1)
            for p in range(PAIRS):
                for k in range(2):
                    act.wait_ge(S("z_ps"), 2 * p + k + 1)
                    nc.scalar.copy(zs[:, 2 * p:2 * p + 2, 2 * k:2 * k + 2].rearrange("p t c n -> p c t n"),
                                   ps[:, 4 * p + 2 * k, :].rearrange("p (c t n) -> p c t n", c=2, t=2)
                                   ).then_inc(S("z"), 1)
            for t in range(NT):
                act.wait_ge(S("shifted"), t + 1)
                nc.scalar.activation(prob[:, t], prob[:, t], ACT.Exp).then_inc(S("exp"), 1)
            for t in range(NT):
                act.wait_ge(S("v_ps"), t + 1)
                nc.scalar.copy(vs[:, t].rearrange("p i n -> p (i n)"), ps[:, 2 * t + 1, :]).then_inc(S("v"), 1)
            for t in range(NT):
                act.wait_ge(S("probT_ps"), t + 1)
                nc.scalar.copy(probT[:, t].rearrange("p a b -> p (a b)"), ps[:, 2 * t, :]).then_inc(S("probT"), 1)

            for t in range(NT):
                act.wait_ge(S("xT_ps"), NT + t + 1)
                nc.scalar.copy(xT[:, t], ps[:, 2 * t, 0:P]).then_inc(S("xT"), 1)
            act.wait_ge(S("lg"), 1)
            nc.scalar.activation(ex[:].rearrange("p t e -> p (t e)"), lg[:].rearrange("p t e -> p (t e)"),
                                 ACT.Exp).then_inc(S("ex"), 1)
            act.wait_ge(S("vo2_ps"), 1)
            nc.scalar.copy(vo2[:], ps[0:D, 5, 0:256]).then_inc(S("vo2"), 1)
            act.wait_ge(S("xg_ps"), 1)
            nc.scalar.copy(xg[:, 0:SLOTS // 2], ps[:, 0, 0:SLOTS // 2]).then_inc(S("xg0"), 1)
            act.wait_ge(S("slot_ps"), 1)
            nc.scalar.copy(slot_all[:], ps[:, 3, :]).then_inc(S("slot_all"), 1)
            act.wait_ge(S("ws0_in"), 16)
            for b, (bank, chunks) in enumerate(HID0_BANKS):
                if b % 2 == 0:
                    act.wait_ge(S("hid0_ps"), b + 1)
                    for k, c in enumerate(chunks):
                        nc.scalar.activation(hid0[:, c], ps[:, bank, k * CAP:(k + 1) * CAP], ACT.Relu,
                                             bias=moe0_b1[:, c:c + 1]).then_inc(S("hid0_even"), 1)
            for g, some in enumerate(SLOT_CHUNKS):
                act.wait_ge(S("yslot_ps"), g + 1)
                nc.scalar.copy(yslot[:, some[0]:some[-1] + 1, 0],
                               ps[:, 4 + g, some[0] * D:(some[-1] + 1) * D].rearrange("p (c d) -> p c d", d=D)
                               ).then_inc(S("yslot_hi"), 1)
            act.wait_ge(S("prb"), 1)
            for t in range(NT):
                act.wait_ge(S("moe0_ps"), t + 1)
                nc.scalar.mul(y[:, t], ps[:, BACK_BANKS[t], 0:D], prb[:, t:t + 1]).then_inc(S("y_hi"), 1)

            act.wait_ge(S("ones_rows"), 2)
            for p in range(PAIRS):
                for t in (2 * p, 2 * p + 1):
                    act.wait_ge(S("xT_ps"), 2 * NT + t + 1)
                    nc.scalar.copy(xT1[0:D, t], ps[0:D, 2 * t + 1, 0:P]).then_inc(S("xT"), 1)
                for t in (2 * p, 2 * p + 1):
                    act.wait_ge(S("qkv_ps"), t + 1)
                    nc.scalar.activation(qksq[:, t], ps[:, 2 * t, 0:P], ACT.Square).then_inc(S("qksq"), 1)
            act.wait_ge(S("v1_ones"), 2)
            for t in range(NT):
                for i in range(2):
                    rows = slice(i * D, (i + 1) * D)
                    nc.scalar.copy(v1[rows, t, i, :, 1:],
                                   ps[rows, 2 * t, 128:192].rearrange("p (h d) -> p h d", d=HD1)
                                   ).then_inc(S("v1"), 1)
            for t in range(NT):
                act.wait_ge(S("qkT_ps"), t + 1)
                nc.scalar.copy(kTs[:, t], ps[0:D, 2 * t, 0:P]).then_inc(S("kT"), 1)
            for t in range(NT):
                act.wait_ge(S("taylor_ps"), t + 1)
                nc.scalar.activation(prob[:, t].rearrange("p (g k) -> p g k", g=2),
                                     ps[:, 2 * t:2 * t + 2, 0:256], ACT.Square,
                                     bias=ones[:, 0:1]).then_inc(S("square"), 1)
            for t in range(NT):
                act.wait_ge(S("yaT_ps"), t + 1)
                nc.scalar.copy(yaT[0:D, t], ps[0:D, 2 * t + 1, 0:P]).then_inc(S("yaT"), 1)

            act.wait_ge(S("wf1_in"), 16)
            for t in range(NT):
                act.wait_ge(S("xT_ps"), 3 * NT + t + 1)
                nc.scalar.mul(xsT[:, t], ps[:, 2 * t + 1, 0:P], ln1_w).then_inc(S("high_part"), 1)
            for t in range(NT):
                act.wait_ge(S("two_parts"), NT + t + 1)
                nc.scalar.mul(xT[0:D, t], ps[0:D, 2 * t + 1, 0:P], ln1_w[0:D]).then_inc(S("xT"), 1)
            for t in range(NT):
                act.wait_ge(S("qkT_ps"), NT + t + 1)
                nc.scalar.copy(kTs[:, t], ps[0:D, 2 * t + 1, 0:P]).then_inc(S("qT2"), 1)
            for t in range(NT):
                act.wait_ge(S("shifted"), NT + t + 1)
                nc.scalar.activation(prob[:, t, 0:256], prob[:, t, 0:256], ACT.Exp,
                                     scale=HD2 ** -0.5).then_inc(S("exp"), 1)
            for t in range(NT):
                act.wait_ge(S("v2_ps"), t + 1)
                nc.scalar.copy(vs[:, t, :, 0:P], ps[:, 2 * t + 1, 0:256].rearrange("p (i n) -> p i n", i=2)
                               ).then_inc(S("v2"), 1)
            for t in range(NT):
                act.wait_ge(S("probT_ps"), NT + t + 1)
                nc.scalar.copy(probT[:, t, 0:2].rearrange("p a b -> p (a b)"), ps[:, 2 * t, 0:256]
                               ).then_inc(S("probT"), 1)

            for t in range(NT):
                act.wait_ge(S("xT_ps"), 4 * NT + t + 1)
                nc.scalar.mul(xsT[:, t], ps[:, 2 * t, 0:P], ln2_w).then_inc(S("xT"), 1)
            act.wait_ge(S("lg"), 2)
            nc.scalar.activation(ex[:].rearrange("p t e -> p (t e)"), lg[:].rearrange("p t e -> p (t e)"),
                                 ACT.Exp).then_inc(S("ex"), 1)
            for c in range(CH1):
                n = chunk_rows(c)
                act.wait_ge(S("up_ps"), c + 1)
                if c >= 4:
                    act.wait_ge(S("hid1"), c - 3)
                nc.scalar.activation(up[0:n, c % 4], ps[0:n, UP_BANKS[c % 4], :], ACT.Silu).then_inc(S("silu"), 1)

        @block.vector
        def _(dve):
            def variances(n, p):
                for t in (2 * p, 2 * p + 1):
                    dve.wait_ge(S(f"h{n}"), t + 1)
                    nc.vector.bn_stats(stats[:, t], h[:, t]).then_inc(S("stats"), 1)
                for t in (2 * p, 2 * p + 1):
                    dve.wait_ge(S("stats"), NT * n + t + 1)
                    nc.vector.bn_aggr(meanvar[:, t], stats[:, t]).then_inc(S("var"), 1)
                two = slice(2 * p, 2 * p + 2)
                dve.wait_ge(S("var"), NT * n + 2 * p + 2)
                nc.vector.tensor_scalar(vareps[:, two, 0:1], meanvar[:, two, 1:2], LN_EPS, None,
                                        ALU.add).then_inc(S("vareps"), 1)

            def normalise_rows(n, p):
                k = 1 if n == 3 else 0
                dve.wait_ge(S("rstd"), PAIRS * n + p + 1)
                for t in (2 * p, 2 * p + 1):
                    nc.vector.tensor_scalar(xn[:, t], wide(h[:, t], 1, 2), meanvar[:, t, 0:1],
                                            rstd[:, t, k:k + 1], ALU.subtract, ALU.mult).then_inc(S("xn"), 1)

            def residual(source, bank, p, name):
                for t in (2 * p, 2 * p + 1):
                    dve.wait_ge(S(source), t + 1)
                    nc.vector.tensor_tensor(h[:, t], h[:, t], ps[:, 2 * t + bank, 0:D],
                                            ALU.add).then_inc(S(name), 1)

            def low_part(n, t, bank, weight):
                dve.wait_ge(S("high_part"), (n > 0) * NT + t + 1)
                if weight is None:
                    ins = nc.vector.tensor_tensor(xsT[D:P, t], ps[D:P, bank, 0:P], xsT[D:P, t].bitcast(F32),
                                                  ALU.subtract)
                else:
                    ins = nc.vector.scalar_tensor_tensor(xsT[D:P, t], ps[D:P, bank, 0:P], weight[D:P],
                                                         xsT[D:P, t].bitcast(F32), ALU.mult, ALU.subtract)
                ins.then_inc(S("two_parts"), 1)

            def softmax_front(n, heads, t):
                scores = ps[:, 2 * t:2 * t + 2, 0:heads * SEQ // 2].rearrange("p g (h k) -> p g h k", k=SEQ)
                m = mx[:, t, 0:heads].rearrange("p (g h) -> p g h", g=2)
                if n == 0:
                    shifted = prob[:, t, 0:heads * SEQ].rearrange("p (h g k) -> p g h k", g=2, k=SEQ)
                else:
                    shifted = prob[:, t, 0:heads * SEQ].rearrange("p (g h k) -> p g h k", g=2, k=SEQ)
                dve.wait_ge(S("scores_ps"), NT * n + t + 1)
                nc.vector.tensor_reduce(m, scores, AX_X, ALU.max).then_inc(S("mx"), 1)
                dve.wait_ge(S("mx"), NT * n + t + 1)
                nc.vector.tensor_tensor(shifted, scores, wide(m, 3, SEQ), ALU.subtract).then_inc(S("shifted"), 1)

            def softmax_sum(n, heads, t):
                dve.wait_ge(S("exp"), NT * n + t + 1)
                nc.vector.tensor_reduce(den[:, t, 0:heads],
                                        prob[:, t, 0:heads * SEQ].rearrange("p (g k) -> p g k", k=SEQ),
                                        AX_X, ALU.add).then_inc(S("den"), 1)
                dve.wait_ge(S("den"), NT * n + t + 1)
                nc.vector.reciprocal(rden[:, t, 0:heads], den[:, t, 0:heads]).then_inc(S("rden"), 1)

            def softmax(n, heads):
                for t in range(NT + 2):
                    if t < NT:
                        softmax_front(n, heads, t)
                    if t >= 2:
                        softmax_sum(n, heads, t - 2)

            step = [0]

            def link(ins):
                step[0] += 1
                ins.then_inc(S("gating_step"), 1)
                dve.wait_ge(S("gating_step"), step[0])

            def first_best(values, best, onehot):
                link(nc.vector.tensor_reduce(best[:], values[:], AX_X, ALU.max))
                link(nc.vector.tensor_tensor(tie[:], values[:], wide(best[:], 2, E), ALU.is_equal))
                link(nc.vector.tensor_tensor(tie[:], tie[:], wide(rank, 1, NT), ALU.mult))
                link(nc.vector.tensor_reduce(tiem[:], tie[:], AX_X, ALU.max))
                link(nc.vector.tensor_tensor(onehot[:], tie[:], wide(tiem[:], 2, E), ALU.is_equal))

            def gated_sum(t, bank, experts, number):
                cols = slice(experts.start * D, experts.stop * D)
                dve.wait_ge(S("moe1_ps"), number + 1)
                nc.vector.tensor_tensor(yg[:, t, experts], ps[:, bank, cols].rearrange("p (e d) -> p e d", d=D),
                                        wide(gate[:, t, experts], 2, D), ALU.mult).then_inc(S("yg"), 1)
                dve.wait_ge(S("yg"), number + 1)
                nc.vector.tensor_reduce(ysum[:, t], yg[:, t, experts].rearrange("p e d -> p d e"), AX_X,
                                        ALU.add).then_inc(S("ysum"), 1)
                dve.wait_ge(S("ysum"), number + 1)
                if number == 0:
                    dve.wait_ge(S("h4"), NT)
                nc.vector.tensor_tensor(h[:, t], h[:, t], ysum[:, t], ALU.add).then_inc(S("h5"), 1)

            def low_slots(g):
                some = slice(SLOT_CHUNKS[g][0], SLOT_CHUNKS[g][-1] + 1)
                dve.wait_ge(S("yslot_hi"), g + 1)
                nc.vector.tensor_tensor(
                    yslot[:, some, 1],
                    ps[:, 4 + g, some.start * D:some.stop * D].rearrange("p (c d) -> p c d", d=D),
                    yslot[:, some, 0].bitcast(F32), ALU.subtract).then_inc(S("yslot_lo"), 1)

            nc.vector.memset(v1[:], 0.0).then_inc(S("v1_zero"), 1)
            dve.wait_ge(S("v1_zero"), 1)
            for i in range(2):
                nc.vector.memset(v1[i * D:(i + 1) * D, :, i, :, 0:1], 1.0).then_inc(S("v1_ones"), 1)
            nc.vector.memset(xT1[64:65], 1.0).then_inc(S("ones_rows"), 1)
            nc.vector.memset(yaT[64:65], 1.0).then_inc(S("ones_rows"), 1)
            dve.wait_ge(S("cbf_in"), 16)
            nc.vector.tensor_copy(cbf[:], cbf32[:]).then_inc(S("cbf"), 1)

            dve.wait_ge(S("kq0_hi"), 1)
            nc.vector.tensor_tensor(kq0_lo, ps[:, 1, :], kq0_hi.bitcast(F32), ALU.subtract).then_inc(S("kq0_lo"), 1)
            dve.wait_ge(S("pos"), 1)
            for p in range(PAIRS):
                for t in (2 * p, 2 * p + 1):
                    dve.wait_ge(S("e_ps"), t + 1)
                    nc.vector.tensor_tensor(h[:, t], ps[:, 2 * t, 0:D], pos, ALU.add).then_inc(S("h0"), 1)
                variances(0, p)
            for p in range(PAIRS):
                normalise_rows(0, p)
            for t in range(NT):
                low_part(0, t, XT_BANKS0[t], None)
            softmax(0, H0)
            last = prob[:, NT - 1].rearrange("p (g k) -> p g k", k=SEQ)
            dve.wait_ge(S("rden"), NT)
            nc.vector.tensor_tensor(last, last, wide(rden[:, NT - 1], 2, SEQ), ALU.mult).then_inc(S("prob_last"), 1)
            for p in range(PAIRS):
                residual("attn_ps", 1, p, "h1")
                variances(1, p)
            for p in range(PAIRS):
                normalise_rows(1, p)

            for t in range(NT):
                dve.wait_ge(S("xn"), NT + t + 1)
                nc.vector.tensor_copy(xs[:, t, 0], xn[:, t, 0]).then_inc(S("xs_hi"), 1)
            dve.wait_ge(S("ws0_in"), 16)
            dve.wait_ge(S("con_in"), 16)
            dve.wait_ge(S("logits_ps"), 1)
            link(nc.vector.tensor_tensor(lg[:], ps[:, 1, 0:NT * E].rearrange("p (t e) -> p t e", e=E),
                                         wide(gate_b, 1, NT), ALU.add))
            link(nc.vector.tensor_reduce(lgm[:], lg[:], AX_X, ALU.max))
            nc.vector.tensor_tensor(lg[:], lg[:], wide(lgm[:], 2, E), ALU.subtract).then_inc(S("lg"), 1)

            dve.wait_ge(S("ex"), 1)
            first_best(ex, top, hot)
            nc.vector.tensor_copy(hot_b[:], hot[:]).then_inc(S("hot_b"), 1)
            for t in range(NT):
                dve.wait_ge(S("xs_hi"), t + 1)
                nc.vector.tensor_tensor(xs[:, t, 1], xn[:, t, 0], xs[:, t, 0].bitcast(F32),
                                        ALU.subtract).then_inc(S("xs"), 1)
            dve.wait_ge(S("counts_ps"), 1)
            counts = ps[:, 7, 0:NT * E].rearrange("p (t e) -> p t e", e=E)
            nc.vector.tensor_scalar(over[:], counts, float(CAP), float(2 * SLOTS), ALU.is_gt,
                                    ALU.mult).then_inc(S("over"), 1)
            link(nc.vector.tensor_tensor(place[:], counts, wide(slot_base, 1, NT), ALU.add))
            dve.wait_ge(S("over"), 1)
            link(nc.vector.tensor_tensor(place[:], place[:], over[:], ALU.add))
            link(nc.vector.tensor_tensor(place[:], place[:], hot[:], ALU.mult))
            nc.vector.tensor_reduce(slot[:], place[:], AX_X, ALU.add).then_inc(S("slot"), 1)
            dve.wait_ge(S("slots_in"), 16)
            dve.wait_ge(S("slot"), 1)
            for t in range(NT):
                nc.vector.tensor_scalar(take[:, t], slots[:], slot[:, t:t + 1], None,
                                        ALU.is_equal).then_inc(S("take"), 1)
            link(nc.vector.tensor_reduce(exs[:], ex[:], AX_X, ALU.add))
            nc.vector.reciprocal(prb[:], exs[:]).then_inc(S("prb"), 1)
            dve.wait_ge(S("xg_ps"), 2)
            nc.vector.tensor_copy(xg[:, SLOTS // 2:], ps[:, 2, 0:SLOTS // 2]).then_inc(S("xg1"), 1)
            for b, (bank, chunks) in enumerate(HID0_BANKS):
                if b % 2 == 1:
                    dve.wait_ge(S("hid0_ps"), b + 1)
                    for k, c in enumerate(chunks):
                        nc.vector.tensor_scalar(hid0[:, c], ps[:, bank, k * CAP:(k + 1) * CAP],
                                                moe0_b1[:, c:c + 1], 0.0, ALU.add,
                                                ALU.max).then_inc(S("hid0_odd"), 1)
                    if b == 1:
                        dve.wait_ge(S("slot_all"), 1)
                    for c in PUT_AFTER[b]:
                        nc.vector.tensor_scalar(put[:, c], slot_all[:], slot_id[:, c:c + 1], None,
                                                ALU.is_equal).then_inc(S("put"), 1)
            half_e = E // 2
            for g in range(2):
                dve.wait_ge(S("yT_ps"), g + 1)
                nc.vector.tensor_tensor(
                    yT[:, g * SLOTS // 2:(g + 1) * SLOTS // 2].rearrange("p (e s) -> p e s", s=CAP),
                    ps[0:D, 2 * g, 0:SLOTS // 2].rearrange("p (e s) -> p e s", s=CAP),
                    wide(moe0_b2[:, g * half_e:(g + 1) * half_e], 2, CAP), ALU.add).then_inc(S("yT"), 1)
                if g == 0:
                    low_slots(0)
            low_slots(1)
            def clean(p, step):
                two = slice(2 * p, 2 * p + 2)
                if step:
                    dve.wait_ge(S(f"clean{p}"), step)
                if step == 0:
                    for t in (2 * p, 2 * p + 1):
                        dve.wait_ge(S("y_hi"), t + 1)
                        ins = nc.vector.scalar_tensor_tensor(y[:, t], ps[:, BACK_BANKS[t], D:2 * D],
                                                             prb[:, t:t + 1], y[:, t], ALU.mult, ALU.add)
                        if t % 2 == 0:
                            ins.then_inc(S(f"y_even{p}"), 1)
                    dve.wait_ge(S(f"y_even{p}"), 1)
                elif step == 1:
                    ins = nc.vector.tensor_scalar(above[:, two], y[:, two], F32_MAX, None, ALU.is_gt)
                elif step == 2:
                    ins = nc.vector.scalar_tensor_tensor(side[:, two], y[:, two], -F32_MAX, above[:, two],
                                                         ALU.is_lt, ALU.subtract)
                elif step == 3:
                    ins = nc.vector.tensor_scalar(finite[:, two], y[:, two], 0.0, 0.0, ALU.mult, ALU.is_equal)
                elif step == 4:
                    ins = nc.vector.tensor_tensor(y[:, two], h[:, two], y[:, two], ALU.add)
                elif step == 5:
                    ins = nc.vector.scalar_tensor_tensor(h[:, two], side[:, two], -1e4, h[:, two], ALU.mult,
                                                         ALU.add)
                else:
                    ins = nc.vector.copy_predicated(h[:, two], finite[:, two], y[:, two])
                    ins.then_inc(S("h2"), 2)
                    return
                ins.then_inc(S(f"clean{p}"), 1)

            for k in range(9):
                if k < 7:
                    clean(0, k)
                if k == 7:
                    variances(2, 0)
                if k >= 2:
                    clean(1, k - 2)
            normalise_rows(2, 0)
            variances(2, 1)
            normalise_rows(2, 1)

            def inverse_norms(p, step):
                two = slice(2 * p, 2 * p + 2)
                s, r, c = qkss[:, two], qkr[:, two], qkc[:, two]
                if step:
                    dve.wait_ge(S(f"inverse_norms{p}"), step)
                if step == 0:
                    dve.wait_ge(S("qksq"), 2 * p + 2)
                    ins = nc.vector.tensor_reduce(s, qksq[:, two].rearrange("p t (g d) -> p t g d", d=HD1),
                                                  AX_X, ALU.add)
                elif step == 1:
                    ins = nc.vector.tensor_scalar(s, s, NORM_EPS ** 2 / HD1 ** 0.5, None, ALU.max)
                elif step == 2:
                    ins = nc.vector.tensor_scalar(r.bitcast(I32), s.bitcast(I32), -0.5, float(0x5F3759DF),
                                                  ALU.mult, ALU.add)
                elif step == 11:
                    ins = nc.vector.tensor_tensor(r, r, wide(wte[:], 1, 2), ALU.mult)
                elif step in (3, 6, 9):
                    ins = nc.vector.scalar_tensor_tensor(c, r, -0.5, r, ALU.mult, ALU.mult)
                elif step in (4, 7, 10):
                    ins = nc.vector.tensor_tensor(c, c, s, ALU.mult)
                else:
                    ins = nc.vector.scalar_tensor_tensor(r, c, 1.5, r, ALU.add, ALU.mult)
                ins.then_inc(S(f"inverse_norms{p}"), 1)

            dve.wait_ge(S("wte_in"), 16)
            def scale_qk(p):
                dve.wait_ge(S(f"inverse_norms{p}"), NORM_STEPS)
                for t in (2 * p, 2 * p + 1):
                    dve.wait_ge(S("v1"), 2 * (t + 1))
                    nc.vector.tensor_tensor(qk[:, t].rearrange("p (g d) -> p g d", d=HD1),
                                            ps[:, 2 * t, 0:P].rearrange("p (g d) -> p g d", d=HD1),
                                            wide(qkr[:, t], 2, HD1), ALU.mult).then_inc(S("qk"), 1)

            def mask_queries(t):
                dve.wait_ge(S("qkT_ps"), t + 1)
                nc.vector.tensor_tensor(qm[:, t], wide(ps[0:D, 2 * t + 1, 0:P], 1, 4),
                                        wide(headmask1, 2, P), ALU.mult).then_inc(S("qm"), 1)

            dve.wait_ge(S("wu0_split"), 2)
            for k in range(NORM_STEPS + NORM_LAG):
                if k < NORM_STEPS:
                    inverse_norms(0, k)
                if k == NORM_STEPS:
                    scale_qk(0)
                if k >= NORM_LAG:
                    inverse_norms(1, k - NORM_LAG)
                if k in MASK_AT:
                    mask_queries(MASK_AT.index(k))
            scale_qk(1)
            for t in (2, 3):
                mask_queries(t)
            for t in range(NT):
                dve.wait_ge(S("square"), t + 1)
                nc.vector.tensor_scalar(prob[:, t], prob[:, t], 1.0, None, ALU.add).then_inc(S("taylor"), 1)
            for t in range(NT):
                dve.wait_ge(S("ynum_ps"), t + 1)
                num = ps[0:D, 2 * t, 0:144].rearrange("p (g d) -> p g d", d=HD1 + 1)
                link(nc.vector.reciprocal(rnorm[:, t].unsqueeze(2), num[:, :, 0:1]))
                nc.vector.tensor_tensor(ya[:, t].rearrange("p i (h d) -> p (i h) d", d=HD1), num[:, :, 1:],
                                        wide(rnorm[:, t], 2, HD1), ALU.mult).then_inc(S("ya"), 1)
            for p in range(PAIRS):
                two = slice(2 * p, 2 * p + 2)
                residual("proj_ps", 0, p, "h3")
                variances(3, p)
                nc.vector.tensor_scalar(vareps[:, two, 1:2], meanvar[:, two, 1:2], 1.0 + RMS_EPS,
                                        LN_EPS * RMS_EPS, ALU.mult, ALU.add).then_inc(S("vareps2"), 1)
            for p in range(PAIRS):
                normalise_rows(3, p)
            dve.wait_ge(S("wu1_split"), 2)

            for t in range(NT):
                low_part(3, t, 2 * t + 1, ln1_w)
            for t in range(NT):
                dve.wait_ge(S("qk2_ps"), t + 1)
                nc.vector.tensor_tensor(rot[:, t].rearrange("p a b -> p (a b)"), ps[:, 2 * t, 0:256], rope,
                                        ALU.mult).then_inc(S("rot"), 1)
                dve.wait_ge(S("rot"), t + 1)
                nc.vector.tensor_tensor(qk[:, t], rot[:, t, 0], rot[:, t, 1], ALU.add).then_inc(S("qk"), 1)
            for t in range(NT):
                dve.wait_ge(S("qkT_ps"), NT + t + 1)
                nc.vector.tensor_tensor(qm[:, t, 0:2], wide(ps[0:D, 2 * t, 0:P], 1, 2),
                                        wide(headmask2, 2, P), ALU.mult).then_inc(S("kT2"), 1)
            softmax(1, H2)
            dve.wait_ge(S("rstd_x"), PAIRS)
            for t in range(NT):
                nc.vector.tensor_scalar(x[:, t], h[:, t], meanvar[:, t, 0:1], rstd[:, t, 0:1],
                                        ALU.subtract, ALU.mult).then_inc(S("x0"), 1)
            dve.wait_ge(S("x0"), NT)
            for p in range(PAIRS):
                two = slice(2 * p, 2 * p + 2)
                for t in (2 * p, 2 * p + 1):
                    dve.wait_ge(S("attn_ps"), NT + t + 1)
                    nc.vector.tensor_tensor(x[:, t], x[:, t], ps[:, 2 * t + 1, 0:D], ALU.add).then_inc(S("x1"), 1)
                for t in (2 * p, 2 * p + 1):
                    dve.wait_ge(S("x1"), t + 1)
                    nc.vector.tensor_tensor_reduce(xn[:, t, 0], x[:, t], x[:, t], 1.0 / D, 0.0, ALU.mult,
                                                   ALU.add, meanvar[:, t, 1:2]).then_inc(S("var"), 1)
                dve.wait_ge(S("var"), 4 * NT + 2 * p + 2)
                nc.vector.tensor_scalar(vareps[:, two, 0:1], meanvar[:, two, 1:2], RMS_EPS, None,
                                        ALU.add).then_inc(S("vareps"), 1)
            for p in range(PAIRS):
                dve.wait_ge(S("rstd"), 4 * PAIRS + p + 1)
                for t in (2 * p, 2 * p + 1):
                    nc.vector.tensor_scalar(xn[:, t], wide(x[:, t], 1, 2), rstd[:, t, 0:1], None,
                                            ALU.mult).then_inc(S("xn"), 1)

            for t in range(NT):
                dve.wait_ge(S("xT"), 4 * NT + t + 1)
                nc.vector.scalar_tensor_tensor(xsT[D:P, t], ps[D:P, 2 * t, 0:P], ln2_w[D:P], xsT[D:P, t].bitcast(F32),
                                               ALU.mult, ALU.subtract).then_inc(S("xsT"), 1)
            dve.wait_ge(S("logits_ps"), 2)
            link(nc.vector.tensor_copy(lg[:], ps[:, 7, 0:NT * E].rearrange("p (t e) -> p t e", e=E)))
            link(nc.vector.tensor_reduce(lgm[:], lg[:], AX_X, ALU.max))
            nc.vector.tensor_tensor(lg[:], lg[:], wide(lgm[:], 2, E), ALU.subtract).then_inc(S("lg"), 1)
            def product(c):
                n = chunk_rows(c)
                dve.wait_ge(S("silu"), c + 1)
                nc.vector.tensor_tensor(hid(c)[0:n], up[0:n, c % 4], ps[0:n, UP_BANKS[c % 4] + 1, :],
                                        ALU.mult).then_inc(S("hid1"), 1)

            dve.wait_ge(S("ex"), 2)
            first_best(ex, top, hot)
            product(0)
            link(nc.vector.scalar_tensor_tensor(rest[:].rearrange("p t e -> p (t e)"),
                                                hot[:].rearrange("p t e -> p (t e)"), -2.0,
                                                ex[:].rearrange("p t e -> p (t e)"), ALU.mult, ALU.add))
            product(1)
            first_best(rest, top, hot2)
            product(2)
            link(nc.vector.tensor_tensor(both[:], hot[:], hot2[:], ALU.add))
            link(nc.vector.tensor_tensor(both[:], both[:], ex[:], ALU.mult))
            product(3)
            link(nc.vector.tensor_reduce(prb[:], both[:], AX_X, ALU.add))
            link(nc.vector.tensor_reduce(exs[:], ex[:], AX_X, ALU.add))
            product(4)
            link(nc.vector.scalar_tensor_tensor(prb[:], exs[:], 1e-9, prb[:], ALU.mult, ALU.add))
            link(nc.vector.reciprocal(prb[:], prb[:]))
            product(5)
            link(nc.vector.tensor_tensor(gate[:], both[:], wide(prb[:], 2, E), ALU.mult))
            for c in range(6, CH1):
                product(c)
            for t in range(NT - 1):
                gated_sum(t, 2 * t, slice(0, E), t)
            gated_sum(NT - 1, 6, slice(0, E // 2), NT - 1)
            dve.wait_ge(S("h5"), NT)
            gated_sum(NT - 1, 7, slice(E // 2, E), NT)

        @block.tensor
        def _(pe):
            def transpose_xn(n, banks, t):
                pe.wait_ge(S("xn"), NT * n + t + 1)
                nc.tensor.transpose(ps[:, banks[t], 0:P], xn[:, t].rearrange("p a b -> p (a b)"),
                                    ident).then_inc(S("xT_ps"), 1)

            def attend(n, pairs):
                for t in range(NT + 2):
                    if t < NT:
                        if n == 0 and t == NT - 1:
                            pe.wait_ge(S("prob_last"), 1)
                        else:
                            pe.wait_ge(S("prob"), (NT - 1) * n + t + 1)
                        for c in range(pairs):
                            mm = nc.tensor.transpose(ps[:, 2 * t, c * P:(c + 1) * P],
                                                     prob[:, t, c * P:(c + 1) * P], ident)
                        mm.then_inc(S("probT_ps"), 1)
                    if t >= 2:
                        u = t - 2
                        pe.wait_ge(S("probT"), NT * n + u + 1)
                        pe.wait_ge(S("v2" if n else "v"), u + 1)
                        for i in range(2):
                            for c in range(pairs):
                                mm = nc.tensor.matmul(ps[i * D:(i + 1) * D, 2 * u + 1, 0:D],
                                                      probT[:, u, c, i * D:(i + 1) * D],
                                                      vs[:, u, i, c * D:(c + 1) * D],
                                                      start=(c == 0), stop=(c == pairs - 1))
                        mm.then_inc(S("attn_ps"), 1)

            def keep_clock_up(count, bank):
                for _ in range(count):
                    nc.tensor.matmul(ps[:, bank, :], zeros[:, 0:P], zeros[:], start=True, stop=True)

            pe.wait_ge(S("zeros_set"), 1)
            keep_clock_up(WARM_FIRST, 4)

            pe.wait_ge(S("wpo_in"), 16)
            pe.wait_ge(S("con_in"), 16)
            nc.tensor.matmul(ps[0:66, 5, 0:P], pos_w1, grid1, start=True, stop=True).then_inc(S("poshid_ps"), 1)
            pe.wait_ge(S("wem_in"), 16)
            for c in range(KC):
                pe.wait_ge(S(f"pat{c}_in"), 16)
                mm = nc.tensor.matmul(ps[0:D, 7, :], wem[:, c * D:(c + 1) * D], pat[:, c],
                                      start=(c == 0), stop=(c == KC - 1))
                if c == 0:
                    pe.wait_ge(S("poshid"), 1)
                    nc.tensor.matmul(ps[:, 6, 0:D], poshid[:], pos_w2, start=True,
                                     stop=True).then_inc(S("pos_ps"), 1)
                if c == 2:
                    pe.wait_ge(S("wa0_in"), 16)
                    for n in range(H0):
                        cols = slice(n * D, (n + 1) * D)
                        for g in range(2):
                            kq = nc.tensor.matmul(ps[g * D:(g + 1) * D, 1, cols], qT0[:, cols], kT[:, cols],
                                                  start=True, stop=True)
                    kq.then_inc(S("kq0_ps"), 1)
            mm.then_inc(S("embed_ps"), 1)
            for t in range(NT):
                pe.wait_ge(S("eT"), t + 1)
                if t == NT - 1:
                    pe.wait_ge(S("pos"), 1)
                nc.tensor.transpose(ps[:, 2 * t, 0:D], eT[:, t * P:(t + 1) * P],
                                    ident[0:D, 0:D]).then_inc(S("e_ps"), 1)
            for n in range(H0):
                cols = slice(n * D, (n + 1) * D)
                mm = nc.tensor.matmul(ps[0:D, 5, cols], vinT[:, cols], vout[:, cols], start=True, stop=True)
            mm.then_inc(S("vo0_ps"), 1)

            pe.wait_ge(S("kq0_lo"), 1)
            for t in range(NT):
                transpose_xn(0, XT_BANKS0, t)
            for p in range(PAIRS):
                pe.wait_ge(S("two_parts"), 2 * p + 2)
                if p == 1:
                    pe.wait_ge(S("xT"), NT)
                for c in range(PAIRS0):
                    for part in (kq0_hi, kq0_lo):
                        mm = nc.tensor.matmul(ps[:, 4 * p + c // 2 * 2, c % 2 * 256:(c % 2 + 1) * 256],
                                              part[:, c * P:(c + 1) * P],
                                              xsT[:, 2 * p:2 * p + 2].rearrange("p t n -> p (t n)"),
                                              start=(part is kq0_hi), stop=(part is kq0_lo))
                    if c % 2 == 1:
                        mm.then_inc(S("z_ps"), 1)
            pe.wait_ge(S("cbf"), 1)
            for t in range(NT):
                pe.wait_ge(S("z"), 2 * (t // 2 + 1))
                pe.wait_ge(S("vo0"), 1)
                pe.wait_ge(S("xT"), NT)
                for g in range(2):
                    nc.tensor.matmul(ps[:, 2 * t + g, 0:256], ident_b, causal_b, start=True, stop=False,
                                     skip_group_check=True)
                for g in range(2):
                    for i in range(2):
                        mm = nc.tensor.matmul(ps[i * D:(i + 1) * D, 2 * t + g, 0:256],
                                              xT[g * D:(g + 1) * D, t, i * D:(i + 1) * D],
                                              zs[g * D:(g + 1) * D, t, :, i * D:(i + 1) * D],
                                              start=False, stop=True, skip_group_check=True)
                mm.then_inc(S("scores_ps"), 1)
            vo0_heads = vo0[:].rearrange("p (c g e) -> p g c e", g=2, e=D)
            for t in range(NT):
                pe.wait_ge(S("shifted"), t + 1)
                for i in range(2):
                    for g in range(2):
                        mm = nc.tensor.matmul(ps[g * D:(g + 1) * D, 2 * t + 1, i * 256:(i + 1) * 256],
                                              xT[0:D, t, i * D:(i + 1) * D], vo0_heads[:, g],
                                              start=True, stop=True)
                mm.then_inc(S("v_ps"), 1)
            attend(0, PAIRS0)

            pe.wait_ge(S("ws0_in"), 16)
            for t in range(NT + 2):
                if t < NT:
                    transpose_xn(1, [0, 2, 4, 6], t)
                if t == 2:
                    pe.wait_ge(S("h1"), NT)
                if t >= 2:
                    pe.wait_ge(S("xT"), NT + t - 1)
                    mm = nc.tensor.matmul(ps[:, 1, (t - 2) * E:(t - 1) * E], xT[0:D, t - 2], gate_w,
                                          start=True, stop=True)
            mm.then_inc(S("logits_ps"), 1)
            pe.wait_ge(S("wf1_in"), 16)
            for n in range(H2):
                kv = n // (H2 // KV2)
                mm = nc.tensor.matmul(ps[0:D, 5, n * D:(n + 1) * D], wv2[:, kv * D:(kv + 1) * D],
                                      wo2[:, n * D:(n + 1) * D], start=True, stop=True)
            mm.then_inc(S("vo2_ps"), 1)
            keep_clock_up(3, 4)
            pe.wait_ge(S("hot_b"), 1)
            hots = hot_b[:].rearrange("p t e -> p (t e)")
            nc.tensor.matmul(ps[:, 7, 0:NT * E], upto_b, hots, start=True, stop=True, skip_group_check=True)
            for d in range(1, NT):
                mm = nc.tensor.matmul(ps[:, 7, d * E:NT * E], ones_b, hots[:, 0:(NT - d) * E],
                                      start=False, stop=True, skip_group_check=True)
            mm.then_inc(S("counts_ps"), 1)
            def spread_slots(tiles):
                for t in tiles:
                    mm = nc.tensor.matmul(ps[:, 3, t * P:(t + 1) * P], slot[:, t:t + 1].broadcast_to([P, P]),
                                          ident, start=True, stop=True)
                return mm

            keep_clock_up(3, 4)
            pe.wait_ge(S("slot"), 1)
            spread_slots(range(2))
            pe.wait_ge(S("xs"), NT)
            for t in range(NT):
                pe.wait_ge(S("take"), t + 1)
                for g in range(2):
                    mm = nc.tensor.matmul(ps[:, 2 * g, 0:SLOTS // 2], xs[:, t].rearrange("p a b -> p (a b)"),
                                          take[:, t, g * SLOTS // 2:(g + 1) * SLOTS // 2],
                                          start=(t == 0), stop=(t == NT - 1))
                    if t == NT - 1:
                        mm.then_inc(S("xg_ps"), 1)
            spread_slots(range(2, NT)).then_inc(S("slot_ps"), 1)
            pe.wait_ge(S("wu0_split"), 2)
            pe.wait_ge(S("xg0"), 1)
            for b, (bank, chunks) in enumerate(HID0_BANKS):
                if bank == 3:
                    pe.wait_ge(S("slot_all"), 1)
                for k, c in enumerate(chunks):
                    e = c // 2
                    if e >= E // 2:
                        pe.wait_ge(S("xg1"), 1)
                    for part in (wu0_hi, wu0_lo):
                        mm = nc.tensor.matmul(ps[:, bank, k * CAP:(k + 1) * CAP], part[:, c * P:(c + 1) * P],
                                              xg[:, e * CAP:(e + 1) * CAP], start=(part is wu0_hi),
                                              stop=(part is wu0_lo))
                mm.then_inc(S("hid0_ps"), 1)
            pe.wait_ge(S("wd0_in"), 16)
            for e in range(E):
                for c in (2 * e, 2 * e + 1):
                    pe.wait_ge(S("hid0_even"), HID0_READ[c][0])
                    if HID0_READ[c][1]:
                        pe.wait_ge(S("hid0_odd"), HID0_READ[c][1])
                    mm = nc.tensor.matmul(ps[0:D, 2 * (e // 4), e % 4 * CAP:(e % 4 + 1) * CAP], wd0[:, c],
                                          hid0[:, c], start=(c % 2 == 0), stop=(c % 2 == 1))
                if e % 4 == 3:
                    mm.then_inc(S("yT_ps"), 1)
            for g, some in enumerate(SLOT_CHUNKS):
                pe.wait_ge(S("yT"), g + 1)
                for c in some:
                    mm = nc.tensor.transpose(ps[:, 4 + g, c * D:(c + 1) * D], yT[:, c * P:(c + 1) * P],
                                             ident[0:D, 0:D])
                mm.then_inc(S("yslot_ps"), 1)
            keep_clock_up(2, 3)
            pe.wait_ge(S("put"), SC)
            for g, some in enumerate(SLOT_CHUNKS):
                pe.wait_ge(S("yslot_lo"), g + 1)
                for t in range(NT):
                    for c in some:
                        mm = nc.tensor.matmul(ps[:, BACK_BANKS[t], 0:P], put[:, c, t * P:(t + 1) * P],
                                              yslot[:, c].rearrange("p a b -> p (a b)"),
                                              start=(c == 0), stop=(c == SC - 1))
                    if g == 1:
                        mm.then_inc(S("moe0_ps"), 1)

            pe.wait_ge(S("wa1_in"), 16)
            for p in range(PAIRS):
                for t in (2 * p, 2 * p + 1):
                    transpose_xn(2, [1, 3, 5, 7], t)
                for t in (2 * p, 2 * p + 1):
                    pe.wait_ge(S("xT"), 2 * NT + t + 1)
                    nc.tensor.matmul(ps[:, 2 * t, 0:192], xT1[:, t], qkv_w1, start=True,
                                     stop=True).then_inc(S("qkv_ps"), 1)
            pe.wait_ge(S("v1"), 2 * NT)
            def transpose_qk(t):
                pe.wait_ge(S("qk"), t + 1)
                for s in range(2):
                    mm = nc.tensor.transpose(ps[0:D, 2 * t + 1 - s, 0:P], qk[:, t, s * D:(s + 1) * D], ident)
                mm.then_inc(S("qkT_ps"), 1)

            def cosines(t):
                pe.wait_ge(S("kT"), t + 1)
                pe.wait_ge(S("qm"), t + 1)
                for g in range(2):
                    rows = slice(g * 32, (g + 1) * 32)
                    for i in range(2):
                        mm = nc.tensor.matmul(ps[i * D:(i + 1) * D, 2 * t + g, 0:256],
                                              kTs[rows, t, i * D:(i + 1) * D],
                                              qm[rows, t, :, i * D:(i + 1) * D],
                                              start=True, stop=True)
                mm.then_inc(S("taylor_ps"), 1)

            transpose_qk(0)
            transpose_qk(1)
            cosines(0)
            transpose_qk(2)
            transpose_qk(3)
            for t in range(1, NT):
                cosines(t)
            for step in range(NT + 2):
                if step < NT:
                    t = step
                    pe.wait_ge(S("taylor"), t + 1)
                    num = ps[0:D, 2 * t, 0:144].rearrange("p (i h d) -> p i h d", i=2, h=H1)
                    for n in range(H1):
                        mm = nc.tensor.matmul(num[:, :, n], prob[:, t, n * SEQ:(n + 1) * SEQ], v1[:, t, :, n],
                                              start=True, stop=True)
                    mm.then_inc(S("ynum_ps"), 1)
                if 1 <= step <= NT:
                    t = step - 1
                    pe.wait_ge(S("ya"), t + 1)
                    for i in range(2):
                        mm = nc.tensor.transpose(ps[0:D, 2 * t + 1, i * D:(i + 1) * D], ya[:, t, i],
                                                 ident[0:D, 0:D])
                    mm.then_inc(S("yaT_ps"), 1)
                if step >= 2:
                    t = step - 2
                    pe.wait_ge(S("yaT"), t + 1)
                    nc.tensor.matmul(ps[:, 2 * t, 0:D], yaT[:, t], proj_w1, start=True,
                                     stop=True).then_inc(S("proj_ps"), 1)

            keep_clock_up(3, 1)
            for t in range(NT):
                transpose_xn(3, [1, 3, 5, 7], t)
            keep_clock_up(1, 0)
            pe.wait_ge(S("qk_w2_split"), 2)
            for t in range(NT):
                pe.wait_ge(S("two_parts"), NT + t + 1)
                for part in (qk_w2_hi, qk_w2_lo):
                    mm = nc.tensor.matmul(ps[:, 2 * t, 0:256], xsT[:, t], part, start=(part is qk_w2_hi),
                                          stop=(part is qk_w2_lo))
                mm.then_inc(S("qk2_ps"), 1)
            for t in range(NT):
                pe.wait_ge(S("qk"), NT + t + 1)
                pe.wait_ge(S("xT"), 3 * NT + t + 1)
                for s in range(2):
                    mm = nc.tensor.transpose(ps[0:D, 2 * t + 1 - s, 0:P], qk[:, t, s * D:(s + 1) * D], ident)
                mm.then_inc(S("qkT_ps"), 1)
            for t in range(NT):
                pe.wait_ge(S("qT2"), t + 1)
                pe.wait_ge(S("kT2"), t + 1)
                for g in range(2):
                    nc.tensor.matmul(ps[:, 2 * t + g, 0:P], ident_b, causal_b[:, 0:P], start=True, stop=False,
                                     skip_group_check=True)
                for g in range(2):
                    rows = slice(g * 32, (g + 1) * 32)
                    for i in range(2):
                        mm = nc.tensor.matmul(ps[i * D:(i + 1) * D, 2 * t + g, 0:P],
                                              kTs[rows, t, i * D:(i + 1) * D],
                                              qm[rows, t, 0:2, i * D:(i + 1) * D],
                                              start=False, stop=True, skip_group_check=True)
                mm.then_inc(S("scores_ps"), 1)
            pe.wait_ge(S("vo2"), 1)
            pe.wait_ge(S("xT"), 4 * NT)
            for t in range(NT):
                pe.wait_ge(S("shifted"), NT + t + 1)
                for i in range(2):
                    for g in range(2):
                        mm = nc.tensor.matmul(ps[g * D:(g + 1) * D, 2 * t + 1, i * P:(i + 1) * P],
                                              xT[0:D, t, i * D:(i + 1) * D],
                                              vo2[:].rearrange("p (c g e) -> p g c e", g=2, e=D)[:, g],
                                              start=True, stop=True)
                mm.then_inc(S("v2_ps"), 1)
            attend(1, 2)

            keep_clock_up(4, 0)
            pe.wait_ge(S("x1"), NT)
            def route(t):
                pe.wait_ge(S("xsT"), t + 1)
                return nc.tensor.matmul(ps[:, 7, t * E:(t + 1) * E], xsT[:, t].bitcast(F32), router_w,
                                        start=True, stop=True)

            for t in range(NT):
                transpose_xn(4, [0, 2, 4, 6], t)
                if t >= 2:
                    route(t - 2)
            keep_clock_up(1, 3)
            for t in range(2, NT):
                mm = route(t)
            mm.then_inc(S("logits_ps"), 1)
            pe.wait_ge(S("wu1_split"), 2)
            xsT_all = xsT[:].rearrange("p t n -> p (t n)")
            for c in range(CH1):
                n = chunk_rows(c)
                if c == 3:
                    pe.wait_ge(S("lg"), 2)
                if c >= 4:
                    pe.wait_ge(S("hid1"), c - 3)
                for g in range(2):
                    at = g * E * HID1 + c * P
                    for part in (wu1_hi, wu1_lo):
                        mm = nc.tensor.matmul(ps[0:n, UP_BANKS[c % 4] + g, :], part[:, at:at + n], xsT_all,
                                              start=(part is wu1_hi), stop=(part is wu1_lo))
                mm.then_inc(S("up_ps"), 1)
            pe.wait_ge(S("wd1_in"), 16)
            def down(t, c, bank, pieces, start):
                n, at = chunk_rows(c), DOWN_AT[c] + pieces[0]
                e = CHUNKS1[c][pieces[0]][0]
                return nc.tensor.matmul(ps[:, bank, e * D:(e + len(pieces)) * D],
                                        hid(c)[0:n, t * P:(t + 1) * P],
                                        wd1[0:n, at * D:(at + len(pieces)) * D], start=start, stop=True,
                                        skip_group_check=True)

            for t in range(NT - 1):
                for c in range(CH1):
                    if t == 0:
                        pe.wait_ge(S("hid1"), max(c + 1, CH1 - 2))
                    mm = down(t, c, 2 * t, range(len(CHUNKS1[c])), c == 0)
                mm.then_inc(S("moe1_ps"), 1)
            t = NT - 1
            half_at = E // 2 - CHUNKS1[SPLIT_CHUNK][0][0]
            for c in range(SPLIT_CHUNK):
                down(t, c, 6, range(len(CHUNKS1[c])), c == 0)
            down(t, SPLIT_CHUNK, 6, range(half_at), False).then_inc(S("moe1_ps"), 1)
            down(t, SPLIT_CHUNK, 7, range(half_at, len(CHUNKS1[SPLIT_CHUNK])), True)
            for c in range(SPLIT_CHUNK + 1, CH1):
                mm = down(t, c, 7, range(len(CHUNKS1[c])), False)
            mm.then_inc(S("moe1_ps"), 1)
HID0_BANKS = [(4, [0, 1, 2]), (5, [3, 4, 5]), (6, [6, 7, 8]), (7, [9, 10, 11]), (1, [12, 13]), (3, [14, 15])]
HID0_READ = {}
for _b, (_, _chunks) in enumerate(HID0_BANKS):
    for _k, _c in enumerate(_chunks):
        _done = [sum(len(x) for _, x in HID0_BANKS[_b % 2:_b:2]) + _k + 1]
        _other = [sum(len(x) for _, x in HID0_BANKS[1 - _b % 2:_b:2])]
        HID0_READ[_c] = tuple(_done + _other) if _b % 2 == 0 else tuple(_other + _done)
PUT_AFTER = {1: [0, 1], 3: [2, 3], 5: list(range(4, SC))}
SLOT_CHUNKS = [range(SLOTS // 2 // P), range(SLOTS // 2 // P, SC)]
BACK_BANKS = [1, 3, 6, 7]
WARM_FIRST = 9
XT_BANKS0 = [1, 3, 7, 6]
UP_BANKS = [0, 2, 4, 6]


def shape_constants():
    con = np.zeros((P, 534 + SC), np.float32)
    con[:, 0:128] = np.eye(P)
    inv_freq = 1.0 / 10000.0 ** (np.arange(0, HD2, 2, dtype=np.float32) / HD2)
    freqs = np.outer(np.arange(SEQ, dtype=np.float32), inv_freq)
    emb = np.concatenate([freqs, freqs], axis=-1)
    sign = np.where(np.arange(HD2) < HD2 // 2, -1.0, 1.0).astype(np.float32)
    con[:, 128:256] = np.tile(np.cos(emb), (2, 8))
    con[:, 256:384] = np.tile(np.sin(emb) * sign, (2, 8))
    row = np.arange(D)
    con[0:D, 384:388] = (row[:, None] % 32 // HD1) == np.arange(4)
    con[0:D, 388:390] = (row[:, None] % 32 // HD2) == np.arange(2)
    con[:, 390:398] = np.arange(E, 0, -1)
    side = 128 // PATCH
    token = np.arange(P) % SEQ
    con[0, 398:526] = (token // side).astype(np.float32) / np.float32(side - 1)
    con[1, 398:526] = (token % side).astype(np.float32) / np.float32(side - 1)
    con[2, 398:526] = 1.0
    con[:, 526:534] = CAP * np.arange(E) - 1
    con[:, 534:] = P * np.arange(SC) + np.arange(P)[:, None]
    bf = np.zeros((P, 640), np.float32)
    bf[:, 0:128] = np.eye(P)
    pos = np.arange(P) % SEQ
    bf[:, 128:384] = np.where(np.tile(np.arange(SEQ), 4)[None, :] > pos[:, None], NEG, 0.0)
    bf[:, 384:512] = np.triu(np.ones((P, P)))
    bf[:, 512:640] = 1.0
    return con, bf


def lay_out(a):
    f = np.float32
    con, bf = shape_constants()
    side = 128 // PATCH
    x = a["x"].reshape(IMG, 3, side, PATCH, side, PATCH).transpose(0, 2, 4, 1, 3, 5).reshape(NT, P, KC, P)
    m = {"patches": x.transpose(3, 2, 0, 1).reshape(P, KC, TOK), "consts": con, "consts_bf": bf,
         "slot_row": np.arange(SLOTS, dtype=f)}
    m["w_embed"] = a["L0_tok_Wp"].reshape(KC, P, D).transpose(1, 0, 2).reshape(P, KC * D)
    w = np.zeros((66, 130), f)
    w[0:64, 0:64], w[64, 0:64], w[65, 0:64] = a["L0_tok_W2"], a["L0_tok_b2"], a["L0_tok_bp"]
    w[0:2, 64:128], w[2, 64:128], w[2, 128:130] = a["L0_tok_W1"], a["L0_tok_b1"], 1.0
    m["w_pos"] = w
    m["w_attn0"] = np.concatenate([
        a["L0_attn_key_matrices"].transpose(2, 0, 1).reshape(D, 512),
        a["L0_attn_query_matrices"].transpose(2, 0, 1).reshape(D, 512),
        a["L0_attn_value_in_matrices"].transpose(2, 0, 1).reshape(D, 512),
        a["L0_attn_value_out_matrices"].transpose(1, 0, 2).reshape(D, 512)], axis=1)
    m["w_up0"] = a["L0_ffn_w1"].transpose(1, 0, 2).reshape(D, E * F0)
    m["w_down0"] = a["L0_ffn_w2"].reshape(CH0, P, D).transpose(1, 0, 2).reshape(P, CH0 * D)
    w = np.zeros((P, 40), f)
    w[:, 0:16] = a["L0_ffn_b1"].reshape(CH0, P).T
    w[0:D, 16:24] = a["L0_ffn_gate_w"]
    w[:, 24:32] = a["L0_ffn_gate_b"][None, :]
    w[0:D, 32:40] = a["L0_ffn_b2"].T
    m["w_small0"] = w
    w = np.zeros((65, 256), f)
    w[0:64, 0:192], w[64, 0:192] = a["L1_attn_Wqkv"].T, a["L1_attn_bqkv"]
    w[0:64, 192:256], w[64, 192:256] = a["L1_attn_Wproj"].T, a["L1_attn_bproj"]
    m["w_attn1"] = w
    w = np.ones((P, 16), f)
    w[:, 0:8] = a["L1_attn_temperature"].reshape(1, H1)
    m["w_temp"] = w
    w = np.zeros((P, 650), f)
    half = np.arange(HD2)
    swapped = (half + HD2 // 2) % HD2
    wq = a["L1_ffn_wq"].reshape(H2, HD2, D)
    wk = np.repeat(a["L1_ffn_wk"].reshape(KV2, HD2, D), H2 // KV2, axis=0)
    w[0:D, 0:64] = wq.reshape(64, D).T
    w[0:D, 64:128] = wk.reshape(64, D).T
    w[0:D, 128:192] = wq[:, swapped].reshape(64, D).T
    w[0:D, 192:256] = wk[:, swapped].reshape(64, D).T
    w[0:HD2, 256:384] = a["L1_ffn_wv"].reshape(KV2, HD2, D).transpose(1, 0, 2).reshape(HD2, 128)
    w[0:HD2, 384:640] = a["L1_ffn_wo"].reshape(D, H2, HD2).transpose(2, 1, 0).reshape(HD2, 256)
    w[D:P, 0:256] = w[0:D, 0:256]
    w[:, 640] = np.concatenate([a["L1_ffn_ln1_w"]] * 2)
    w[:, 641] = np.concatenate([a["L1_ffn_ln2_w"]] * 2)
    w[:, 642:650] = np.concatenate([a["L1_ffn_router_w"].T] * 2)
    m["w_ffn1"] = w
    m["w_up1"] = np.concatenate([a["L1_ffn_w1"].reshape(E * HID1, D).T, a["L1_ffn_w3"].reshape(E * HID1, D).T],
                                axis=1)
    w2 = a["L1_ffn_w2"].transpose(0, 2, 1)
    w = np.zeros((P, DOWN_AT[-1] * D), f)
    for c, pieces in enumerate(CHUNKS1):
        row = 0
        for k, (e, first, n) in enumerate(pieces):
            at = (DOWN_AT[c] + k) * D
            w[row:row + n, at:at + D] = w2[e, first:first + n]
            row += n
    m["w_down1"] = w
    return {k: np.ascontiguousarray(v) for k, v in m.items()}


def kernel(**inputs):
    import concourse.bacc as bacc
    from concourse.bass_utils import run_bass_kernel_spmd

    arrays = lay_out({k: np.asarray(v) for k, v in inputs.items()})
    nc = bacc.Bacc("TRN2", target_bir_lowering=False, num_devices=1)
    args = {k: nc.dram_tensor(k, v.shape, mybir.dt.from_np(v.dtype), kind="ExternalInput").ap()
            for k, v in arrays.items()}
    out = nc.dram_tensor("out", (TOK, D), F32, kind="ExternalOutput").ap()
    build(nc, **args, out=out)
    result = run_bass_kernel_spmd(nc, [arrays], core_ids=[0])
    return result.results[0]["out"].reshape(IMG, SEQ, D)
```
